# Optimizing a Trainium2 kernel written in Bass

```python
import numpy as np
import jax
import jax.numpy as jnp

def _softmax(x, axis=-1):
    return jax.nn.softmax(x, axis=axis)

def _gelu(x):
    return jax.nn.gelu(x, approximate=True)

def _silu(x):
    return jax.nn.silu(x)

def _sigmoid(x):
    return jax.nn.sigmoid(x)

def _layernorm(x, axis=-1, eps=1e-05):
    m = jnp.mean(x, axis=axis, keepdims=True)
    v = jnp.var(x, axis=axis, keepdims=True)
    return (x - m) / jnp.sqrt(v + eps)

def _scatter_add(tgt, idx, src, axis=0):
    return tgt.at[idx].add(src)

def _segment_sum(src, seg, n):
    return jax.ops.segment_sum(src, seg, n)
kernel_name = 'mk_decoder_preln_d2_seqx_r4_9b2c69'

def setup_inputs(seed: int=0):
    np.random.seed(seed)
    _w = jnp.asarray

    def _rec_inputs():
        import jax
        import jax.numpy as jnp
        _rk = jax.random.key(seed)
        x = -0.0002928 + 1 * jax.random.normal(jax.random.fold_in(_rk, 1), (32, 112, 256), jnp.float32)
        _lenS = 112 - jax.random.randint(jax.random.fold_in(_rk, 7), (32,), 0, max(1, 112 // 4) + 1, jnp.int32)
        _lenS2 = 375 - jax.random.randint(jax.random.fold_in(_rk, 8), (32,), 0, max(1, 375 // 4) + 1, jnp.int32)
        _ctx_1024P = jax.random.normal(jax.random.fold_in(_rk, 11), (32, 16, 256), jnp.float32)
        _ctx_1024c = jax.random.dirichlet(jax.random.fold_in(_rk, 511), 0.3 * jnp.ones((16,), jnp.float32), (32, 375))
        _ctx_1024t = jnp.einsum('bsk,bkd->bsd', _ctx_1024c, _ctx_1024P)
        _ctx_1024t = _ctx_1024t * jax.lax.rsqrt(jnp.mean(jnp.square(_ctx_1024t)) + 1e-12) * 0.953939
        ctx_1024 = -1.39393e-06 + 0.999914 * (_ctx_1024t + 0.3 * jax.random.normal(jax.random.fold_in(_rk, 611), (32, 375, 256), jnp.float32))
        return (x, ctx_1024)
    x, ctx_1024 = _rec_inputs()

    def _L0_attn_setup():
        import jax, jax.numpy as jnp
        import numpy as np
        B, N, E, H = (2, 512, 256, 8)
        HID = 256
        D = HID // H
        EPS = 1e-08

        def rms_norm(x, scale):
            rms = jnp.linalg.norm(x, axis=-1, keepdims=True) * x.shape[-1] ** (-0.5)
            return scale * (x / (rms + EPS))
        key = jax.random.key(seed)
        ks = jax.random.split(key, 12)
        s = 0.02
        return {'x': jax.random.normal(ks[0], (B, N, E), jnp.float32), 'Wq': jax.random.normal(ks[1], (HID, E), jnp.float32) * s, 'bq': jnp.zeros((HID,), jnp.float32), 'Wk': jax.random.normal(ks[2], (HID, E), jnp.float32) * s, 'bk': jnp.zeros((HID,), jnp.float32), 'Wv': jax.random.normal(ks[3], (HID, E), jnp.float32) * s, 'bv': jnp.zeros((HID,), jnp.float32), 'Wu': jax.random.normal(ks[4], (HID, E), jnp.float32) * s, 'bu': jnp.zeros((HID,), jnp.float32), 'Wo': jax.random.normal(ks[5], (E, HID), jnp.float32) * s, 'bo': jnp.zeros((E,), jnp.float32), 'scale': jnp.ones((HID,), jnp.float32)}
    _L0_attn_all = _L0_attn_setup()
    _L0_attn_in = {k: v for k, v in _L0_attn_all.items() if k in ('Wq', 'bq', 'Wk', 'bk', 'Wv', 'bv', 'Wu', 'bu', 'Wo', 'bo', 'scale')}
    del _L0_attn_all

    def _L0_xattn_setup():
        import jax, jax.numpy as jnp
        import numpy as np
        import math
        D_MODEL = 256
        N_HEADS = 16
        D_HEAD = D_MODEL // N_HEADS
        key = jax.random.key(seed)
        ks = jax.random.split(key, 11)
        N, L, S = (2, 512, 512)
        inp = {'queries': jax.random.normal(ks[0], (N, L, D_MODEL), dtype=jnp.float32), 'keys': jax.random.normal(ks[1], (N, S, D_MODEL), dtype=jnp.float32), 'values': jax.random.normal(ks[2], (N, S, D_MODEL), dtype=jnp.float32), 'Wq': jax.random.normal(ks[3], (D_MODEL, N_HEADS * D_HEAD), dtype=jnp.float32) / math.sqrt(D_MODEL), 'bq': jnp.zeros((N_HEADS * D_HEAD,), dtype=jnp.float32), 'Wk': jax.random.normal(ks[4], (D_MODEL, N_HEADS * D_HEAD), dtype=jnp.float32) / math.sqrt(D_MODEL), 'bk': jnp.zeros((N_HEADS * D_HEAD,), dtype=jnp.float32), 'Wv': jax.random.normal(ks[5], (D_MODEL, N_HEADS * D_HEAD), dtype=jnp.float32) / math.sqrt(D_MODEL), 'bv': jnp.zeros((N_HEADS * D_HEAD,), dtype=jnp.float32), 'Wo': jax.random.normal(ks[6], (N_HEADS * D_HEAD, D_MODEL), dtype=jnp.float32) / math.sqrt(N_HEADS * D_HEAD), 'bo': jnp.zeros((D_MODEL,), dtype=jnp.float32)}
        return inp
    _L0_xattn_all = _L0_xattn_setup()
    _L0_xattn_in = {k: v for k, v in _L0_xattn_all.items() if k in ('Wq', 'bq', 'Wk', 'bk', 'Wv', 'bv', 'Wo', 'bo')}
    del _L0_xattn_all

    def _L0_ffn_setup():
        import jax, jax.numpy as jnp
        import numpy as np
        S_LEN, BATCH, HIDDEN = (512, 2, 256)
        N_HEADS, N_KV = (16, 8)
        N_EXP, TOP_K, CAP_F = (8, 2, 1.25)
        FFN = 1024
        HEAD_DIM = HIDDEN // N_HEADS
        Q_PER_KV = N_HEADS // N_KV
        EPS = 1e-05
        NEG = -1000000000.0

        def _ln(x, w, b):
            mu = jnp.mean(x, -1, keepdims=True)
            var = jnp.var(x, -1, keepdims=True)
            return (x - mu) * jax.lax.rsqrt(var + EPS) * w + b

        def _forward(hidden_states, ln1_weight, ln1_bias, ln2_weight, ln2_bias, qkv_weight, proj_weight, router_weight, moe_w1, moe_w2):
            S, B, H = hidden_states.shape
            ln1 = _ln(hidden_states, ln1_weight, ln1_bias)
            qkv = (ln1 @ qkv_weight.T).reshape(S, B, N_KV, (Q_PER_KV + 2) * HEAD_DIM)
            q_dim = Q_PER_KV * HEAD_DIM
            q = qkv[..., :q_dim].reshape(S, B, N_HEADS, HEAD_DIM)
            k = jnp.repeat(qkv[..., q_dim:q_dim + HEAD_DIM], Q_PER_KV, axis=2)
            v = jnp.repeat(qkv[..., q_dim + HEAD_DIM:], Q_PER_KV, axis=2)
            scores = jnp.einsum('sbhd,tbhd->bhst', q, k) / jnp.sqrt(jnp.float32(HEAD_DIM))
            causal = jnp.tril(jnp.ones((S, S), bool))
            attn = jax.nn.softmax(jnp.where(causal[None, None], scores, NEG), axis=-1)
            attn_out = jnp.einsum('bhst,tbhd->sbhd', attn, v).reshape(S, B, H)
            hidden_after_attn = hidden_states + attn_out @ proj_weight.T
            x = _ln(hidden_after_attn, ln2_weight, ln2_bias).reshape(-1, H)
            N = S * B
            probs = jax.nn.softmax(x.astype(jnp.float32) @ router_weight, axis=-1)
            top_p, top_i = jax.lax.top_k(probs, TOP_K)
            top_p = top_p / jnp.sum(top_p, -1, keepdims=True)
            flat_exp = top_i.reshape(-1)
            order = jnp.argsort(flat_exp)
            sorted_exp = flat_exp[order]
            counts = jnp.bincount(sorted_exp, length=N_EXP)
            offsets = jnp.concatenate([jnp.zeros((1,), counts.dtype), jnp.cumsum(counts)])
            within = jnp.arange(N * TOP_K) - offsets[sorted_exp]
            cap = int(np.ceil(N * TOP_K / N_EXP * CAP_F))
            keep = within < cap
            slot = jnp.where(keep, sorted_exp * cap + within, N_EXP * cap)
            tok_id = order // TOP_K
            padded_tokens = jnp.zeros((N_EXP * cap + 1, H), x.dtype).at[slot].set(x[tok_id])[:-1]
            padded_probs = jnp.zeros((N_EXP * cap + 1,), jnp.float32).at[slot].set(top_p.reshape(-1)[order])[:-1]
            padded_ids = jnp.zeros((N_EXP * cap + 1,), jnp.int32).at[slot].set(tok_id.astype(jnp.int32))[:-1]
            exp_in = padded_tokens.reshape(N_EXP, cap, H)
            act = jax.nn.gelu(jnp.einsum('ech,ehf->ecf', exp_in, moe_w1), approximate=False)
            exp_out = jnp.einsum('ecf,efh->ech', act, moe_w2).reshape(N_EXP * cap, H)
            weighted = exp_out * padded_probs[:, None].astype(exp_out.dtype)
            moe = jnp.zeros((N, H), exp_out.dtype).at[padded_ids].add(weighted)
            return hidden_after_attn + moe.reshape(S, B, H)
        ks = jax.random.split(jax.random.key(seed), 6)
        qkv_out = N_KV * (Q_PER_KV + 2) * HEAD_DIM
        sc = 0.02
        return {'hidden_states': jax.random.normal(ks[0], (S_LEN, BATCH, HIDDEN), jnp.float32), 'ln1_weight': jnp.ones((HIDDEN,), jnp.float32), 'ln1_bias': jnp.zeros((HIDDEN,), jnp.float32), 'ln2_weight': jnp.ones((HIDDEN,), jnp.float32), 'ln2_bias': jnp.zeros((HIDDEN,), jnp.float32), 'qkv_weight': jax.random.normal(ks[1], (qkv_out, HIDDEN), jnp.float32) * sc, 'proj_weight': jax.random.normal(ks[2], (HIDDEN, HIDDEN), jnp.float32) * sc, 'router_weight': jax.random.normal(ks[3], (HIDDEN, N_EXP), jnp.float32) * sc, 'moe_w1': jax.random.normal(ks[4], (N_EXP, HIDDEN, FFN), jnp.float32) * sc, 'moe_w2': jax.random.normal(ks[5], (N_EXP, FFN, HIDDEN), jnp.float32) * sc}
    _L0_ffn_all = _L0_ffn_setup()
    _L0_ffn_in = {k: v for k, v in _L0_ffn_all.items() if k in ('ln1_weight', 'ln1_bias', 'ln2_weight', 'ln2_bias', 'qkv_weight', 'proj_weight', 'router_weight', 'moe_w1', 'moe_w2')}
    del _L0_ffn_all

    def _L1_attn_setup():
        import jax, jax.numpy as jnp
        import numpy as np
        D = 256
        D_FFN = 512
        CHUNK = 64

        def rms_norm(x, g, eps=1e-06):
            norm = jax.lax.rsqrt(jnp.mean(x * x, axis=-1, keepdims=True) + eps)
            return x * norm * g

        def bit_linear(x, w):
            x_scale = jnp.clip(jnp.max(jnp.abs(x), axis=-1, keepdims=True), 1e-05, None)
            x_q = jnp.clip(jnp.round(x / x_scale * 127.0), -128, 127)
            w_mean = jnp.mean(w)
            w_c = w - w_mean
            w_scale = jnp.clip(jnp.mean(jnp.abs(w_c)), 1e-05, None)
            w_q = jnp.clip(jnp.round(w_c / w_scale), -1, 1)
            y = jnp.einsum('bsi,oi->bso', x_q, w_q) * (w_scale * x_scale / 127.0)
            return y

        def chunked_scan(decay, value, chunk_size=CHUNK):
            b, s, d = decay.shape
            pad = (chunk_size - s % chunk_size) % chunk_size
            if pad > 0:
                decay = jnp.pad(decay, ((0, 0), (0, pad), (0, 0)), constant_values=1.0)
                value = jnp.pad(value, ((0, 0), (0, pad), (0, 0)), constant_values=0.0)
            n = (s + pad) // chunk_size
            dc = decay.reshape(b, n, chunk_size, d)
            vc = value.reshape(b, n, chunk_size, d)
            log_dc = jnp.log(jnp.clip(dc, 1e-10, None))
            cum_decay = jnp.exp(jnp.cumsum(log_dc, axis=2))
            weighted = vc / jnp.clip(cum_decay, 1e-10, None)
            intra = cum_decay * jnp.cumsum(weighted, axis=2)
            cd_t = jnp.moveaxis(cum_decay, 1, 0)
            in_t = jnp.moveaxis(intra, 1, 0)

            def step(state, inputs):
                cd_c, intra_c = inputs
                chunk_states = intra_c + cd_c * state[:, None, :]
                return (chunk_states[:, -1], chunk_states)
            init = jnp.zeros((b, d), dtype=decay.dtype)
            _, states = jax.lax.scan(step, init, (cd_t, in_t))
            states = jnp.moveaxis(states, 0, 1).reshape(b, n * chunk_size, d)
            return states[:, :s]

        def make_decay_bias(d):
            q = d // 4
            return jnp.concatenate([jnp.full((q,), -2.2, jnp.float32), jnp.zeros((2 * q,), jnp.float32), jnp.full((d - 3 * q,), 4.6, jnp.float32)])
        key = jax.random.key(seed)
        ks = jax.random.split(key, 7)
        b, s = (4, 1024)
        return {'x': jax.random.normal(ks[0], (b, s, D), jnp.float32), 'w_gate': jax.random.normal(ks[1], (D_FFN, D), jnp.float32) * 0.02, 'w_down': jax.random.normal(ks[2], (D, D_FFN), jnp.float32) * 0.02, 'w_a': jax.random.normal(ks[3], (D, D), jnp.float32) * 0.02, 'w_i': jax.random.normal(ks[4], (D, D), jnp.float32) * 0.02, 'w_v': jax.random.normal(ks[5], (D, D), jnp.float32) * 0.02, 'decay_bias': make_decay_bias(D), 'g_pre': jnp.ones((D,), jnp.float32), 'g_post': jnp.ones((D,), jnp.float32)}
    _L1_attn_all = _L1_attn_setup()
    _L1_attn_in = {k: v for k, v in _L1_attn_all.items() if k in ('w_gate', 'w_down', 'w_a', 'w_i', 'w_v', 'decay_bias', 'g_pre', 'g_post')}
    del _L1_attn_all

    def _L1_xattn_setup():
        import jax, jax.numpy as jnp
        import numpy as np
        HEADS = 8
        DIM_HEAD = 64
        SCALE = 8.0
        EPS = 1e-05

        def layer_norm(x, g, b):
            mu = jnp.mean(x, axis=-1, keepdims=True)
            var = jnp.mean((x - mu) ** 2, axis=-1, keepdims=True)
            return (x - mu) * jax.lax.rsqrt(var + EPS) * g + b
        key = jax.random.key(seed)
        ks = jax.random.split(key, 6)
        b, n, dim = (4, 1024, 256)
        inner = HEADS * DIM_HEAD
        return {'x': jax.random.normal(ks[0], (b, n, dim), jnp.float32), 'context': jax.random.normal(ks[1], (b, n, dim), jnp.float32), 'Wq': jax.random.normal(ks[2], (dim, inner), jnp.float32) * 0.03, 'Wkv': jax.random.normal(ks[3], (dim, 2 * inner), jnp.float32) * 0.03, 'null_kv': jax.random.normal(ks[4], (2, DIM_HEAD), jnp.float32), 'ln_q_g': jnp.ones((inner,), jnp.float32), 'ln_q_b': jnp.zeros((inner,), jnp.float32), 'ln_out_g': jnp.ones((inner,), jnp.float32), 'ln_out_b': jnp.zeros((inner,), jnp.float32), 'Wout': jax.random.normal(ks[5], (inner, dim), jnp.float32) * 0.03}
    _L1_xattn_all = _L1_xattn_setup()
    _L1_xattn_in = {k: v for k, v in _L1_xattn_all.items() if k in ('Wq', 'Wkv', 'null_kv', 'ln_q_g', 'ln_q_b', 'ln_out_g', 'ln_out_b', 'Wout')}
    del _L1_xattn_all

    def _L1_ffn_setup():
        import jax, jax.numpy as jnp
        import numpy as np
        EPS = 1e-05
        key = jax.random.key(seed)
        kx, kw, kb = jax.random.split(key, 3)
        B, S, K, N = (8, 2048, 256, 256)
        x = jax.random.normal(kx, (B, S, K), dtype=jnp.float32)
        W = jax.random.normal(kw, (N, K), dtype=jnp.float32) * 0.02
        weight_scale = jnp.maximum(jnp.max(jnp.abs(W), axis=1, keepdims=True) / 127.0, EPS)
        weight_int8 = jnp.clip(jnp.round(W / weight_scale), -128, 127).astype(jnp.int8)
        bias = jax.random.normal(kb, (N,), dtype=jnp.float32) * 0.01
        return {'x': x, 'weight_int8': weight_int8, 'weight_scale': weight_scale, 'bias': bias}
    _L1_ffn_all = _L1_ffn_setup()
    _L1_ffn_in = {k: v for k, v in _L1_ffn_all.items() if k in ('weight_int8', 'weight_scale', 'bias')}
    del _L1_ffn_all
    return {'x': x, 'ctx_1024': ctx_1024, 'L0_attn_Wq': _L0_attn_in['Wq'], 'L0_attn_bq': _L0_attn_in['bq'], 'L0_attn_Wk': _L0_attn_in['Wk'], 'L0_attn_bk': _L0_attn_in['bk'], 'L0_attn_Wv': _L0_attn_in['Wv'], 'L0_attn_bv': _L0_attn_in['bv'], 'L0_attn_Wu': _L0_attn_in['Wu'], 'L0_attn_bu': _L0_attn_in['bu'], 'L0_attn_Wo': _L0_attn_in['Wo'], 'L0_attn_bo': _L0_attn_in['bo'], 'L0_attn_scale': _L0_attn_in['scale'], 'L0_xattn_Wq': _L0_xattn_in['Wq'], 'L0_xattn_bq': _L0_xattn_in['bq'], 'L0_xattn_Wk': _L0_xattn_in['Wk'], 'L0_xattn_bk': _L0_xattn_in['bk'], 'L0_xattn_Wv': _L0_xattn_in['Wv'], 'L0_xattn_bv': _L0_xattn_in['bv'], 'L0_xattn_Wo': _L0_xattn_in['Wo'], 'L0_xattn_bo': _L0_xattn_in['bo'], 'L0_ffn_ln1_weight': _L0_ffn_in['ln1_weight'], 'L0_ffn_ln1_bias': _L0_ffn_in['ln1_bias'], 'L0_ffn_ln2_weight': _L0_ffn_in['ln2_weight'], 'L0_ffn_ln2_bias': _L0_ffn_in['ln2_bias'], 'L0_ffn_qkv_weight': _L0_ffn_in['qkv_weight'], 'L0_ffn_proj_weight': _L0_ffn_in['proj_weight'], 'L0_ffn_router_weight': _L0_ffn_in['router_weight'], 'L0_ffn_moe_w1': _L0_ffn_in['moe_w1'], 'L0_ffn_moe_w2': _L0_ffn_in['moe_w2'], 'L1_attn_w_gate': _L1_attn_in['w_gate'], 'L1_attn_w_down': _L1_attn_in['w_down'], 'L1_attn_w_a': _L1_attn_in['w_a'], 'L1_attn_w_i': _L1_attn_in['w_i'], 'L1_attn_w_v': _L1_attn_in['w_v'], 'L1_attn_decay_bias': _L1_attn_in['decay_bias'], 'L1_attn_g_pre': _L1_attn_in['g_pre'], 'L1_attn_g_post': _L1_attn_in['g_post'], 'L1_xattn_Wq': _L1_xattn_in['Wq'], 'L1_xattn_Wkv': _L1_xattn_in['Wkv'], 'L1_xattn_null_kv': _L1_xattn_in['null_kv'], 'L1_xattn_ln_q_g': _L1_xattn_in['ln_q_g'], 'L1_xattn_ln_q_b': _L1_xattn_in['ln_q_b'], 'L1_xattn_ln_out_g': _L1_xattn_in['ln_out_g'], 'L1_xattn_ln_out_b': _L1_xattn_in['ln_out_b'], 'L1_xattn_Wout': _L1_xattn_in['Wout'], 'L1_ffn_weight_int8': _L1_ffn_in['weight_int8'], 'L1_ffn_weight_scale': _L1_ffn_in['weight_scale'], 'L1_ffn_bias': _L1_ffn_in['bias']}

def reference(x, ctx_1024, L0_attn_Wq, L0_attn_bq, L0_attn_Wk, L0_attn_bk, L0_attn_Wv, L0_attn_bv, L0_attn_Wu, L0_attn_bu, L0_attn_Wo, L0_attn_bo, L0_attn_scale, L0_xattn_Wq, L0_xattn_bq, L0_xattn_Wk, L0_xattn_bk, L0_xattn_Wv, L0_xattn_bv, L0_xattn_Wo, L0_xattn_bo, L0_ffn_ln1_weight, L0_ffn_ln1_bias, L0_ffn_ln2_weight, L0_ffn_ln2_bias, L0_ffn_qkv_weight, L0_ffn_proj_weight, L0_ffn_router_weight, L0_ffn_moe_w1, L0_ffn_moe_w2, L1_attn_w_gate, L1_attn_w_down, L1_attn_w_a, L1_attn_w_i, L1_attn_w_v, L1_attn_decay_bias, L1_attn_g_pre, L1_attn_g_post, L1_xattn_Wq, L1_xattn_Wkv, L1_xattn_null_kv, L1_xattn_ln_q_g, L1_xattn_ln_q_b, L1_xattn_ln_out_g, L1_xattn_ln_out_b, L1_xattn_Wout, L1_ffn_weight_int8, L1_ffn_weight_scale, L1_ffn_bias):
    import jax
    import jax.numpy as jnp

    def _L0_attn_ref(x, Wq, bq, Wk, bk, Wv, bv, Wu, bu, Wo, bo, scale):
        import jax, jax.numpy as jnp
        import numpy as np
        B, N, E, H = (2, 512, 256, 8)
        HID = 256
        D = HID // H
        EPS = 1e-08

        def rms_norm(x, scale):
            rms = jnp.linalg.norm(x, axis=-1, keepdims=True) * x.shape[-1] ** (-0.5)
            return scale * (x / (rms + EPS))
        n = x.shape[-2]
        q = x @ Wq.T + bq
        u = x @ Wu.T + bu
        k = x @ Wk.T + bk
        v = x @ Wv.T + bv
        u = jax.nn.silu(u)
        v = jax.nn.silu(v)
        to_heads = lambda t: t.reshape(*t.shape[:-1], H, D).swapaxes(-3, -2)
        q, k, v = map(to_heads, (q, k, v))
        q = jax.nn.elu(q)
        k = jax.nn.elu(k)
        mask = jnp.tril(jnp.ones((n, n), q.dtype))
        energy = jnp.einsum('bhnd,bhmd->bhnm', q, k) * mask
        out = jnp.einsum('bhnm,bhmd->bhnd', energy, v)
        out = out.swapaxes(-3, -2).reshape(*x.shape[:-1], HID)
        out = rms_norm(out, scale)
        out = u * out
        return out @ Wo.T + bo

    def _L0_xattn_ref(queries, keys, values, Wq, bq, Wk, bk, Wv, bv, Wo, bo):
        import jax, jax.numpy as jnp
        import numpy as np
        import math
        D_MODEL = 256
        N_HEADS = 16
        D_HEAD = D_MODEL // N_HEADS
        N, L, _ = queries.shape
        S = keys.shape[1]
        H, D = (N_HEADS, D_HEAD)
        q = (queries @ Wq + bq).reshape(N, L, H, D)
        k = (keys @ Wk + bk).reshape(N, S, H, D)
        v = (values @ Wv + bv).reshape(N, S, H, D)
        sm = jnp.einsum('nlhd,nshd->nlhs', q, k) / math.sqrt(D)
        sm = jax.nn.softmax(sm, axis=1)
        attn = jnp.einsum('nlhs,nshd->nlhd', sm, v).reshape(N, L, H * D)
        return attn @ Wo + bo

    def _L0_ffn_ref(hidden_states, ln1_weight, ln1_bias, ln2_weight, ln2_bias, qkv_weight, proj_weight, router_weight, moe_w1, moe_w2):
        import jax, jax.numpy as jnp
        import numpy as np
        S_LEN, BATCH, HIDDEN = (512, 2, 256)
        N_HEADS, N_KV = (16, 8)
        N_EXP, TOP_K, CAP_F = (8, 2, 1.25)
        FFN = 1024
        HEAD_DIM = HIDDEN // N_HEADS
        Q_PER_KV = N_HEADS // N_KV
        EPS = 1e-05
        NEG = -1000000000.0

        def _ln(x, w, b):
            mu = jnp.mean(x, -1, keepdims=True)
            var = jnp.var(x, -1, keepdims=True)
            return (x - mu) * jax.lax.rsqrt(var + EPS) * w + b

        def _forward(hidden_states, ln1_weight, ln1_bias, ln2_weight, ln2_bias, qkv_weight, proj_weight, router_weight, moe_w1, moe_w2):
            S, B, H = hidden_states.shape
            ln1 = _ln(hidden_states, ln1_weight, ln1_bias)
            qkv = (ln1 @ qkv_weight.T).reshape(S, B, N_KV, (Q_PER_KV + 2) * HEAD_DIM)
            q_dim = Q_PER_KV * HEAD_DIM
            q = qkv[..., :q_dim].reshape(S, B, N_HEADS, HEAD_DIM)
            k = jnp.repeat(qkv[..., q_dim:q_dim + HEAD_DIM], Q_PER_KV, axis=2)
            v = jnp.repeat(qkv[..., q_dim + HEAD_DIM:], Q_PER_KV, axis=2)
            scores = jnp.einsum('sbhd,tbhd->bhst', q, k) / jnp.sqrt(jnp.float32(HEAD_DIM))
            causal = jnp.tril(jnp.ones((S, S), bool))
            attn = jax.nn.softmax(jnp.where(causal[None, None], scores, NEG), axis=-1)
            attn_out = jnp.einsum('bhst,tbhd->sbhd', attn, v).reshape(S, B, H)
            hidden_after_attn = hidden_states + attn_out @ proj_weight.T
            x = _ln(hidden_after_attn, ln2_weight, ln2_bias).reshape(-1, H)
            N = S * B
            probs = jax.nn.softmax(x.astype(jnp.float32) @ router_weight, axis=-1)
            top_p, top_i = jax.lax.top_k(probs, TOP_K)
            top_p = top_p / jnp.sum(top_p, -1, keepdims=True)
            flat_exp = top_i.reshape(-1)
            order = jnp.argsort(flat_exp)
            sorted_exp = flat_exp[order]
            counts = jnp.bincount(sorted_exp, length=N_EXP)
            offsets = jnp.concatenate([jnp.zeros((1,), counts.dtype), jnp.cumsum(counts)])
            within = jnp.arange(N * TOP_K) - offsets[sorted_exp]
            cap = int(np.ceil(N * TOP_K / N_EXP * CAP_F))
            keep = within < cap
            slot = jnp.where(keep, sorted_exp * cap + within, N_EXP * cap)
            tok_id = order // TOP_K
            padded_tokens = jnp.zeros((N_EXP * cap + 1, H), x.dtype).at[slot].set(x[tok_id])[:-1]
            padded_probs = jnp.zeros((N_EXP * cap + 1,), jnp.float32).at[slot].set(top_p.reshape(-1)[order])[:-1]
            padded_ids = jnp.zeros((N_EXP * cap + 1,), jnp.int32).at[slot].set(tok_id.astype(jnp.int32))[:-1]
            exp_in = padded_tokens.reshape(N_EXP, cap, H)
            act = jax.nn.gelu(jnp.einsum('ech,ehf->ecf', exp_in, moe_w1), approximate=False)
            exp_out = jnp.einsum('ecf,efh->ech', act, moe_w2).reshape(N_EXP * cap, H)
            weighted = exp_out * padded_probs[:, None].astype(exp_out.dtype)
            moe = jnp.zeros((N, H), exp_out.dtype).at[padded_ids].add(weighted)
            return hidden_after_attn + moe.reshape(S, B, H)
        return _forward(hidden_states, ln1_weight, ln1_bias, ln2_weight, ln2_bias, qkv_weight, proj_weight, router_weight, moe_w1, moe_w2)

    def _L1_attn_ref(x, w_gate, w_down, w_a, w_i, w_v, decay_bias, g_pre, g_post):
        import jax, jax.numpy as jnp
        import numpy as np
        D = 256
        D_FFN = 512
        CHUNK = 64

        def rms_norm(x, g, eps=1e-06):
            norm = jax.lax.rsqrt(jnp.mean(x * x, axis=-1, keepdims=True) + eps)
            return x * norm * g

        def bit_linear(x, w):
            x_scale = jnp.clip(jnp.max(jnp.abs(x), axis=-1, keepdims=True), 1e-05, None)
            x_q = jnp.clip(jnp.round(x / x_scale * 127.0), -128, 127)
            w_mean = jnp.mean(w)
            w_c = w - w_mean
            w_scale = jnp.clip(jnp.mean(jnp.abs(w_c)), 1e-05, None)
            w_q = jnp.clip(jnp.round(w_c / w_scale), -1, 1)
            y = jnp.einsum('bsi,oi->bso', x_q, w_q) * (w_scale * x_scale / 127.0)
            return y

        def chunked_scan(decay, value, chunk_size=CHUNK):
            b, s, d = decay.shape
            pad = (chunk_size - s % chunk_size) % chunk_size
            if pad > 0:
                decay = jnp.pad(decay, ((0, 0), (0, pad), (0, 0)), constant_values=1.0)
                value = jnp.pad(value, ((0, 0), (0, pad), (0, 0)), constant_values=0.0)
            n = (s + pad) // chunk_size
            dc = decay.reshape(b, n, chunk_size, d)
            vc = value.reshape(b, n, chunk_size, d)
            log_dc = jnp.log(jnp.clip(dc, 1e-10, None))
            cum_decay = jnp.exp(jnp.cumsum(log_dc, axis=2))
            weighted = vc / jnp.clip(cum_decay, 1e-10, None)
            intra = cum_decay * jnp.cumsum(weighted, axis=2)
            cd_t = jnp.moveaxis(cum_decay, 1, 0)
            in_t = jnp.moveaxis(intra, 1, 0)

            def step(state, inputs):
                cd_c, intra_c = inputs
                chunk_states = intra_c + cd_c * state[:, None, :]
                return (chunk_states[:, -1], chunk_states)
            init = jnp.zeros((b, d), dtype=decay.dtype)
            _, states = jax.lax.scan(step, init, (cd_t, in_t))
            states = jnp.moveaxis(states, 0, 1).reshape(b, n * chunk_size, d)
            return states[:, :s]

        def make_decay_bias(d):
            q = d // 4
            return jnp.concatenate([jnp.full((q,), -2.2, jnp.float32), jnp.zeros((2 * q,), jnp.float32), jnp.full((d - 3 * q,), 4.6, jnp.float32)])
        h = rms_norm(x, g_pre)
        a = jax.nn.sigmoid(bit_linear(h, w_a) + decay_bias)
        i_gate = jax.nn.sigmoid(bit_linear(h, w_i))
        v = bit_linear(h, w_v)
        input_signal = jnp.sqrt(jnp.clip(1.0 - a * a, 1e-08, None)) * (i_gate * v)
        rec_out = chunked_scan(a, input_signal)
        ffn_out = bit_linear(jax.nn.silu(bit_linear(rms_norm(rec_out, g_post), w_gate)), w_down)
        return x + rec_out + ffn_out

    def _L1_xattn_ref(x, context, Wq, Wkv, null_kv, ln_q_g, ln_q_b, ln_out_g, ln_out_b, Wout):
        import jax, jax.numpy as jnp
        import numpy as np
        HEADS = 8
        DIM_HEAD = 64
        SCALE = 8.0
        EPS = 1e-05

        def layer_norm(x, g, b):
            mu = jnp.mean(x, axis=-1, keepdims=True)
            var = jnp.mean((x - mu) ** 2, axis=-1, keepdims=True)
            return (x - mu) * jax.lax.rsqrt(var + EPS) * g + b
        b, n, _ = x.shape
        m = context.shape[1]
        h, d = (HEADS, DIM_HEAD)
        q = x @ Wq
        kv = context @ Wkv
        k, v = jnp.split(kv, 2, axis=-1)
        q = layer_norm(q, ln_q_g, ln_q_b)
        split = lambda t: t.reshape(t.shape[0], t.shape[1], h, d).transpose(0, 2, 1, 3)
        q, k, v = (split(q), split(k), split(v))
        nk = jnp.broadcast_to(null_kv[0], (b, h, 1, d))
        nv = jnp.broadcast_to(null_kv[1], (b, h, 1, d))
        k = jnp.concatenate([nk, k], axis=2)
        v = jnp.concatenate([nv, v], axis=2)
        q = jax.nn.softmax(q, axis=-1) * SCALE
        k = jax.nn.softmax(k, axis=2)
        ctx = jnp.einsum('bhnd,bhne->bhde', k, v)
        out = jnp.einsum('bhnd,bhde->bhne', q, ctx)
        out = out.transpose(0, 2, 1, 3).reshape(b, n, h * d)
        out = layer_norm(out, ln_out_g, ln_out_b)
        return out @ Wout

    def _L1_ffn_ref(x, weight_int8, weight_scale, bias):
        import jax, jax.numpy as jnp
        import numpy as np
        EPS = 1e-05
        B, S, K = x.shape
        x2 = x.reshape(-1, K)
        x_scale = jnp.maximum(jnp.abs(x2).max() / 127.0, EPS)
        x_int8 = jnp.clip(jnp.round(x2 / x_scale), -128, 127).astype(jnp.int8)
        acc_i32 = jax.lax.dot_general(x_int8, weight_int8.T, dimension_numbers=(((1,), (0,)), ((), ())), preferred_element_type=jnp.int32)
        out = acc_i32.astype(jnp.float32) * x_scale * weight_scale.T
        out = out + bias
        return out.reshape(B, S, -1)
    x = x + _L0_attn_ref(_layernorm(x, axis=-1), L0_attn_Wq, L0_attn_bq, L0_attn_Wk, L0_attn_bk, L0_attn_Wv, L0_attn_bv, L0_attn_Wu, L0_attn_bu, L0_attn_Wo, L0_attn_bo, L0_attn_scale)
    x = x + _L0_xattn_ref(_layernorm(x, axis=-1), ctx_1024, ctx_1024, L0_xattn_Wq, L0_xattn_bq, L0_xattn_Wk, L0_xattn_bk, L0_xattn_Wv, L0_xattn_bv, L0_xattn_Wo, L0_xattn_bo)
    x = x + _L0_ffn_ref(_layernorm(x, axis=-1), L0_ffn_ln1_weight, L0_ffn_ln1_bias, L0_ffn_ln2_weight, L0_ffn_ln2_bias, L0_ffn_qkv_weight, L0_ffn_proj_weight, L0_ffn_router_weight, L0_ffn_moe_w1, L0_ffn_moe_w2)
    x = x + _L1_attn_ref(_layernorm(x, axis=-1), L1_attn_w_gate, L1_attn_w_down, L1_attn_w_a, L1_attn_w_i, L1_attn_w_v, L1_attn_decay_bias, L1_attn_g_pre, L1_attn_g_post)
    x = x + _L1_xattn_ref(_layernorm(x, axis=-1), ctx_1024, L1_xattn_Wq, L1_xattn_Wkv, L1_xattn_null_kv, L1_xattn_ln_q_g, L1_xattn_ln_q_b, L1_xattn_ln_out_g, L1_xattn_ln_out_b, L1_xattn_Wout)
    x = x + _L1_ffn_ref(_layernorm(x, axis=-1), L1_ffn_weight_int8, L1_ffn_weight_scale, L1_ffn_bias)
    return x

_drawn_inputs = setup_inputs


def setup_inputs(seed=0):
    import zlib

    import numpy as np

    out = dict(_drawn_inputs(seed))
    spreads = {'L0_attn_bq': (0.0, 0.739),
     'L0_attn_bk': (0.0, 0.343),
     'L0_attn_bv': (0.0, 0.36),
     'L0_attn_bu': (0.0, 0.6),
     'L0_attn_bo': (0.0, 0.1),
     'L0_attn_scale': (1.0, 0.6),
     'L0_xattn_bq': (0.0, 2.0),
     'L0_xattn_bk': (0.0, 0.1),
     'L0_xattn_bv': (0.0, 0.1),
     'L0_xattn_bo': (0.0, 0.1),
     'L0_ffn_ln1_weight': (1.0, 0.6),
     'L0_ffn_ln1_bias': (0.0, 0.8),
     'L0_ffn_ln2_weight': (1.0, 0.6),
     'L0_ffn_ln2_bias': (0.0, 0.755),
     'L1_attn_g_pre': (1.0, 0.6),
     'L1_attn_g_post': (1.0, 0.6),
     'L1_xattn_ln_q_g': (1.0, 0.6),
     'L1_xattn_ln_q_b': (0.0, 2.0),
     'L1_xattn_ln_out_g': (1.0, 0.6),
     'L1_xattn_ln_out_b': (0.0, 0.489)}
    factors = {'L0_ffn_qkv_weight': 4.321,
     'L0_ffn_proj_weight': 4.077,
     'L0_ffn_router_weight': 2.713,
     'L1_attn_w_gate': 7.109,
     'L1_attn_w_down': 7.129,
     'L1_attn_w_a': 8.0,
     'L1_attn_w_i': 8.0,
     'L1_xattn_Wq': 8.0,
     'L1_xattn_null_kv': 8.0,
     'L1_ffn_weight_scale': 6.649,
     'L1_ffn_bias': 36.219,
     'L1_xattn_Wkv': 3.176}
    for name, (base, spread) in spreads.items():
        noise = np.random.default_rng([zlib.crc32(name.encode()), seed]).standard_normal(out[name].shape)
        drawn = base * np.exp(spread * noise) if base else spread * noise
        out[name] = jnp.asarray(drawn.astype(out[name].dtype))
    for name, factor in factors.items():
        out[name] = (out[name] * factor).astype(out[name].dtype)
    return out
```

```python
from contextlib import ExitStack, contextmanager

import concourse.bass as bass
from concourse import mybir

FP32 = mybir.dt.float32
BF16 = mybir.dt.bfloat16
I32 = mybir.dt.int32
I8 = mybir.dt.int8
ALU = mybir.AluOpType
ACT = mybir.ActivationFunctionType
AX = mybir.AxisListType

P = 128
NB, S, D = 32, 112, 256
T = 375
DC = D // P
TC, TN = 3, 125
TOK = NB * S
NT = TOK // P
NE, CAP, F = 8, 1120, 1024
ROWS = NE * CAP


@contextmanager
def semaphores(nc, prefix):
    made = []

    def sem(name):
        made.append(nc.alloc_semaphore(name=prefix + name))
        return made[-1]

    yield sem
    nc.clear_and_free_semaphores(made)
    nc.all_engine_barrier()


def later(k):
    return k >= 1 if isinstance(k, int) else True


def pipeline(eng, n, stages, unroll=2):
    most = max(lag for _, lag in stages)

    def step(k, p):
        for fn, lag in stages:
            q = p - lag
            kk, pp = k + q // unroll, q % unroll
            if isinstance(k, int) and not 0 <= unroll * kk + pp < n:
                continue
            fn(kk, pp)

    first = -(-(most + 2) // unroll)
    last = n // unroll
    for s in range(unroll * min(first, last)):
        step(s // unroll, s % unroll)
    if last > first:
        with eng.Fori(first, last) as k:
            for p in range(unroll):
                step(k, p)
    for s in range(n, n + most):
        step(s // unroll, s % unroll)


class Chain:

    def __init__(self, eng, sem):
        self.eng, self.sem, self.n = eng, sem, 0

    def begin(self):
        if self.n:
            self.eng.sem_clear(self.sem)
        self.n = 0

    def link(self, ins):
        self.n += 1
        ins.then_inc(self.sem, 1)
        self.eng.wait_ge(self.sem, self.n)


def rsqrt(nc, ch, y, v, t, ti):
    ch.link(nc.vector.tensor_scalar(ti, v.bitcast(I32), 1, None, ALU.logical_shift_right))
    ch.link(nc.vector.tensor_scalar(y.bitcast(I32), ti, -1.0, float(0x5F3759DF), ALU.mult, ALU.add))
    for _ in range(3):
        ch.link(nc.vector.scalar_tensor_tensor(t, y, -0.5, y, ALU.mult, ALU.mult))
        ch.link(nc.vector.tensor_tensor(t, t, v, ALU.mult))
        ch.link(nc.vector.scalar_tensor_tensor(y, t, 1.5, y, ALU.add, ALU.mult))


class Norm:

    def __init__(self, nc, sb, name, n, rows, eps):
        self.nc, self.eps, self.rows = nc, eps, rows
        self.st = sb(f"{name}_st", [n, rows, 6])
        self.mv = sb(f"{name}_mv", [n, rows, 2])
        self.ve = sb(f"{name}_ve", [n, rows])
        self.rs = sb(f"{name}_rs", [n, rows])
        self.t = sb(f"{name}_t", [n, rows])
        self.ti = sb(f"{name}_ti", [n, rows], I32)

    def stats(self, ch, src):
        nc = self.nc
        for r in range(self.rows):
            last = nc.vector.bn_stats(self.st[:, r, :], src(r))
        ch.link(last)
        for r in range(self.rows):
            last = nc.vector.bn_aggr(self.mv[:, r, :], self.st[:, r, :])
        ch.link(last)
        ch.link(nc.vector.tensor_scalar(self.ve[:], self.mv[:, :, 1], self.eps, None, ALU.add))
        rsqrt(nc, ch, self.rs[:], self.ve[:], self.t[:], self.ti[:])

    def apply(self, r, out, src):
        return self.nc.vector.tensor_scalar(out, src, self.mv[:, r, 0:1], self.rs[:, r:r + 1],
                                            ALU.subtract, ALU.mult)


class TokenRows:

    def __init__(self, nc, sb, sem, eps=1e-5, parts=8):
        self.nc, self.parts = nc, parts
        self.x = sb("x_all", [S, NB, D])
        self.norm = Norm(nc, sb, "ln_all", S, NB, eps)
        self.loaded = [sem(f"x_loaded{i}") for i in range(parts)]
        self.stored = sem("x_stored")

    def load(self, eng, x_in):
        per = NB // self.parts
        for i in range(self.parts):
            eng.dma_start(self.x[:, i * per:(i + 1) * per],
                          x_in[i * per:(i + 1) * per].rearrange("b s n -> s b n")).then_inc(self.loaded[i], 16)

    def stats(self, eng, ch):
        per = NB // self.parts

        def row(b):
            if b % per == 0:
                eng.wait_ge(self.loaded[b // per], 16)
            return self.x[:, b]

        self.norm.stats(ch, row)

    def batch(self, b, count=1):
        if count > 1:
            return self.x[:, bass.ds(b, count)]
        return self.x[:, b] if isinstance(b, int) else self.x[:, bass.ds(b, 1)].rearrange("s b n -> s (b n)")

    def normed(self, b, out):
        m = self.norm
        mean = m.mv[:, b, 0:1] if isinstance(b, int) else m.mv[:, bass.ds(b, 1), 0]
        scale = m.rs[:, b:b + 1] if isinstance(b, int) else m.rs[:, bass.ds(b, 1)]
        return self.nc.vector.tensor_scalar(out, self.batch(b), mean, scale, ALU.subtract, ALU.mult)


def constants(nc, keep):
    sb = lambda n, s, d=FP32: keep.enter_context(nc.sbuf_tensor(n, s, d))
    c = {}
    c["ident"] = sb("ident", [P, P])
    c["ones"] = sb("ones", [P, P])
    c["head32"] = sb("head32", [P, 4])
    c["head16"] = sb("head16", [P, 8])
    c["before"] = sb("before", [P, P])
    c["first"] = sb("first", [P, NE])
    c["expert_row"] = sb("expert_row", [P, NE])
    c["ident_bf"] = sb("ident_bf", [P, P], BF16)
    c["hidden_bf"] = sb("hidden_bf", [P, P], BF16)
    c["causal_half"] = sb("causal_half", [P, S])
    return c


def build_constants(nc, c, keep):
    made = keep.enter_context(nc.semaphore("constants_made"))
    with nc.Block() as block:

        @block.gpsimd
        def _(g):
            n = [0]

            def link(ins):
                n[0] += 1
                ins.then_inc(made, 1)
                g.wait_ge(made, n[0])

            def band(ap, lo, width, pattern_len):
                link(nc.gpsimd.affine_select(out=ap, in_=ap, compare_op=ALU.is_ge, fill=0.0, base=-lo,
                                             pattern=[[-width, pattern_len]], channel_multiplier=1))
                link(nc.gpsimd.affine_select(out=ap, in_=ap, compare_op=ALU.is_ge, fill=0.0,
                                             base=lo + width - 1, pattern=[[width, pattern_len]],
                                             channel_multiplier=-1))

            link(nc.gpsimd.memset(c["ones"][:], 1.0))
            link(nc.gpsimd.memset(c["ident"][:], 0.0))
            link(nc.gpsimd.affine_select(out=c["ident"][:], in_=c["ident"][:], compare_op=ALU.not_equal,
                                         fill=1.0, base=0, pattern=[[-1, P]], channel_multiplier=1))
            link(nc.gpsimd.memset(c["head32"][:], 1.0))
            band(c["head32"][:], 0, 32, 4)
            link(nc.gpsimd.tensor_copy(c["ident_bf"][:], c["ident"][:]))
            link(nc.gpsimd.memset(c["before"][:], 1.0))
            link(nc.gpsimd.affine_select(out=c["before"][:], in_=c["before"][:], compare_op=ALU.is_gt, fill=0.0,
                                         base=0, pattern=[[1, P]], channel_multiplier=-1))
            link(nc.gpsimd.iota(c["first"][:], pattern=[[-1, NE]], base=NE, channel_multiplier=0,
                                allow_small_or_imprecise_dtypes=True))
            link(nc.gpsimd.iota(c["expert_row"][:], pattern=[[CAP, NE]], base=-ROWS, channel_multiplier=0,
                                allow_small_or_imprecise_dtypes=True))
            link(nc.gpsimd.memset(c["hidden_bf"][:], -4e9))
            for d in range(P // 4):
                link(nc.gpsimd.affine_select(out=c["hidden_bf"][:], in_=c["hidden_bf"][:], compare_op=ALU.not_equal,
                                             fill=0.0, base=-4 * d, pattern=[[-1, P]], channel_multiplier=1))
            link(nc.gpsimd.memset(c["head16"][:], 1.0))
            band(c["head16"][:], 0, 16, 8)
            link(nc.gpsimd.memset(c["causal_half"][:], 0.5))
            link(nc.gpsimd.affine_select(out=c["causal_half"][:], in_=c["causal_half"][:],
                                         compare_op=ALU.is_ge, fill=0.0, base=0, pattern=[[1, S]],
                                         channel_multiplier=-1))


def linear_attention(nc, x_in, x_out, w, c):
    N2 = 2 * S
    UN = NB // 2
    with ExitStack() as own:
        sb = lambda n, s, d=FP32: own.enter_context(nc.sbuf_tensor("la_" + n, s, d))
        pb = lambda n: own.enter_context(nc.psum_tensor("la_ps_" + n, [P, 512], FP32))
        sem = own.enter_context(semaphores(nc, "la_"))
        two = lambda n: [sem(f"{n}{i}") for i in range(2)]

        wt = {m: sb("w" + m, [P, DC, D]) for m in "qkuvo"}
        bias = {m: sb("b" + m, [P, DC]) for m in "qku"}
        half_bu = sb("half_bu", [P, DC])
        scale = sb("scale", [P, DC])
        half_scale = sb("half_scale", [P, DC])
        bvo = {m: sb("bb" + m, [S, 2, D]) for m in "vo"}
        rows = TokenRows(nc, sb, sem)
        xn = sb("xn", [S, 2, D])
        xnT = sb("xnT", [P, DC, N2])
        e_q = sb("e_q", [P, DC, N2])
        e_k = sb("e_k", [P, DC, N2])
        th_u = sb("th_u", [P, DC, N2])
        u_b = sb("u_b", [P, DC, N2])
        kT = sb("kT", [P, 2, DC, N2])
        qT = sb("qT", [P, DC, N2])
        qm = sb("qm", [P, 2, DC, 2, 4, S])
        v_b = sb("v_b", [S, 2, D])
        th_v = sb("th_v", [S, 2, D])
        v_s = sb("v_s", [S, 2, 2, D])
        su = sb("su", [P, 2, DC, N2])
        en = sb("en", [S, 2, 4, S])
        oT = sb("oT", [P, DC, N2])
        sq = sb("sq", [P, DC, N2])
        gT = sb("gT", [P, DC, N2])

        ss = sb("ss", [S, 2])
        rr = sb("rr", [S, 2])
        rt = sb("rt", [S, 2])
        rti = sb("rti", [S, 2], I32)

        ps_t, ps_q, ps_k, ps_u, ps_v, ps_o = (pb(m) for m in ("t", "q", "k", "u", "v", "o"))
        ps_e = [pb("e0"), pb("e1")]

        weights = sem("weights_loaded")
        xb_done, xn_done, t_done, xnT_done = sem("xb_done"), sem("xn_done"), sem("t_done"), sem("xnT_done")
        q_done, k_done, u_done, v_done = (sem(m + "_done") for m in "qkuv")
        eq_done, ek_done, tu_done, ub_done, tv_done = (sem(m) for m in ("eq_done", "ek_done", "tu_done", "ub_done", "tv_done"))
        eluq_done, eluk_done, qm_done, vb_done, vs_done, su_done = (sem(m) for m in ("eluq_done", "eluk_done", "qm_done", "vb_done", "vs_done", "su_done"))
        e_done = two("e_done")
        em_done = two("em_done")
        o_done, oT_done, sq_done, g_done, ss_done, ssc_done, y_done, r_done = (
            sem(m) for m in ("o_done", "oT_done", "sq_done", "g_done", "ss_done", "ssc_done", "y_done", "r_done"))
        x2_done = two("x2_done")
        chain = sem("chain")

        block = own.enter_context(nc.Block())

        def item(k, p):
            return 2 * k + p

        def after(k, p, eng, s, per=1, back=1):
            if isinstance(k, int) and item(k, p) < back:
                return
            eng.wait_ge(s, (item(k, p) - back + 1) * per)

        @block.sync
        def _(sp):
            rows.load(sp, x_in)
            for m in "qkuvo":
                sp.dma_start(wt[m][:], w["W" + m].rearrange("(c p) n -> p c n", p=P)).then_inc(weights, 16)
            for m in "qku":
                sp.dma_start(bias[m][:], w["b" + m].rearrange("(c p) -> p c", p=P),
                             allow_slow_non_contiguous=True).then_inc(weights, 16)
            sp.dma_start(scale[:], w["scale"].rearrange("(c p) -> p c", p=P),
                             allow_slow_non_contiguous=True).then_inc(weights, 16)
            for m in "vo":
                for b in range(2):
                    sp.dma_start(bvo[m][:, b], w["b" + m].rearrange("(a n) -> a n", a=1).to_broadcast([S, D])).then_inc(weights, 16)



            def store(k, p):
                sp.wait_ge(x2_done[p], k + 1)
                dst = x_out[bass.ds(2 * item(k, p), 2)] if not isinstance(k, int) else x_out[2 * item(k, p):2 * item(k, p) + 2]
                sp.dma_start(dst.rearrange("b s n -> s b n"), rows.batch(2 * item(k, p), 2)).then_inc(rows.stored, 16)

            pipeline(sp, UN, [(store, 2)])
            sp.wait_ge(rows.stored, 16 * UN)

        @block.gpsimd
        def _(g):
            g.wait_ge(weights, 16 * 13)

            def biased(k, p):
                g.wait_ge(xn_done, item(k, p) + 1)
                x = rows.batch(2 * item(k, p), 2)
                nc.gpsimd.tensor_tensor(x, x, bvo["o"][:], ALU.add).then_inc(xb_done, 1)

            pipeline(g, UN, [(biased, 0)])

        @block.vector
        def _(dve):
            ch = Chain(dve, chain)
            rows.stats(dve, ch)
            dve.wait_ge(weights, 16 * 13)
            ch.link(nc.vector.tensor_scalar(half_bu[:], bias["u"][:], 0.5, None, ALU.mult))
            ch.link(nc.vector.tensor_scalar(half_scale[:], scale[:], 0.5, None, ALU.mult))



            def norm(k, p):
                after(k, p, dve, t_done)
                rows.normed(2 * item(k, p), xn[:, 0])
                rows.normed(2 * item(k, p) + 1, xn[:, 1]).then_inc(xn_done, 1)

            def elu(k, p, dst, e, done, ps, b, elu_done):
                dve.wait_ge(done, item(k, p) + 1)
                ch.link(nc.vector.tensor_scalar(e[:], e[:], 1.0, -1.0, ALU.min, ALU.add))
                for i in range(DC):
                    last = nc.vector.scalar_tensor_tensor(dst[:, i], ps[:, i * N2:(i + 1) * N2], b[:, i:i + 1],
                                                          e[:, i], ALU.add, ALU.max)
                last.then_inc(elu_done, 1)

            def elu_k(k, p):
                ch.begin()
                after(k, p, dve, e_done[0], 2, 2)
                after(k, p, dve, e_done[1], 2, 2)
                elu(k, p, kT[:, p], e_k, ek_done, ps_k, bias["k"], eluk_done)

            def elu_q(k, p):
                ch.begin()
                after(k, p, dve, qm_done)
                elu(k, p, qT, e_q, eq_done, ps_q, bias["q"], eluq_done)

            def masked_q(k, p):
                after(k, p, dve, e_done[0], 2, 2)
                after(k, p, dve, e_done[1], 2, 2)
                dve.wait_ge(eluq_done, item(k, p) + 1)
                for j in range(4):
                    for i in range(DC):
                        last = nc.vector.tensor_scalar(qm[:, p, i, :, j, :], qT[:, i].rearrange("p (b n) -> p b n", b=2),
                                                       c["head32"][:, j:j + 1], None, ALU.mult)
                last.then_inc(qm_done, 1)
            def products(k, p):
                dve.wait_ge(v_done, item(k, p) + 1)
                after(k, p, dve, tv_done)
                nc.vector.tensor_tensor(v_b[:].rearrange("p b n -> p (b n)"), ps_v[0:S, :],
                                        bvo["v"][:].rearrange("p b n -> p (b n)"), ALU.add).then_inc(vb_done, 1)
                dve.wait_ge(tu_done, item(k, p) + 1)
                dve.wait_ge(ub_done, item(k, p) + 1)
                after(k, p, dve, g_done, 1, 2)
                nc.vector.scalar_tensor_tensor(su[:, p], th_u[:], 1.0, u_b[:], ALU.add, ALU.mult).then_inc(su_done, 1)
                dve.wait_ge(tv_done, item(k, p) + 1)
                dve.wait_ge(vb_done, item(k, p) + 1)
                after(k, p, dve, r_done, 4, 2)
                nc.vector.scalar_tensor_tensor(v_s[:, p], th_v[:], 1.0, v_b[:], ALU.add, ALU.mult).then_inc(vs_done, 1)

            def mask(b):
                def fn(k, p):
                    for i in range(DC):
                        dve.wait_ge(e_done[i], 2 * item(k, p) + b + 1)
                        if not (isinstance(k, int) and item(k, p) == 0 and b == 0):
                            dve.wait_ge(r_done, 4 * item(k, p) + 2 * b - 2 + i + 1)
                        nc.vector.tensor_tensor(en[:, i], ps_e[i][0:S, 0:4 * S].rearrange("p (j n) -> p j n", j=4),
                                                c["causal_half"][0:S].unsqueeze(1).to_broadcast([S, 4, S]),
                                                ALU.mult).then_inc(em_done[i], 1)
                return fn

            def gate(k, p):
                dve.wait_ge(oT_done, item(k, p) + 1)
                dve.wait_ge(su_done, item(k, p) + 1)
                after(k, p, dve, y_done)
                for i in range(DC):
                    last = nc.vector.scalar_tensor_tensor(gT[:, i], su[:, p, i], half_scale[:, i:i + 1], oT[:, i],
                                                          ALU.mult, ALU.mult)
                last.then_inc(g_done, 1)

            def root(k, p):
                ch.begin()
                if later(k) or p > 0:
                    dve.wait_ge(x2_done[1 - p], k + p)
                dve.wait_ge(ss_done, item(k, p) + 1)
                ch.link(nc.vector.tensor_copy(ss[:], ps_o[0:S, 2 * N2:2 * N2 + 2]))
                rsqrt(nc, ch, rr[:], ss[:], rt[:], rti[:])
                ch.link(nc.vector.tensor_tensor(rr[:], rr[:], ss[:], ALU.mult))
                ch.link(nc.vector.tensor_scalar(rr[:], rr[:], 1.0 / 16, 1e-8, ALU.mult, ALU.add))
                nc.vector.reciprocal(rr[:], rr[:]).then_inc(ssc_done, 1)

            def residual(k, p):
                dve.wait_ge(y_done, item(k, p) + 1)
                dve.wait_ge(ssc_done, item(k, p) + 1)
                dve.wait_ge(xb_done, item(k, p) + 1)
                for b in range(2):
                    x = rows.batch(2 * item(k, p) + b)
                    last = nc.vector.scalar_tensor_tensor(x, ps_v[0:S, b * D:(b + 1) * D], rr[:, b:b + 1],
                                                          x, ALU.mult, ALU.add)
                last.then_inc(x2_done[p], 1)

            pipeline(dve, UN, [(norm, 0), (mask(0), 1), (mask(1), 1), (elu_q, 0), (masked_q, 0), (elu_k, 0), (gate, 1), (root, 1), (residual, 1), (products, 0)])

        @block.tensor
        def _(pe):
            pe.wait_ge(weights, 16 * 13)

            def transposed(k, p):
                pe.wait_ge(xn_done, item(k, p) + 1)
                after(k, p, pe, xnT_done)
                for i in range(DC):
                    for b in range(2):
                        last = nc.tensor.transpose(ps_t[:, i * N2 + b * S:i * N2 + (b + 1) * S],
                                                   xn[:, b, i * P:(i + 1) * P], c["ident"][0:S, 0:S])
                last.then_inc(t_done, 1)

            def project(m, ps, free, done):
                def fn(k, p):
                    pe.wait_ge(xnT_done, item(k, p) + 1)
                    after(k, p, pe, free)
                    for o in range(DC):
                        for i in range(DC):
                            last = nc.tensor.matmul(ps[:, o * N2:(o + 1) * N2], wt[m][:, i, o * P:(o + 1) * P],
                                                    xnT[:, i], start=i == 0, stop=i == DC - 1)
                    last.then_inc(done, 1)
                return fn

            def values(k, p):
                pe.wait_ge(xnT_done, item(k, p) + 1)
                if not (isinstance(k, int) and item(k, p) == 0):
                    pe.wait_ge(x2_done[1 - p], k + p)
                for b in range(2):
                    for i in range(DC):
                        last = nc.tensor.matmul(ps_v[0:S, b * D:(b + 1) * D], xnT[:, i, b * S:(b + 1) * S],
                                                wt["v"][:, i], start=i == 0, stop=i == DC - 1)
                last.then_inc(v_done, 1)

            def energy(b):
                def fn(k, p):
                    pe.wait_ge(eluk_done, item(k, p) + 1)
                    pe.wait_ge(qm_done, item(k, p) + 1)
                    for i in range(DC):
                        if not (isinstance(k, int) and item(k, p) == 0 and b == 0):
                            pe.wait_ge(em_done[i], 2 * item(k, p) + b)
                        nc.tensor.matmul(ps_e[i][0:S, 0:4 * S], kT[:, p, i, b * S:(b + 1) * S],
                                         qm[:, p, i, b].rearrange("p j n -> p (j n)"),
                                         start=True, stop=True).then_inc(e_done[i], 1)
                return fn

            def weighted(b):
                def fn(k, p):
                    pe.wait_ge(vs_done, item(k, p) + 1)
                    after(k, p, pe, oT_done)
                    after(k, p, pe, ssc_done)
                    for i in range(DC):
                        pe.wait_ge(em_done[i], 2 * item(k, p) + b + 1)
                        for j in range(4):
                            last = nc.tensor.matmul(ps_o[32 * j:32 * j + 32, i * N2 + b * S:i * N2 + (b + 1) * S],
                                                    v_s[:, p, b, i * P + 32 * j:i * P + 32 * j + 32], en[:, i, j],
                                                    start=True, stop=True, skip_group_check=True)
                        last.then_inc(r_done, 1)
                return fn

            def output(k, p):
                pe.wait_ge(sq_done, item(k, p) + 1)
                for b in range(2):
                    for i in range(DC):
                        last = nc.tensor.matmul(ps_o[0:S, 2 * N2 + b:2 * N2 + b + 1], sq[:, i, b * S:(b + 1) * S],
                                                c["ones"][:, 0:1], start=i == 0, stop=i == DC - 1,
                                                skip_group_check=True)
                last.then_inc(ss_done, 1)
                pe.wait_ge(g_done, item(k, p) + 1)
                for b in range(2):
                    for i in range(DC):
                        last = nc.tensor.matmul(ps_v[0:S, b * D:(b + 1) * D], gT[:, i, b * S:(b + 1) * S],
                                                wt["o"][:, i], start=i == 0, stop=i == DC - 1)
                last.then_inc(y_done, 1)

            project_q, project_k, project_u = (project("q", ps_q, eluq_done, q_done), project("k", ps_k, eluk_done, k_done),
                                               project("u", ps_u, ub_done, u_done))
            pipeline(pe, UN, [(energy(0), 1), (transposed, 0), (weighted(0), 1), (energy(1), 1), (project_q, 0), (weighted(1), 1),
                              (project_k, 0), (project_u, 0), (output, 1), (values, 0)])

        @block.scalar
        def _(act):
            def copy_t(k, p):
                act.wait_ge(t_done, item(k, p) + 1)
                after(k, p, act, v_done)
                nc.scalar.activation(xnT[:].rearrange("p c n -> p (c n)"), ps_t[:, 0:2 * N2], ACT.Copy).then_inc(xnT_done, 1)

            def exp(e, ps, b, got, done, free):
                def fn(k, p):
                    act.wait_ge(got, item(k, p) + 1)
                    after(k, p, act, free)
                    for i in range(DC):
                        last = nc.scalar.activation(e[:, i], ps[:, i * N2:(i + 1) * N2], ACT.Exp, bias=b[:, i:i + 1])
                    last.then_inc(done, 1)
                return fn

            def gates(k, p):
                act.wait_ge(u_done, item(k, p) + 1)
                after(k, p, act, su_done)
                for i in range(DC):
                    last = nc.scalar.activation(th_u[:, i], ps_u[:, i * N2:(i + 1) * N2], ACT.Tanh,
                                                bias=half_bu[:, i:i + 1], scale=0.5)
                last.then_inc(tu_done, 1)
                for i in range(DC):
                    last = nc.scalar.activation(u_b[:, i], ps_u[:, i * N2:(i + 1) * N2], ACT.Identity, bias=bias["u"][:, i:i + 1])
                last.then_inc(ub_done, 1)
            def values(k, p):
                act.wait_ge(vb_done, item(k, p) + 1)
                after(k, p, act, vs_done)
                nc.scalar.activation(th_v[:], v_b[:], ACT.Tanh, scale=0.5).then_inc(tv_done, 1)

            def squares(k, p):
                act.wait_ge(r_done, 4 * item(k, p) + 4)
                after(k, p, act, g_done)
                nc.scalar.activation(oT[:].rearrange("p c n -> p (c n)"), ps_o[:, 0:2 * N2], ACT.Copy).then_inc(oT_done, 1)
                act.wait_ge(oT_done, item(k, p) + 1)
                after(k, p, act, ss_done)
                nc.scalar.activation(sq[:], oT[:], ACT.Square).then_inc(sq_done, 1)

            act.wait_ge(weights, 16 * 13)
            exp_q = exp(e_q, ps_q, bias["q"], q_done, eq_done, eluq_done)
            exp_k = exp(e_k, ps_k, bias["k"], k_done, ek_done, eluk_done)
            pipeline(act, UN, [(copy_t, 0), (exp_q, 0), (squares, 1), (exp_k, 0), (gates, 0), (values, 0)])


def cross_attention(nc, x_in, ctx, x_out, w, c):
    H, DH = 16, 16
    HC = H // DC
    HS = H * S
    W4 = 4 * S
    with ExitStack() as own:
        sb = lambda n, s, d=FP32: own.enter_context(nc.sbuf_tensor("ca_" + n, s, d))
        sem = own.enter_context(semaphores(nc, "ca_"))
        two = lambda n: [sem(f"{n}{i}") for i in range(2)]
        per_chunk = lambda n: [sem(f"{n}{i}") for i in range(TC)]

        wt = {m: sb("w" + m, [P, DC, D]) for m in "qkvo"}
        bias = {m: sb("b" + m, [P, DC]) for m in "qk"}
        bv = sb("bv", [TN, D])
        bo = sb("bo", [S, D])

        ct = sb("ct", [TN, 2, TC, D])
        xn = sb("xn", [S, D])
        xcT = sb("xcT", [P, DC, T + S])
        kT = sb("kT", [P, 2, DC, T])
        qb = sb("qb", [P, DC, S])
        qm = sb("qm", [P, 2, DC, HC, S])
        vb = sb("vb", [TN, 2, TC, D])
        vm = sb("vm", [TN, TC, H // 2, 64])
        es = sb("es", [TN, TC, HS])
        mx = sb("mx", [TN, TC, H])
        rs = sb("rs", [TN, TC, H])
        aT = sb("aT", [P, DC, S])
        rows = TokenRows(nc, sb, sem)
        bank_a, bank_b, bank_c, bank_d = (own.enter_context(nc.psum_tensor("ca_bank_" + m, [P, 512], FP32)) for m in "abcd")
        ps_s = own.enter_context(nc.psum_tensor("ca_scores", [P, 4, 512], FP32))

        weights = sem("weights_loaded")
        c_ready = two("c_ready")
        vm_zero = sem("vm_zero")
        xn_done, t_done, xcT_done, kq_done, kT_done, qm_done, v_done, vb_done, qb_done = (
            sem(m) for m in ("xn_done", "t_done", "xcT_done", "kq_done", "kT_done", "qm_done", "v_done", "vb_done", "qb_done"))
        s_done, max_done, sub_done = (two(m) for m in ("s_done", "max_done", "sub_done"))
        exp_done, sum_done, vn_done, av_done = (per_chunk(m) for m in ("exp_done", "sum_done", "vn_done", "av_done"))
        aT_done, o_done, xb_done, y_done = (sem(m) for m in ("aT_done", "o_done", "xb_done", "y_done"))
        chain = sem("chain")

        def n(k, p):
            return 2 * k + p

        def after(k, p, eng, s):
            if not (isinstance(k, int) and n(k, p) == 0):
                eng.wait_ge(s, n(k, p))

        block = own.enter_context(nc.Block())

        @block.sync
        def _(sp):
            rows.load(sp, x_in)
            for m in "qkvo":
                sp.dma_start(wt[m][:], w["W" + m].rearrange("(c p) n -> p c n", p=P)).then_inc(weights, 16)
            for m in "qk":
                sp.dma_start(bias[m][:], w["b" + m].rearrange("(c p) -> p c", p=P),
                             allow_slow_non_contiguous=True).then_inc(weights, 16)
            sp.dma_start(bv[:], w["bv"].rearrange("(a n) -> a n", a=1).to_broadcast([TN, D])).then_inc(weights, 16)
            sp.dma_start(bo[:], w["bo"].rearrange("(a n) -> a n", a=1).to_broadcast([S, D])).then_inc(weights, 16)

            def load(k, p):
                if later(k):
                    sp.wait_ge(t_done, n(k, p) - 1)
                sp.dma_start(ct[:, p], ctx[n(k, p)].rearrange("(c t) n -> t c n", c=TC)).then_inc(c_ready[p], 16)



            def store(k, p):
                sp.wait_ge(y_done, n(k, p) + 1)
                sp.dma_start(x_out[n(k, p)], rows.batch(n(k, p))).then_inc(rows.stored, 16)

            pipeline(sp, NB, [(load, 0), (store, 3)])
            sp.wait_ge(rows.stored, 16 * NB)

        @block.vector
        def _(dve):
            ch = Chain(dve, chain)
            rows.stats(dve, ch)

            def norm(k, p):
                after(k, p, dve, t_done)
                rows.normed(n(k, p), xn[:]).then_inc(xn_done, 1)

            def values(k, p):
                dve.wait_ge(v_done, n(k, p) + 1)
                if later(k):
                    dve.wait_ge(vn_done[TC - 1], n(k, p) - 1)
                nc.vector.tensor_tensor(vb[:, p, 0:2], bank_b[0:TN, :].rearrange("t (c n) -> t c n", c=2),
                                        bv[:].unsqueeze(1).to_broadcast([TN, 2, D]), ALU.add)
                nc.vector.tensor_tensor(vb[:, p, 2], bank_c[0:TN, 0:D], bv[:], ALU.add).then_inc(vb_done, 1)

            def shifted(t):
                def fn(k, p):
                    for i in range(DC):
                        scores = ps_s[0:TN, 2 * i:2 * i + 2, 0:W4].rearrange("t b (h n) -> t b h n", h=4)
                        top = mx[:, t, HC * i:HC * (i + 1)].rearrange("t (b h) -> t b h", b=2)
                        dve.wait_ge(s_done[i], TC * n(k, p) + t + 1)
                        nc.vector.tensor_reduce(top, scores, AX.X, ALU.max).then_inc(max_done[i], 1)
                        dve.wait_ge(max_done[i], TC * n(k, p) + t + 1)
                        after(k, p, dve, av_done[t])
                        nc.vector.tensor_tensor(es[:, t, i * HC * S:(i + 1) * HC * S].rearrange("t (b h n) -> t b h n", b=2, h=4),
                                                scores, top.unsqueeze(3).to_broadcast([TN, 2, 4, S]),
                                                ALU.subtract).then_inc(sub_done[i], 1)
                return fn

            def summed(t):
                def fn(k, p):
                    ch.begin()
                    dve.wait_ge(exp_done[t], n(k, p) + 1)
                    after(k, p, dve, vn_done[t])
                    ch.link(nc.vector.tensor_reduce(rs[:, t], es[:, t].rearrange("t (h n) -> t h n", h=H), AX.X, ALU.add))
                    nc.vector.reciprocal(rs[:, t], rs[:, t]).then_inc(sum_done[t], 1)
                return fn

            def residual(k, p):
                dve.wait_ge(o_done, n(k, p) + 1)
                dve.wait_ge(xb_done, n(k, p) + 1)
                nc.vector.tensor_tensor(rows.batch(n(k, p)), bank_d[0:S, D:2 * D], rows.batch(n(k, p)), ALU.add).then_inc(y_done, 1)

            pipeline(dve, NB, [(shifted(0), 2), (summed(2), 3), (shifted(1), 2), (summed(0), 2), (values, 1), (norm, 0),
                               (summed(1), 2), (residual, 3), (shifted(2), 2)])

        @block.tensor
        def _(pe):
            pe.wait_ge(weights, 16 * 8)

            def transposed(k, p):
                pe.wait_ge(c_ready[p], 16 * (k + 1))
                after(k, p, pe, kT_done)
                after(k, p, pe, vb_done)
                for i, bank in enumerate((bank_a, bank_b)):
                    for t in range(TC):
                        nc.tensor.transpose(bank[:, t * TN:(t + 1) * TN], ct[:, p, t, i * P:(i + 1) * P],
                                            c["ident"][0:TN, 0:TN])
                pe.wait_ge(xn_done, n(k, p) + 1)
                for i, bank in enumerate((bank_a, bank_b)):
                    last = nc.tensor.transpose(bank[:, T:T + S], xn[:, i * P:(i + 1) * P], c["ident"][0:S, 0:S])
                last.then_inc(t_done, 1)

            def project(k, p):
                pe.wait_ge(xcT_done, n(k, p) + 1)
                for o, bank in enumerate((bank_c, bank_a)):
                    for m, lo, hi in (("k", 0, T), ("q", T, T + S)):
                        for i in range(DC):
                            last = nc.tensor.matmul(bank[:, lo:hi], wt[m][:, i, o * P:(o + 1) * P], xcT[:, i, lo:hi],
                                                    start=i == 0, stop=i == DC - 1)
                last.then_inc(kq_done, 1)
                for t in range(2):
                    for i in range(DC):
                        nc.tensor.matmul(bank_b[0:TN, t * D:(t + 1) * D], xcT[:, i, t * TN:(t + 1) * TN], wt["v"][:, i],
                                         start=i == 0, stop=i == DC - 1)
                pe.wait_ge(kT_done, n(k, p) + 1)
                pe.wait_ge(qb_done, n(k, p) + 1)
                for i in range(DC):
                    last = nc.tensor.matmul(bank_c[0:TN, 0:D], xcT[:, i, 2 * TN:3 * TN], wt["v"][:, i],
                                            start=i == 0, stop=i == DC - 1)
                last.then_inc(v_done, 1)

            def scores(t):
                def fn(k, p):
                    if t == 0:
                        pe.wait_ge(kT_done, n(k, p) + 1)
                    for i in range(DC):
                        if t == 0:
                            pe.wait_ge(qm_done, DC * n(k, p) + i + 1)
                        if t > 0 or not (isinstance(k, int) and n(k, p) == 0):
                            pe.wait_ge(sub_done[i], TC * n(k, p) + t)
                        for h in range(2):
                            last = nc.tensor.matmul(ps_s[0:TN, 2 * i + h, 0:W4], kT[:, p, i, t * TN:(t + 1) * TN],
                                                    qm[:, p, i, 4 * h:4 * h + 4].rearrange("p h n -> p (h n)"),
                                                    start=True, stop=True)
                        last.then_inc(s_done[i], 1)
                return fn

            def weighted(t):
                def fn(k, p):
                    if t == 0:
                        after(k, p, pe, y_done)
                    pe.wait_ge(vn_done[t], n(k, p) + 1)
                    for i in range(DC):
                        for j in range(4):
                            for e in range(2):
                                m = 4 * i + j
                                last = nc.tensor.matmul(bank_d[32 * j:32 * j + 32, i * S:(i + 1) * S],
                                                        vm[:, t, m, 32 * e:32 * e + 32],
                                                        es[:, t, (2 * m + e) * S:(2 * m + e + 1) * S],
                                                        start=t == 0 and i == 0 and e == 0, stop=t == TC - 1 and e == 1,
                                                        skip_group_check=True)
                    last.then_inc(av_done[t], 1)
                return fn

            def output(k, p):
                pe.wait_ge(aT_done, n(k, p) + 1)
                for i in range(DC):
                    last = nc.tensor.matmul(bank_d[0:S, D:2 * D], aT[:, i], wt["o"][:, i], start=i == 0, stop=i == DC - 1)
                last.then_inc(o_done, 1)

            pipeline(pe, NB, [(scores(0), 2), (transposed, 1), (weighted(1), 3), (scores(1), 2), (project, 1),
                              (weighted(2), 3), (output, 3), (scores(2), 2), (weighted(0), 2)])

        @block.scalar
        def _(act):
            act.wait_ge(weights, 16 * 8)

            def exps(t):
                def fn(k, p):
                    for i in range(DC):
                        half = es[:, t, i * HC * S:(i + 1) * HC * S]
                        act.wait_ge(sub_done[i], TC * n(k, p) + t + 1)
                        last = nc.scalar.activation(half, half, ACT.Exp, scale=DH ** -0.5)
                    last.then_inc(exp_done[t], 1)
                return fn

            def copy_a(k, p):
                act.wait_ge(av_done[TC - 1], n(k, p) + 1)
                after(k, p, act, o_done)
                nc.scalar.activation(aT[:].rearrange("p c n -> p (c n)"), bank_d[:, 0:DC * S], ACT.Copy).then_inc(aT_done, 1)

            def copy_t(k, p):
                act.wait_ge(t_done, n(k, p) + 1)
                after(k, p, act, v_done)
                for i, bank in enumerate((bank_a, bank_b)):
                    last = nc.scalar.activation(xcT[:, i], bank[:, 0:T + S], ACT.Copy)
                last.then_inc(xcT_done, 1)

            def copy_kq(k, p):
                act.wait_ge(kq_done, n(k, p) + 1)
                if not (isinstance(k, int) and n(k, p) == 0):
                    act.wait_ge(qm_done, DC * n(k, p))
                for o, bank in enumerate((bank_c, bank_a)):
                    last = nc.scalar.activation(qb[:, o], bank[:, T:T + S], ACT.Identity, bias=bias["q"][:, o:o + 1])
                last.then_inc(qb_done, 1)
                if later(k):
                    act.wait_ge(s_done[1], TC * (n(k, p) - 1))
                for o, bank in enumerate((bank_c, bank_a)):
                    last = nc.scalar.activation(kT[:, p, o], bank[:, 0:T], ACT.Identity, bias=bias["k"][:, o:o + 1])
                last.then_inc(kT_done, 1)

            pipeline(act, NB, [(exps(0), 2), (copy_t, 1), (copy_kq, 1), (exps(1), 2), (copy_a, 3), (exps(2), 2)])

        @block.gpsimd
        def _(g):
            nc.gpsimd.memset(vm[:], 0.0).then_inc(vm_zero, 1)
            g.wait_ge(vm_zero, 1)
            g.wait_ge(weights, 16 * 8)

            def mask_q(k, p):
                g.wait_ge(qb_done, n(k, p) + 1)
                if later(k):
                    g.wait_ge(s_done[1], TC * (n(k, p) - 1))
                for i in range(DC):
                    nc.gpsimd.tensor_tensor(qm[:, p, i], qb[:, i].unsqueeze(1).to_broadcast([P, HC, S]),
                                            c["head16"][:].unsqueeze(2).to_broadcast([P, HC, S]),
                                            ALU.mult).then_inc(qm_done, 1)

            def biased(k, p):
                g.wait_ge(xn_done, n(k, p) + 1)
                nc.gpsimd.tensor_tensor(rows.batch(n(k, p)), rows.batch(n(k, p)), bo[:], ALU.add).then_inc(xb_done, 1)

            def normalized(t):
                def fn(k, p):
                    g.wait_ge(sum_done[t], n(k, p) + 1)
                    g.wait_ge(vb_done, n(k, p) + 1)
                    after(k, p, g, av_done[t])
                    for e in range(2):
                        pair = lambda a: a.rearrange("t (m e n) -> t m e n", e=2, n=DH)[:, :, e]
                        last = nc.gpsimd.tensor_tensor(
                            vm[:, t, :, 48 * e:48 * e + DH], pair(vb[:, p, t]),
                            rs[:, t].rearrange("t (m e) -> t m e", e=2)[:, :, e].unsqueeze(2).to_broadcast([TN, H // 2, DH]),
                            ALU.mult)
                    last.then_inc(vn_done[t], 1)
                return fn

            pipeline(g, NB, [(normalized(2), 3), (normalized(0), 2), (mask_q, 1), (biased, 2), (normalized(1), 2)])


def moe_attention(nc, x_in, base, xf, logits, w, c):
    G, DH = 8, 16
    with ExitStack() as own:
        sb = lambda n, s, d=FP32: own.enter_context(nc.sbuf_tensor("ma_" + n, s, d))
        pb = lambda n, s: own.enter_context(nc.psum_tensor("ma_ps_" + n, s, FP32))
        sem = own.enter_context(semaphores(nc, "ma_"))
        two = lambda n: [sem(f"{n}{i}") for i in range(2)]

        wqkv = sb("wqkv", [P, DC, 4, P])
        wp = sb("wp", [P, DC, D])
        wr = sb("wr", [P, DC, NE])
        aff = {m: sb(m, [P, DC]) for m in ("ln1_weight", "ln1_bias", "ln2_weight", "ln2_bias")}
        x = sb("x", [P, NT, D])
        hid = sb("hid", [P, 4, D])
        xn = sb("xn", [P, D])
        lnT = sb("lnT", [P, DC, P])
        qT = sb("qT", [P, 2, 2, P])
        kb = sb("kb", [P, P])
        km = sb("km", [P, 2, G, P])
        vz = sb("vz", [P, 4, G, 3 * DH])
        es = sb("es", [P, 2, G, P])
        en = sb("en", [P, 2, G, P])
        mx = sb("mx", [P, 2, G])
        rs = sb("rs", [P, 2, G])
        pt = sb("pt", [P, 2, G, P])
        aT = sb("aT", [P, DC, P])
        ha = sb("ha", [P, D])

        xo = sb("xo", [P, 2, D])
        xoT = sb("xoT", [P, DC, P])
        lg = sb("lg", [P, 2, NE])
        n1 = Norm(nc, sb, "n1", P, NT, 1e-5)
        n3 = Norm(nc, sb, "n3", P, 1, 1e-5)
        v2 = sb("v2", [P, NT])
        rs2 = sb("rs2", [P, NT])
        ps_t = pb("t", [P, 512])
        ps_l = pb("l", [P, 512])
        ps_qkv = pb("qkv", [P, 512])
        ps_s = [pb(f"s{r}", [P, 2, 512]) for r in range(2)]
        ps_o = pb("o", [P, 512])

        weights = sem("weights_loaded")
        x_loaded = [sem(f"x_loaded{i}") for i in range(7)]
        f_stored, l_stored, b_stored = two("f_stored"), two("l_stored"), sem("b_stored")
        s_done, max_done, sub_done, exp_done, sum_done, pn_done, p_done, pt_done = (
            two(m) for m in ("s_done", "max_done", "sub_done", "exp_done", "sum_done", "pn_done", "p_done", "pt_done"))
        hid_done, vz_zero, xn_done, t_done, lnT_done, qkv_done, q_done, kb_done, km_done, vz_done = (
            sem(m) for m in ("hid_done", "vz_zero", "xn_done", "t_done", "lnT_done", "qkv_done", "q_done", "kb_done", "km_done", "vz_done"))
        av_done, aT_done, proj_done, ha_done, bs_done, xo_done, t2_done, xoT_done, r_done, lg_done = (
            sem(m) for m in ("av_done", "aT_done", "proj_done", "ha_done", "bs_done", "xo_done", "t2_done", "xoT_done", "r_done", "lg_done"))
        chain = sem("chain")
        chain2 = sem("chain2")
        tiles = lambda a: a.rearrange("(p t) n -> t p n", t=NT)
        NW = 16 * 7

        def n(k, p):
            return 4 * k + p

        def turn(k, p):
            return 2 * k + p // 2

        def after(k, p, eng, s, back=1):
            if not (isinstance(k, int) and n(k, p) < back):
                eng.wait_ge(s, n(k, p) - back + 1)

        def slot_free(k, p, eng, s):
            if not (isinstance(k, int) and n(k, p) < 2):
                eng.wait_ge(s[p % 2], 16 * turn(k, p))

        def tile(k, p):
            i = n(k, p)
            return x[:, i] if isinstance(i, int) else x[:, bass.ds(i, 1)].rearrange("p a n -> p (a n)")

        block = own.enter_context(nc.Block())

        @block.sync
        def _(sp):
            for i in range(7):
                sp.dma_start(x[:, 4 * i:4 * i + 4], x_in.rearrange("(p t) n -> p t n", t=NT)[:, 4 * i:4 * i + 4]).then_inc(x_loaded[i], 16)
            sp.dma_start(wqkv[:], w["qkv_weight"].rearrange("(c p) (f n) -> p c f n", p=P, f=4)).then_inc(weights, 16)
            sp.dma_start(wp[:], w["proj_weight"].rearrange("(c p) n -> p c n", p=P)).then_inc(weights, 16)
            sp.dma_start(wr[:], w["router_weight"].rearrange("(c p) n -> p c n", p=P)).then_inc(weights, 16)
            for m in aff:
                sp.dma_start(aff[m][:], w[m].rearrange("(c p) -> p c", p=P), allow_slow_non_contiguous=True).then_inc(weights, 16)

            def store_b(k, p):
                sp.wait_ge(ha_done, n(k, p) + 1)
                sp.dma_start(tiles(base)[n(k, p)], tile(k, p)).then_inc(b_stored, 16)

            def store_f(k, p):
                sp.wait_ge(xo_done, n(k, p) + 1)
                sp.dma_start(tiles(xf)[n(k, p)], xo[:, p % 2]).then_inc(f_stored[p % 2], 16)
                sp.wait_ge(lg_done, n(k, p) + 1)
                sp.dma_start(tiles(logits)[n(k, p)], lg[:, p % 2]).then_inc(l_stored[p % 2], 16)

            pipeline(sp, NT, [(store_b, 4), (store_f, 5)], 4)
            sp.wait_ge(b_stored, 16 * NT)
            for s in (*f_stored, *l_stored):
                sp.wait_ge(s, 16 * (NT // 2))

        @block.vector
        def _(dve):
            ch, ch2 = Chain(dve, chain), Chain(dve, chain2)

            def loaded_tile(t):
                if t % 4 == 0:
                    dve.wait_ge(x_loaded[t // 4], 16)
                return x[:, t]

            n1.stats(ch, loaded_tile)
            ch.link(nc.vector.tensor_tensor(v2[:], n1.rs[:], n1.rs[:], ALU.mult))
            ch.link(nc.vector.tensor_tensor(v2[:], v2[:], n1.mv[:, :, 1], ALU.mult))
            ch.link(nc.vector.tensor_scalar(v2[:], v2[:], 1e-5, None, ALU.add))
            rsqrt(nc, ch, rs2[:], v2[:], n1.t[:], n1.ti[:])

            def norms(k, p):
                i = n(k, p)
                col = lambda t: t[:, i:i + 1] if isinstance(i, int) else t[:, bass.ds(i, 1)]
                mean = n1.mv[:, i, 0:1] if isinstance(i, int) else n1.mv[:, bass.ds(i, 1), 0]
                after(k, p, dve, ha_done, 4)
                after(k, p, dve, bs_done, 4)
                nc.vector.tensor_scalar(hid[:, p], tile(k, p), mean, col(n1.rs), ALU.subtract, ALU.mult).then_inc(hid_done, 1)
                after(k, p, dve, t_done)
                dve.wait_ge(hid_done, n(k, p) + 1)
                nc.vector.tensor_scalar(xn[:], hid[:, p], col(rs2), None, ALU.mult).then_inc(xn_done, 1)

            def shifted(r):
                def fn(k, p):
                    scores = ps_s[r][:].rearrange("q b (h n) -> q (b h) n", h=4)
                    dve.wait_ge(s_done[r], n(k, p) + 1)
                    nc.vector.tensor_reduce(mx[:, r], scores, AX.X, ALU.max).then_inc(max_done[r], 1)
                    dve.wait_ge(max_done[r], n(k, p) + 1)
                    after(k, p, dve, pn_done[r])
                    nc.vector.tensor_tensor(es[:, r], scores, mx[:, r].unsqueeze(2).to_broadcast([P, G, P]),
                                            ALU.subtract).then_inc(sub_done[r], 1)
                return fn

            def summed(r):
                def fn(k, p):
                    ch2.begin()
                    dve.wait_ge(exp_done[r], n(k, p) + 1)
                    after(k, p, dve, pn_done[r])
                    ch2.link(nc.vector.tensor_reduce(rs[:, r], es[:, r], AX.X, ALU.add))
                    nc.vector.reciprocal(rs[:, r], rs[:, r]).then_inc(sum_done[r], 1)
                return fn

            def residual(k, p):
                ch.begin()
                dve.wait_ge(proj_done, n(k, p) + 1)
                dve.wait_ge(bs_done, n(k, p) + 1)
                after(k, p, dve, xo_done)
                ch.link(nc.vector.tensor_tensor(ha[:], hid[:, p], ps_o[:, D:2 * D], ALU.add))
                nc.vector.tensor_tensor(tile(k, p), tile(k, p), ps_o[:, D:2 * D], ALU.add).then_inc(ha_done, 1)
                n3.stats(ch, lambda r: ha[:])
                after(k, p, dve, t2_done, 2)
                slot_free(k, p, dve, f_stored)
                n3.apply(0, xo[:, p % 2], ha[:]).then_inc(xo_done, 1)

            pipeline(dve, NT, [(shifted(0), 1), (norms, 0), (shifted(1), 1), (summed(0), 1), (summed(1), 1), (residual, 3)], 4)

        @block.tensor
        def _(pe):
            pe.wait_ge(weights, NW)

            def transposed(k, p):
                pe.wait_ge(xn_done, n(k, p) + 1)
                after(k, p, pe, lnT_done)
                for i in range(DC):
                    last = nc.tensor.transpose(ps_t[:, i * P:(i + 1) * P], xn[:, i * P:(i + 1) * P], c["ident"][:])
                last.then_inc(t_done, 1)

            def project(k, p):
                pe.wait_ge(lnT_done, n(k, p) + 1)
                after(k, p, pe, q_done)
                after(k, p, pe, vz_done)
                for f in range(3):
                    for i in range(DC):
                        nc.tensor.matmul(ps_qkv[:, f * P:(f + 1) * P], wqkv[:, i, f], lnT[:, i], start=i == 0, stop=i == DC - 1)
                for i in range(DC):
                    last = nc.tensor.matmul(ps_qkv[:, 3 * P:4 * P], lnT[:, i], wqkv[:, i, 3], start=i == 0, stop=i == DC - 1)
                last.then_inc(qkv_done, 1)

            def scores(r):
                def fn(k, p):
                    pe.wait_ge(km_done, n(k, p) + 1)
                    pe.wait_ge(q_done, n(k, p) + 1)
                    after(k, p, pe, sub_done[r])
                    after(k, p, pe, pt_done[r], 2)
                    for b in range(2):
                        nc.tensor.matmul(ps_s[r][:, b], qT[:, p % 2, r], km[:, p % 2, 4 * b:4 * b + 4].rearrange("p g n -> p (g n)"),
                                         start=True, stop=False)
                        last = nc.tensor.matmul(ps_s[r][:, b], c["ident_bf"][:],
                                                c["hidden_bf"][:].unsqueeze(1).to_broadcast([P, 4, P]), start=False, stop=True)
                    last.then_inc(s_done[r], 1)
                return fn

            def probs(r):
                def fn(k, p):
                    pe.wait_ge(pn_done[r], n(k, p) + 1)
                    if not (isinstance(k, int) and n(k, p) == NT - 1):
                        pe.wait_ge(sub_done[r], n(k, p) + 2)
                    for g in range(G):
                        last = nc.tensor.transpose(ps_s[r][:, g // 4, (g % 4) * P:(g % 4 + 1) * P], en[:, r, g], c["ident"][:])
                    last.then_inc(p_done[r], 1)
                return fn

            def weighted(k, p):
                pe.wait_ge(pt_done[0], n(k, p) + 1)
                pe.wait_ge(pt_done[1], n(k, p) + 1)
                after(k, p, pe, aT_done)
                after(k, p, pe, ha_done)
                for g in range(G):
                    for r in range(2):
                        j = g % 4
                        last = nc.tensor.matmul(ps_o[32 * j:32 * j + 32, g // 4 * P:(g // 4 + 1) * P],
                                                vz[:, p, g, DH * (1 - r):DH * (1 - r) + 32], pt[:, r, g],
                                                start=r == 0, stop=r == 1, skip_group_check=True)
                last.then_inc(av_done, 1)

            def output(k, p):
                pe.wait_ge(aT_done, n(k, p) + 1)
                after(k, p, pe, ha_done)
                for i in range(DC):
                    last = nc.tensor.matmul(ps_o[:, D:2 * D], aT[:, i], wp[:, i], start=i == 0, stop=i == DC - 1)
                last.then_inc(proj_done, 1)

            def route(k, p):
                pe.wait_ge(xo_done, n(k, p) + 1)
                after(k, p, pe, lg_done)
                for i in range(DC):
                    last = nc.tensor.transpose(ps_l[:, i * P:(i + 1) * P], xo[:, p % 2, i * P:(i + 1) * P], c["ident"][:])
                last.then_inc(t2_done, 1)
                pe.wait_ge(xoT_done, n(k, p) + 1)
                for i in range(DC):
                    last = nc.tensor.matmul(ps_l[:, D:D + NE], xoT[:, i], wr[:, i], start=i == 0, stop=i == DC - 1)
                last.then_inc(r_done, 1)

            pipeline(pe, NT, [(scores(0), 1), (scores(1), 1), (transposed, 0), (weighted, 3), (project, 0), (output, 3),
                              (probs(0), 2), (probs(1), 2), (route, 4)], 4)

        @block.scalar
        def _(act):
            act.wait_ge(weights, NW)

            def copy_t(k, p):
                act.wait_ge(t_done, n(k, p) + 1)
                after(k, p, act, qkv_done)
                for i in range(DC):
                    last = nc.scalar.activation(lnT[:, i], ps_t[:, i * P:(i + 1) * P], ACT.Identity,
                                                bias=aff["ln1_bias"][:, i:i + 1], scale=aff["ln1_weight"][:, i:i + 1])
                last.then_inc(lnT_done, 1)

            def copy_qkv(k, p):
                act.wait_ge(qkv_done, n(k, p) + 1)
                after(k, p, act, km_done)
                nc.scalar.activation(kb[:], ps_qkv[:, 2 * P:3 * P], ACT.Copy).then_inc(kb_done, 1)
                after(k, p, act, s_done[1], 2)
                nc.scalar.activation(qT[:, p % 2].rearrange("p r n -> p (r n)"), ps_qkv[:, 0:2 * P], ACT.Copy).then_inc(q_done, 1)
                after(k, p, act, av_done, 4)
                nc.scalar.activation(vz[:, p, :, DH:2 * DH], ps_qkv[:, 3 * P:4 * P].rearrange("p (g n) -> p g n", g=G),
                                     ACT.Copy).then_inc(vz_done, 1)

            def exps(r):
                def fn(k, p):
                    act.wait_ge(sub_done[r], n(k, p) + 1)
                    nc.scalar.activation(es[:, r], es[:, r], ACT.Exp, scale=DH ** -0.5).then_inc(exp_done[r], 1)
                return fn

            def copy_p(r):
                def fn(k, p):
                    act.wait_ge(p_done[r], n(k, p) + 1)
                    after(k, p, act, av_done)
                    nc.scalar.activation(pt[:, r].rearrange("q (b h) n -> q b (h n)", b=2), ps_s[r][:], ACT.Copy).then_inc(pt_done[r], 1)
                return fn

            def copy_a(k, p):
                act.wait_ge(av_done, n(k, p) + 1)
                after(k, p, act, proj_done)
                nc.scalar.activation(aT[:].rearrange("p c n -> p (c n)"), ps_o[:, 0:D], ACT.Copy).then_inc(aT_done, 1)

            def copy_x(k, p):
                act.wait_ge(t2_done, n(k, p) + 1)
                after(k, p, act, r_done)
                for i in range(DC):
                    last = nc.scalar.activation(xoT[:, i], ps_l[:, i * P:(i + 1) * P], ACT.Identity,
                                                bias=aff["ln2_bias"][:, i:i + 1], scale=aff["ln2_weight"][:, i:i + 1])
                last.then_inc(xoT_done, 1)
                act.wait_ge(r_done, n(k, p) + 1)
                slot_free(k, p, act, l_stored)
                nc.scalar.activation(lg[:, p % 2], ps_l[:, D:D + NE], ACT.Copy).then_inc(lg_done, 1)

            act.wait_ge(vz_zero, 1)
            pipeline(act, NT, [(copy_t, 0), (exps(0), 1), (copy_a, 3), (copy_qkv, 0), (exps(1), 1), (copy_p(0), 2),
                               (copy_p(1), 2), (copy_x, 4)], 4)

        @block.gpsimd
        def _(g):
            nc.gpsimd.memset(vz[:], 0.0).then_inc(vz_zero, 1)

            def mask_k(k, p):
                g.wait_ge(kb_done, n(k, p) + 1)
                after(k, p, g, s_done[1], 2)
                nc.gpsimd.tensor_tensor(km[:, p % 2], kb[:].unsqueeze(1).to_broadcast([P, G, P]),
                                        c["head16"][:].unsqueeze(2).to_broadcast([P, G, P]), ALU.mult).then_inc(km_done, 1)

            def base_x(k, p):
                g.wait_ge(hid_done, n(k, p) + 1)
                nc.gpsimd.tensor_tensor(tile(k, p), tile(k, p), hid[:, p], ALU.add).then_inc(bs_done, 1)

            def normalized(r):
                def fn(k, p):
                    g.wait_ge(sum_done[r], n(k, p) + 1)
                    after(k, p, g, p_done[r])
                    nc.gpsimd.tensor_tensor(en[:, r], es[:, r], rs[:, r].unsqueeze(2).to_broadcast([P, G, P]),
                                            ALU.mult).then_inc(pn_done[r], 1)
                return fn

            pipeline(g, NT, [(mask_k, 0), (base_x, 0), (normalized(0), 1), (normalized(1), 1)], 4)


def routing(nc, logits, slots, gates, zeros, xin, yout, c):
    with ExitStack() as own:
        sb = lambda n, s, d=FP32: own.enter_context(nc.sbuf_tensor("ro_" + n, s, d))
        sem = own.enter_context(semaphores(nc, "ro_"))
        lg, ex, one1, one2, a, sel, w, cum, z = (sb(m, [P, NT, NE]) for m in ("lg", "ex", "one1", "one2", "a", "sel", "w", "cum", "z"))
        m1, m2, k1, k2, den = (sb(m, [P, NT]) for m in ("m1", "m2", "k1", "k2", "den"))
        ones = sb("ones", [P, NT])
        sf = sb("sf", [P, 2, NT])
        offs = own.enter_context(nc.psum_tensor("ro_offs", [P, NE], FP32))
        loaded, ready, exp_done, tot_done, offs_done, cleared, chain, z_made, done = (
            sem(m) for m in ("loaded", "shifted_ready", "exp_done", "tot_done", "offs_done", "cleared", "chain", "z_made", "done"))
        block = own.enter_context(nc.Block())
        wide = zeros.shape[1]
        parts = ROWS * D // (P * wide)
        assert parts * P * wide == ROWS * D

        @block.sync
        def _(sp):
            sp.dma_start(lg[:].rearrange("p t e -> p (t e)"), logits.rearrange("(p t) e -> p (t e)", t=NT)).then_inc(loaded, 16)
            sp.wait_ge(z_made, 1)
            flat = xin.rearrange("(a p r) n -> a p (r n)", p=P, a=parts)
            for i in range(parts):
                sp.dma_start(flat[i], zeros[:]).then_inc(cleared, 16)
            sp.dma_start(yout[ROWS:ROWS + 1], zeros[0:1, 0:D]).then_inc(cleared, 16)
            sp.wait_ge(cleared, 16 * (parts + 1))

        @block.gpsimd
        def _(g):
            nc.gpsimd.memset(zeros[:], 0.0).then_inc(z_made, 1)

        @block.tensor
        def _(pe):
            pe.wait_ge(tot_done, 1)
            nc.tensor.matmul(offs[:], c["before"][:], cum[:, NT - 1], start=True, stop=True).then_inc(offs_done, 1)

        @block.scalar
        def _(act):
            act.wait_ge(ready, 1)
            nc.scalar.activation(ex[:], lg[:], ACT.Exp).then_inc(exp_done, 1)

        @block.vector
        def _(dve):
            ch = Chain(dve, chain)
            V = nc.vector
            over = lambda t: t[:].unsqueeze(2).to_broadcast([P, NT, NE])
            each = lambda t: t[:].unsqueeze(1).to_broadcast([P, NT, NE])
            dve.wait_ge(loaded, 16)
            ch.link(V.memset(ones[:], 1.0))
            ch.link(V.tensor_reduce(m1[:], lg[:], AX.X, ALU.max))
            V.tensor_tensor(lg[:], lg[:], over(m1), ALU.subtract).then_inc(ready, 1)
            dve.wait_ge(ready, 1)
            ch.link(V.scalar_tensor_tensor(a[:], lg[:], 0.0, each(c["first"]), ALU.is_equal, ALU.mult))
            ch.link(V.tensor_reduce(k1[:], a[:], AX.X, ALU.max))
            ch.link(V.tensor_tensor(one1[:], each(c["first"]), over(k1), ALU.is_equal))
            ch.link(V.scalar_tensor_tensor(z[:], one1[:], -3e38, lg[:], ALU.mult, ALU.add))
            ch.link(V.tensor_reduce(m2[:], z[:], AX.X, ALU.max))
            ch.link(V.tensor_tensor(a[:], z[:], over(m2), ALU.is_equal))
            ch.link(V.tensor_tensor(a[:], a[:], each(c["first"]), ALU.mult))
            ch.link(V.tensor_reduce(k2[:], a[:], AX.X, ALU.max))
            ch.link(V.tensor_tensor(one2[:], each(c["first"]), over(k2), ALU.is_equal))
            ch.link(V.tensor_tensor(sel[:], one1[:], one2[:], ALU.add))
            for e in range(NE):
                last = V.tensor_tensor_scan(cum[:, :, e], ones[:], sel[:, :, e], 0.0, ALU.mult, ALU.add)
            last.then_inc(tot_done, 1)
            dve.wait_ge(exp_done, 1)
            ch.link(V.tensor_tensor(w[:], ex[:], sel[:], ALU.mult))
            ch.link(V.tensor_reduce(den[:], w[:], AX.X, ALU.add))
            ch.link(V.reciprocal(den[:], den[:]))
            ch.link(V.tensor_tensor(w[:], w[:], over(den), ALU.mult))
            dve.wait_ge(tot_done, 1)
            dve.wait_ge(offs_done, 1)
            ch.link(V.tensor_tensor(cum[:], cum[:], sel[:], ALU.subtract))
            ch.link(V.tensor_copy(m1[:, 0:NE], offs[:]))
            ch.link(V.tensor_tensor(cum[:], cum[:], m1[:, 0:NE].unsqueeze(1).to_broadcast([P, NT, NE]), ALU.add))
            ch.link(V.tensor_scalar(a[:], cum[:], float(CAP), None, ALU.is_lt))
            ch.link(V.tensor_tensor(w[:], w[:], a[:], ALU.mult))
            ch.link(V.tensor_tensor(cum[:], cum[:], each(c["expert_row"]), ALU.add))
            ch.link(V.tensor_tensor(cum[:], cum[:], a[:], ALU.mult))
            for j, one in enumerate((one1, one2)):
                ch.link(V.tensor_tensor(z[:], cum[:], one[:], ALU.mult))
                ch.link(V.tensor_reduce(sf[:, j], z[:], AX.X, ALU.add))
                ch.link(V.tensor_tensor(z[:], w[:], one[:], ALU.mult))
                ch.link(V.tensor_reduce(gates[:, j], z[:], AX.X, ALU.add))
            V.tensor_scalar(slots[:], sf[:], float(ROWS), None, ALU.add).then_inc(done, 1)


def dispatch(nc, xf, slots, xin):
    with ExitStack() as own:
        rows = own.enter_context(nc.sbuf_tensor("di_rows", [P, NT, D], FP32))
        sem = own.enter_context(semaphores(nc, "di_"))
        loaded, sent = sem("loaded"), sem("sent")
        block = own.enter_context(nc.Block())

        @block.sync
        def _(sp):
            sp.dma_start(rows[:], xf.rearrange("(p t) n -> p t n", t=NT)).then_inc(loaded, 16)

        @block.gpsimd
        def _(g):
            g.wait_ge(loaded, 16)
            for t in range(NT):
                for j in range(2):
                    nc.gpsimd.indirect_dma_start(
                        out=xin[0:ROWS], out_offset=bass.IndirectOffsetOnAxis(ap=slots[:, j, t:t + 1], axis=0),
                        in_=rows[:, t], in_offset=None, bounds_check=ROWS - 1, oob_is_err=False).then_inc(sent, 16)
            g.wait_ge(sent, 16 * 2 * NT)


def experts(nc, xin, yout, w1, w2, ln_w, ln_b, c):
    R2 = 2 * S
    PER = CAP // R2
    FC = F // P
    UN = NE * PER
    with ExitStack() as own:
        sb = lambda n, s, d=FP32: own.enter_context(nc.sbuf_tensor("ex_" + n, s, d))
        pb = lambda n: own.enter_context(nc.psum_tensor("ex_ps_" + n, [P, 512], FP32))
        sem = own.enter_context(semaphores(nc, "ex_"))
        two = lambda n: [sem(f"{n}{i}") for i in range(2)]
        w1s = sb("w1", [P, 2, DC, F])
        w2s = sb("w2", [P, 2, FC, D])
        aff = [sb(m, [P, DC]) for m in ("weight", "bias")]
        xr = sb("xr", [S, 2, 2, D])
        xT = sb("xT", [P, 2, DC, R2])
        hT = sb("hT", [P, 2, FC, R2])
        y = sb("y", [S, 2, 2, D])
        ps_t = pb("t")
        ps_h = [pb(f"h{i}") for i in range(4)]
        ps_y = [pb(f"y{i}") for i in range(2)]
        affine, w_ready = sem("affine"), two("w_ready")
        x_ready, y_stored = two("x_ready"), two("y_stored")
        t_done, xT_done, m2_done, y_done = sem("t_done"), sem("xT_done"), sem("m2_done"), sem("y_done")
        h_done = [sem(f"h_done{i}") for i in range(4)]
        g_done = [sem(f"g_done{i}") for i in range(4)]
        U = 2 * PER
        rows = lambda a: a[0:ROWS].rearrange("(u b s) n -> u s b n", b=2, s=S)

        def n(k, p):
            return U * k + p

        def turn(k, p):
            return PER * k + p // 2

        def after(k, p, eng, s, back=1):
            if not (isinstance(k, int) and n(k, p) < back):
                eng.wait_ge(s, n(k, p) - back + 1)

        block = own.enter_context(nc.Block())

        @block.sync
        def _(sp):
            for t, a in zip(aff, (ln_w, ln_b)):
                sp.dma_start(t[:], a.rearrange("(c p) -> p c", p=P), allow_slow_non_contiguous=True).then_inc(affine, 16)

            def load(k, p):
                if p % PER == 0:
                    q = p // PER
                    if later(k):
                        sp.wait_ge(m2_done, n(k, p) - PER)
                    sp.dma_start(w1s[:, q], w1[2 * k + q].rearrange("(c p) f -> p c f", p=P)).then_inc(w_ready[q], 16)
                    sp.dma_start(w2s[:, q], w2[2 * k + q].rearrange("(c p) n -> p c n", p=P)).then_inc(w_ready[q], 16)
                after(k, p, sp, t_done, 2)
                sp.dma_start(xr[:, p % 2], rows(xin)[n(k, p)]).then_inc(x_ready[p % 2], 16)

            def store(k, p):
                sp.wait_ge(y_done, n(k, p) + 1)
                sp.dma_start(rows(yout)[n(k, p)], y[:, p % 2]).then_inc(y_stored[p % 2], 16)

            pipeline(sp, UN, [(store, 3), (load, 0)], U)
            for s in y_stored:
                sp.wait_ge(s, 16 * (UN // 2))

        @block.tensor
        def _(pe):
            def transposed(k, p):
                pe.wait_ge(x_ready[p % 2], 16 * (turn(k, p) + 1))
                after(k, p, pe, xT_done)
                for i in range(DC):
                    for b in range(2):
                        last = nc.tensor.transpose(ps_t[:, i * R2 + b * S:i * R2 + (b + 1) * S],
                                                   xr[:, p % 2, b, i * P:(i + 1) * P], c["ident"][0:S, 0:S])
                last.then_inc(t_done, 1)

            def up(k, p):
                pe.wait_ge(xT_done, n(k, p) + 1)
                if p % PER == 0:
                    pe.wait_ge(w_ready[p // PER], 32 * (k + 1))
                for h in range(4):
                    after(k, p, pe, g_done[h])
                    for j in range(2):
                        f = 2 * h + j
                        for i in range(DC):
                            last = nc.tensor.matmul(ps_h[h][:, j * R2:(j + 1) * R2], w1s[:, p // PER, i, f * P:(f + 1) * P],
                                                    xT[:, p % 2, i], start=i == 0, stop=i == DC - 1)
                    last.then_inc(h_done[h], 1)

            def down(k, p):
                after(k, p, pe, y_done, 2)
                for b in range(2):
                    for f in range(FC):
                        if b == 0 and f % 2 == 0:
                            pe.wait_ge(g_done[f // 2], n(k, p) + 1)
                        last = nc.tensor.matmul(ps_y[p % 2][0:S, b * D:(b + 1) * D], hT[:, p % 2, f, b * S:(b + 1) * S],
                                                w2s[:, p // PER, f], start=f == 0, stop=f == FC - 1)
                last.then_inc(m2_done, 1)

            pipeline(pe, UN, [(transposed, 0), (up, 0), (down, 1)], U)

        @block.scalar
        def _(act):
            act.wait_ge(affine, 32)

            def copy_t(k, p):
                act.wait_ge(t_done, n(k, p) + 1)
                after(k, p, act, h_done[3], 2)
                for i in range(DC):
                    last = nc.scalar.activation(xT[:, p % 2, i], ps_t[:, i * R2:(i + 1) * R2], ACT.Identity,
                                                bias=aff[1][:, i:i + 1], scale=aff[0][:, i:i + 1])
                last.then_inc(xT_done, 1)

            def gelus(k, p):
                after(k, p, act, m2_done, 2)
                for h in range(4):
                    act.wait_ge(h_done[h], n(k, p) + 1)
                    nc.scalar.activation(hT[:, p % 2, 2 * h:2 * h + 2].rearrange("p f n -> p (f n)"), ps_h[h][:, 0:2 * R2],
                                         ACT.Gelu).then_inc(g_done[h], 1)

            pipeline(act, UN, [(copy_t, 0), (gelus, 0)], U)

        @block.vector
        def _(dve):
            def copy_y(k, p):
                dve.wait_ge(m2_done, n(k, p) + 1)
                if not (isinstance(k, int) and n(k, p) < 2):
                    dve.wait_ge(y_stored[p % 2], 16 * turn(k, p))
                nc.vector.tensor_copy(y[:, p % 2].rearrange("s b n -> s (b n)"), ps_y[p % 2][0:S, :]).then_inc(y_done, 1)

            pipeline(dve, UN, [(copy_y, 1)], U)


def combine(nc, base, slots, gates, yout, x_out):
    with ExitStack() as own:
        rows = own.enter_context(nc.sbuf_tensor("co_rows", [P, 2, NT, D], FP32))
        acc = own.enter_context(nc.sbuf_tensor("co_acc", [P, NT, D], FP32))
        sem = own.enter_context(semaphores(nc, "co_"))
        loaded = sem("loaded")
        came = [sem(f"came{i}") for i in range(NT)]
        first = sem("first")
        done = sem("done")
        stored = sem("stored")
        block = own.enter_context(nc.Block())

        @block.sync
        def _(sp):
            sp.dma_start(acc[:], base.rearrange("(p t) n -> p t n", t=NT)).then_inc(loaded, 16)
            half = NT // 2
            for i in range(2):
                sp.wait_ge(done, half * (i + 1))
                sp.dma_start(x_out.rearrange("(p t) n -> p t n", t=NT)[:, i * half:(i + 1) * half],
                             acc[:, i * half:(i + 1) * half]).then_inc(stored, 16)
            sp.wait_ge(stored, 32)

        @block.gpsimd
        def _(g):
            for t in range(NT):
                for j in range(2):
                    nc.gpsimd.indirect_dma_start(
                        out=rows[:, j, t], out_offset=None, in_=yout[:],
                        in_offset=bass.IndirectOffsetOnAxis(ap=slots[:, j, t:t + 1], axis=0),
                        bounds_check=ROWS, oob_is_err=False).then_inc(came[t], 16)

        @block.vector
        def _(dve):
            dve.wait_ge(loaded, 16)
            for t in range(NT):
                dve.wait_ge(came[t], 32)
                nc.vector.scalar_tensor_tensor(acc[:, t], rows[:, 0, t], gates[:, 0, t:t + 1], acc[:, t],
                                               ALU.mult, ALU.add).then_inc(first, 1)
                dve.wait_ge(first, t + 1)
                nc.vector.scalar_tensor_tensor(acc[:, t], rows[:, 1, t], gates[:, 1, t:t + 1], acc[:, t],
                                               ALU.mult, ALU.add).then_inc(done, 1)


def moe(nc, base, xf, logits, x_out, w, c):
    with ExitStack() as own:
        slots = own.enter_context(nc.sbuf_tensor("moe_slots", [P, 2, NT], I32))
        gates = own.enter_context(nc.sbuf_tensor("moe_gates", [P, 2, NT], FP32))
        xin = nc.dram_tensor("expert_in", (ROWS, D), FP32).ap()
        yout = nc.dram_tensor("expert_out", (ROWS + 1, D), FP32).ap()
        with nc.sbuf_tensor("zeros", [P, 10 * D], FP32) as zeros:
            routing(nc, logits, slots, gates, zeros, xin, yout, c)
        dispatch(nc, xf, slots, xin)
        experts(nc, xin, yout, w["moe_w1"], w["moe_w2"], w["ln2_weight"], w["ln2_bias"], c)
        combine(nc, base, slots, gates, yout, x_out)


MAGIC = 12582912.0


def ternary_weights(nc, w, wq, wscale, c):
    names = list(wq)
    with ExitStack() as own:
        sb = lambda n, s, d=FP32: own.enter_context(nc.sbuf_tensor("tw_" + n, s, d))
        sem = own.enter_context(semaphores(nc, "tw_"))
        raw = {m: sb("raw_" + m, list(wq[m].shape)) for m in names}
        part = sb("part", [P, len(names)])
        mean = sb("mean", [P, len(names)])
        inv = sb("inv", [P, len(names)])
        tot = own.enter_context(nc.psum_tensor("tw_tot", [P, 16], FP32))
        loaded, summed, total, chain = (sem(m) for m in ("loaded", "summed", "total", "chain"))
        block = own.enter_context(nc.Block())
        flat = lambda t: t[:].rearrange("p c n -> p (c n)")

        @block.sync
        def _(sp):
            for m in names:
                sp.dma_start(raw[m][:], w[m].rearrange("(c p) n -> p c n", p=P)).then_inc(loaded, 16)

        @block.tensor
        def _(pe):
            for i in range(2):
                pe.wait_ge(summed, i + 1)
                nc.tensor.matmul(tot[:, 8 * i:8 * i + len(names)], c["ones"][:], part[:], start=True, stop=True).then_inc(total, 1)

        @block.vector
        def _(dve):
            ch = Chain(dve, chain)
            V = nc.vector
            dve.wait_ge(loaded, 16 * len(names))
            for j, m in enumerate(names):
                last = V.tensor_reduce(part[:, j:j + 1], flat(raw[m]), AX.X, ALU.add)
            last.then_inc(summed, 1)
            dve.wait_ge(total, 1)
            for j, m in enumerate(names):
                last = V.tensor_scalar(mean[:, j:j + 1], tot[:, j:j + 1], 1.0 / (P * raw[m].shape[1] * raw[m].shape[2]), None, ALU.mult)
            ch.link(last)
            for j, m in enumerate(names):
                last = V.tensor_scalar(flat(raw[m]), flat(raw[m]), mean[:, j:j + 1], None, ALU.subtract)
            ch.link(last)
            for j, m in enumerate(names):
                last = V.tensor_reduce(part[:, j:j + 1], flat(raw[m]), AX.X, ALU.add, apply_absolute_value=True)
            last.then_inc(summed, 1)
            dve.wait_ge(total, 2)
            for j, m in enumerate(names):
                last = V.tensor_scalar(mean[:, j:j + 1], tot[:, 8 + j:9 + j], 1.0 / (P * raw[m].shape[1] * raw[m].shape[2]), 1e-5,
                                       ALU.mult, ALU.max)
            ch.link(last)
            ch.link(V.reciprocal(inv[:], mean[:]))
            V.tensor_scalar(wscale[:], mean[:], 1.0 / 127, None, ALU.mult)
            for j, m in enumerate(names):
                ch.link(V.tensor_scalar(flat(raw[m]), flat(raw[m]), inv[:, j:j + 1], 1.0, ALU.mult, ALU.min))
                ch.link(V.tensor_scalar(flat(raw[m]), flat(raw[m]), -1.0, MAGIC, ALU.max, ALU.add))
                ch.link(V.tensor_scalar(flat(wq[m]), flat(raw[m]), -MAGIC, None, ALU.add))


def gated_recurrence(nc, x_in, x_out, w, c):
    UN = NB // 2
    CH = 64
    FD = 512
    FCH = FD // P
    N2 = 2 * S
    with ExitStack() as own:
        sb = lambda n, s, d=FP32: own.enter_context(nc.sbuf_tensor("gr_" + n, s, d))
        pb = lambda n, d=FP32: own.enter_context(nc.psum_tensor("gr_ps_" + n, [P, 2048 // mybir.dt.size(d)], d))
        sem = own.enter_context(semaphores(nc, "gr_"))
        two = lambda n: [sem(f"{n}{i}") for i in range(2)]
        wq = {"w_a": sb("w_a", [P, DC, D], BF16), "w_i": sb("w_i", [P, DC, D], BF16), "w_v": sb("w_v", [P, DC, D], BF16),
              "w_gate": sb("w_gate", [P, DC, FD], BF16), "w_down": sb("w_down", [P, FCH, D], BF16)}
        wscale = sb("wscale", [P, 5])
        ternary_weights(nc, w, wq, wscale, c)

        decay = sb("decay", [S, D])
        g_pre = sb("g_pre", [S, D])
        g_post = sb("g_post", [S, D])
        zero = sb("zero", [P, CH])
        inside = sb("inside", [P, 2 * DC, S])
        xt = sb("xt", [S, 2, 2, D])
        xx = sb("xx", [S, 4, 2, D])
        xl = sb("xl", [S, 2, D])
        h = sb("h", [S, 2, D])
        xs = sb("xs", [S, 2])
        r127 = sb("r127", [S, 2, 2])
        sc = sb("sc", [S, 2, 2, 3])
        qf = sb("qf", [S, 2, D])
        qb = sb("qb", [S, 2, D], BF16)
        xqT = sb("xqT", [P, DC, N2], BF16)
        za = sb("za", [S, 2, D])
        eai = sb("eai", [S, 2, 2 * D])
        ai = sb("ai", [S, 2, 2, 2 * D])
        vv = sb("vv", [S, 2 * D])
        om = sb("om", [S, 2, 2 * D])
        iv = sb("iv", [S, 2, 2 * D])
        sg = sb("sg", [S, 2 * D])
        aT = sb("aT", [P, 2 * DC, S])
        cum = sb("cum", [P, 2 * DC, S])
        rc = sb("rc", [P, 2 * DC, S])
        cs = sb("cs", [P, 2 * DC, S])
        rec = sb("rec", [P, 2 * DC, S])
        rt = sb("rt", [S, 2, 2, D])
        xr = sb("xr", [S, 4, 2, D])
        h2 = sb("h2", [S, 2, D])
        xs2 = sb("xs2", [S, 2])
        r2 = sb("r2", [S, 2, 2])
        sgt = sb("sgt", [S, 2, 2])
        q2f = sb("q2f", [S, 2, D])
        q2b = sb("q2b", [S, 2, D], BF16)
        q2T = sb("q2T", [P, DC, N2], BF16)
        th = sb("th", [S, 2, FD])
        zz = sb("zz", [S, 2, FD])
        hh = sb("hh", [S, 2, FD])
        xs3 = sb("xs3", [S, 2])
        r3 = sb("r3", [S, 2, 2])
        sd = sb("sd", [S, 2, 2])
        q3f = sb("q3f", [S, 2, FD])
        q3b = sb("q3b", [S, 2, FD], BF16)
        q3T = sb("q3T", [P, FCH, N2], BF16)
        y = sb("y", [S, 2, 2, D])
        ms = sb("ms", [S, 2])
        n1, n2, n3 = Norm(nc, sb, "n1", S, 2, 1e-5), Norm(nc, sb, "n2", S, 2, 0.0), Norm(nc, sb, "n3", S, 2, 0.0)
        ps_q, ps_h = pb("q", BF16), pb("h", BF16)
        ps_a, ps_i, ps_v, ps_at, ps_st, ps_r = (pb(m) for m in ("a", "i", "v", "at", "st", "r"))

        const, x_ready, x_stored = sem("const"), two("x_ready"), two("x_stored")
        names = ("xl_done xx_done h_done qf_done qb_done tq_done xqT_done aiv_done za_done ei_done ea_done vv_done ai_done om_done iv_done "
                 "sq_done sg_done t_done wt_done rec_done tr_done rt_done xr_done h2_done q2f_done q2b_done t2_done q2T_done "
                 "gate_done th_done hh_done q3f_done q3b_done t3_done q3T_done down_done y_done")
        m = {x: sem(x) for x in names.split()}
        chain = sem("chain")

        def n(k, p):
            return 4 * k + p

        def turn(k, p):
            return 2 * k + p // 2

        def after(k, p, eng, s, back=1):
            if not (isinstance(k, int) and n(k, p) < back):
                eng.wait_ge(m[s], n(k, p) - back + 1)

        def got(k, p, eng, s):
            eng.wait_ge(m[s], n(k, p) + 1)

        block = own.enter_context(nc.Block())
        row = lambda a: a.rearrange("(a n) -> a n", a=1).to_broadcast([S, D])
        pairs = lambda a: a.rearrange("(u b) s n -> u s b n", b=2)

        @block.sync
        def _(sp):
            for t, a in ((decay, "decay_bias"), (g_pre, "g_pre"), (g_post, "g_post")):
                sp.dma_start(t[:], row(w[a])).then_inc(const, 16)

            def load(k, p):
                after(k, p, sp, "xx_done", 2)
                sp.dma_start(xt[:, p % 2], pairs(x_in)[n(k, p)]).then_inc(x_ready[p % 2], 16)

            def store(k, p):
                got(k, p, sp, "y_done")
                sp.dma_start(pairs(x_out)[n(k, p)], y[:, p % 2]).then_inc(x_stored[p % 2], 16)

            pipeline(sp, UN, [(load, 0), (store, 6)], 4)
            for s in x_stored:
                sp.wait_ge(s, 16 * (UN // 2))

        @block.vector
        def _(dve):
            V = nc.vector
            ch = Chain(dve, chain)
            dve.wait_ge(const, 16 * 3)
            ch.link(V.memset(zero[:], 0.0))
            ch.link(V.memset(inside[:], 1.0))
            ch.link(V.memset(inside[:, :, 0:1], 0.0))
            ch.link(V.memset(inside[:, :, CH:CH + 1], 0.0))

            def rms_rows(nrm, src, g, out, eps):
                for b in range(2):
                    last = V.bn_stats(nrm.st[:, b], src(b))
                ch.link(last)
                for b in range(2):
                    last = V.bn_aggr(nrm.mv[:, b], nrm.st[:, b])
                ch.link(last)
                ch.link(V.tensor_tensor(ms[:], nrm.mv[:, :, 0], nrm.mv[:, :, 0], ALU.mult))
                ch.link(V.scalar_tensor_tensor(nrm.ve[:], ms[:], eps, nrm.mv[:, :, 1], ALU.add, ALU.add))
                rsqrt(nc, ch, nrm.rs[:], nrm.ve[:], nrm.t[:], nrm.ti[:])
                for b in range(2):
                    last = V.scalar_tensor_tensor(out[:, b], src(b), nrm.rs[:, b:b + 1], g[:], ALU.mult, ALU.mult)
                ch.link(last)

            def scale_of(src, xs_, r):
                ch.link(V.tensor_reduce(xs_[:], src[:], AX.X, ALU.max, apply_absolute_value=True))
                ch.link(V.tensor_scalar(xs_[:], xs_[:], 1e-5, None, ALU.max))
                ch.link(V.reciprocal(r, xs_[:]))
                return V.tensor_scalar(r, r, 127.0, None, ALU.mult)

            def d0(k, p):
                ch.begin()
                dve.wait_ge(x_ready[p % 2], 16 * (turn(k, p) + 1))
                n1.stats(ch, lambda b: xt[:, p % 2, b])
                after(k, p, dve, "xx_done")
                n1.apply(0, xl[:, 0], xt[:, p % 2, 0])
                n1.apply(1, xl[:, 1], xt[:, p % 2, 1]).then_inc(m["xl_done"], 1)
                got(k, p, dve, "xl_done")
                after(k, p, dve, "qf_done")
                rms_rows(n2, lambda b: xl[:, b], g_pre, h, 1e-6)
                after(k, p, dve, "vv_done", 2)
                ch.link(scale_of(h, xs, r127[:, p % 2]))
                ch.link(V.tensor_tensor(sc[:, p % 2], xs[:].unsqueeze(2).to_broadcast([S, 2, 3]),
                                        wscale[0:S, 0:3].unsqueeze(1).to_broadcast([S, 2, 3]), ALU.mult))
                V.tensor_scalar(sc[:, p % 2, :, 1], sc[:, p % 2, :, 1], -1.0, None, ALU.mult).then_inc(m["h_done"], 1)

            def integers(src, dst, s_in, s_used, s_out):
                def fn(k, p):
                    got(k, p, dve, s_in)
                    after(k, p, dve, s_used)
                    V.tensor_scalar(dst[:], src[:], -MAGIC, 127.0, ALU.add, ALU.min).then_inc(m[s_out], 1)
                return fn

            def d2(k, p):
                got(k, p, dve, "aiv_done")
                after(k, p, dve, "ea_done")
                for b in range(2):
                    last = V.scalar_tensor_tensor(za[:, b], ps_a[0:S, b * D:(b + 1) * D], sc[:, p % 2, b, 0:1], decay[:],
                                                  ALU.mult, ALU.add)
                last.then_inc(m["za_done"], 1)

            def d3(k, p):
                ch.begin()
                got(k, p, dve, "ea_done")
                got(k, p, dve, "ei_done")
                ch.link(V.tensor_scalar(eai[:], eai[:], 1.0, None, ALU.add))
                after(k, p, dve, "t_done", 2)
                after(k, p, dve, "iv_done", 2)
                V.reciprocal(ai[:, p % 2], eai[:]).then_inc(m["ai_done"], 1)
                got(k, p, dve, "ai_done")
                after(k, p, dve, "sg_done", 2)
                ch.link(V.scalar_tensor_tensor(om[:, p % 2], ai[:, p % 2, 0], -1.0, ai[:, p % 2, 0], ALU.mult, ALU.mult))
                V.tensor_scalar(om[:, p % 2], om[:, p % 2], 1.0, 1e-8, ALU.add, ALU.max).then_inc(m["om_done"], 1)

            def d4(k, p):
                got(k, p, dve, "sq_done")
                got(k, p, dve, "iv_done")
                after(k, p, dve, "t_done")
                V.tensor_tensor(sg[:], om[:, p % 2], iv[:, p % 2], ALU.mult).then_inc(m["sg_done"], 1)

            def d5(k, p):
                ch.begin()
                got(k, p, dve, "t_done")
                flat = lambda t: t[:].rearrange("p j n -> p (j n)")
                ch.link(V.tensor_scalar(flat(aT), ps_at[:, 0:2 * N2], 1e-10, None, ALU.max))
                for j in range(2 * DC):
                    for lo, hi in ((0, CH), (CH, S)):
                        last = V.tensor_tensor_scan(cum[:, j, lo:hi], aT[:, j, lo:hi], zero[:, 0:hi - lo], 1.0, ALU.mult, ALU.add)
                ch.link(last)
                ch.link(V.tensor_scalar(rc[:], cum[:], 1e-10, None, ALU.max))
                ch.link(V.reciprocal(rc[:], rc[:]))
                V.tensor_tensor(flat(rc), ps_st[:, 0:2 * N2], flat(rc), ALU.mult).then_inc(m["wt_done"], 1)
                got(k, p, dve, "wt_done")
                ch.link(V.tensor_tensor_scan(flat(cs), flat(inside), flat(rc), 0.0, ALU.mult, ALU.add))
                after(k, p, dve, "tr_done")
                ch.link(V.tensor_tensor(rec[:], cum[:], cs[:], ALU.mult))
                for j in range(2 * DC):
                    last = V.scalar_tensor_tensor(rec[:, j, CH:S], cum[:, j, CH:S], rec[:, j, CH - 1:CH], rec[:, j, CH:S],
                                                  ALU.mult, ALU.add)
                last.then_inc(m["rec_done"], 1)

            def d6(k, p):
                ch.begin()
                got(k, p, dve, "rt_done")
                after(k, p, dve, "q2f_done")
                rms_rows(n3, lambda b: rt[:, p % 2, b], g_post, h2, 1e-6)
                after(k, p, dve, "th_done", 2)
                ch.link(scale_of(h2, xs2, r2[:, p % 2]))
                V.tensor_scalar(sgt[:, p % 2], xs2[:], wscale[0:S, 3:4], 0.5, ALU.mult, ALU.mult).then_inc(m["h2_done"], 1)

            def d8(k, p):
                ch.begin()
                got(k, p, dve, "th_done")
                after(k, p, dve, "q3f_done")
                ch.link(V.scalar_tensor_tensor(hh[:], th[:], 1.0, zz[:], ALU.add, ALU.mult))
                ch.link(scale_of(hh, xs3, r3[:, p % 2]))
                after(k, p, dve, "y_done", 2)
                V.tensor_scalar(sd[:, p % 2], xs3[:], wscale[0:S, 4:5], None, ALU.mult).then_inc(m["hh_done"], 1)

            def d10(k, p):
                got(k, p, dve, "down_done")
                got(k, p, dve, "xr_done")
                if not (isinstance(k, int) and n(k, p) < 2):
                    dve.wait_ge(x_stored[p % 2], 16 * turn(k, p))
                for b in range(2):
                    last = V.scalar_tensor_tensor(y[:, p % 2, b], ps_v[0:S, b * D:(b + 1) * D], sd[:, p % 2, b:b + 1], xr[:, p, b],
                                                  ALU.mult, ALU.add)
                last.then_inc(m["y_done"], 1)

            pipeline(dve, UN, [(d6, 3), (d4, 2), (d2, 1), (d8, 4), (d10, 5), (d0, 0),
                               (d5, 2), (integers(q2f, q2b, "q2f_done", "t2_done", "q2b_done"), 3), (d3, 1),
                               (integers(q3f, q3b, "q3f_done", "t3_done", "q3b_done"), 4),
                               (integers(qf, qb, "qf_done", "tq_done", "qb_done"), 0)], 4)

        @block.tensor
        def _(pe):
            def reached(k, p, ahead, s):
                pe.wait_ge(m[s], (min(n(k, p) + ahead, UN - 1) if isinstance(k, int) else n(k, p) + ahead) + 1)

            def quantized(src, ps, chunks, s_in, frees, s_out):
                def fn(k, p):
                    got(k, p, pe, s_in)
                    for s_, back in frees:
                        if back > 0:
                            after(k, p, pe, s_, back)
                        else:
                            reached(k, p, -back, s_)
                    for i in range(chunks):
                        for b in range(2):
                            last = nc.tensor.transpose(ps[:, i * N2 + b * S:i * N2 + (b + 1) * S], src[:, b, i * P:(i + 1) * P],
                                                       c["ident_bf"][0:S, 0:S])
                    last.then_inc(m[s_out], 1)
                return fn

            def aiv(k, p):
                got(k, p, pe, "xqT_done")
                after(k, p, pe, "th_done", 4)
                after(k, p, pe, "za_done")
                after(k, p, pe, "ei_done")
                after(k, p, pe, "vv_done")
                after(k, p, pe, "y_done", 5)
                for name, ps in (("w_a", ps_a), ("w_i", ps_i), ("w_v", ps_v)):
                    for b in range(2):
                        for i in range(DC):
                            last = nc.tensor.matmul(ps[0:S, b * D:(b + 1) * D], xqT[:, i, b * S:(b + 1) * S], wq[name][:, i],
                                                    start=i == 0, stop=i == DC - 1)
                last.then_inc(m["aiv_done"], 1)

            def gate(k, p):
                got(k, p, pe, "q2T_done")
                reached(k, p, 3, "za_done")
                reached(k, p, 3, "ei_done")
                after(k, p, pe, "th_done")
                for b, ps in enumerate((ps_a, ps_i)):
                    for i in range(DC):
                        last = nc.tensor.matmul(ps[0:S, :], q2T[:, i, b * S:(b + 1) * S], wq["w_gate"][:, i],
                                                start=i == 0, stop=i == DC - 1)
                last.then_inc(m["gate_done"], 1)

            def down(k, p):
                got(k, p, pe, "q3T_done")
                reached(k, p, 4, "vv_done")
                after(k, p, pe, "y_done")
                for b in range(2):
                    for i in range(FCH):
                        last = nc.tensor.matmul(ps_v[0:S, b * D:(b + 1) * D], q3T[:, i, b * S:(b + 1) * S], wq["w_down"][:, i],
                                                start=i == 0, stop=i == FCH - 1)
                last.then_inc(m["down_done"], 1)

            def channel_major(k, p):
                got(k, p, pe, "sg_done")
                after(k, p, pe, "wt_done")
                for src, ps in ((ai[:, p % 2, 0], ps_at), (sg[:], ps_st)):
                    for i in range(DC):
                        for b in range(2):
                            last = nc.tensor.transpose(ps[:, i * N2 + b * S:i * N2 + (b + 1) * S],
                                                       src[:, b * D + i * P:b * D + (i + 1) * P], c["ident"][0:S, 0:S])
                last.then_inc(m["t_done"], 1)

            def token_major(k, p):
                got(k, p, pe, "rec_done")
                after(k, p, pe, "rt_done")
                for i in range(DC):
                    for b in range(2):
                        last = nc.tensor.transpose(ps_r[0:S, b * D + i * P:b * D + (i + 1) * P], rec[:, 2 * i + b], c["ident"][:])
                last.then_inc(m["tr_done"], 1)

            pipeline(pe, UN, [(token_major, 3),
                              (quantized(qb, ps_q, DC, "qb_done", [("xqT_done", 1)], "tq_done"), 1),
                              (quantized(q2b, ps_h, DC, "q2b_done", [("q2T_done", 1), ("q3T_done", 2)], "t2_done"), 4),
                              (aiv, 1),
                              (quantized(q3b, ps_h, FCH, "q3b_done", [("q3T_done", 1), ("q2T_done", -1)], "t3_done"), 5),
                              (gate, 4), (down, 5), (channel_major, 2)], 4)

        @block.scalar
        def _(act):
            A = nc.scalar.activation

            def root(k, p):
                got(k, p, act, "om_done")
                A(om[:, p % 2], om[:, p % 2], ACT.Sqrt).then_inc(m["sq_done"], 1)

            def copy_rec(k, p):
                got(k, p, act, "tr_done")
                after(k, p, act, "h2_done", 2)
                after(k, p, act, "xr_done", 2)
                A(rt[:, p % 2].rearrange("s b n -> s (b n)"), ps_r[0:S, :], ACT.Copy).then_inc(m["rt_done"], 1)

            def copy_q(dst, ps, s_in, s_used, s_out):
                def fn(k, p):
                    got(k, p, act, s_in)
                    after(k, p, act, s_used)
                    flat = dst[:].rearrange("p c n -> p (c n)")
                    A(flat, ps[:, 0:flat.shape[1]], ACT.Copy).then_inc(m[s_out], 1)
                return fn

            def exponents(k, p):
                got(k, p, act, "aiv_done")
                after(k, p, act, "ai_done")
                for b in range(2):
                    last = A(eai[:, 1, b * D:(b + 1) * D], ps_i[0:S, b * D:(b + 1) * D], ACT.Exp, scale=sc[:, p % 2, b, 1:2])
                last.then_inc(m["ei_done"], 1)
                after(k, p, act, "iv_done")
                for b in range(2):
                    last = A(vv[:, b * D:(b + 1) * D], ps_v[0:S, b * D:(b + 1) * D], ACT.Copy, scale=sc[:, p % 2, b, 2:3])
                last.then_inc(m["vv_done"], 1)
                got(k, p, act, "za_done")
                A(eai[:, 0], za[:].rearrange("s b n -> s (b n)"), ACT.Exp, scale=-1.0).then_inc(m["ea_done"], 1)

            def gates(k, p):
                got(k, p, act, "gate_done")
                after(k, p, act, "hh_done")
                for b, ps in enumerate((ps_a, ps_i)):
                    A(th[:, b], ps[0:S, :], ACT.Tanh, scale=sgt[:, p % 2, b:b + 1])
                    last = A(zz[:, b], ps[0:S, :], ACT.Copy, scale=sgt[:, p % 2, b:b + 1])
                last.then_inc(m["th_done"], 1)

            def quantize(src, r, dst, s_in, s_used, s_out):
                def fn(k, p):
                    got(k, p, act, s_in)
                    after(k, p, act, s_used)
                    for b in range(2):
                        last = A(dst[:, b], src[:, b], ACT.Copy, bias=MAGIC, scale=r[:, p % 2, b:b + 1])
                    last.then_inc(m[s_out], 1)
                return fn

            pipeline(act, UN, [(root, 2), (copy_rec, 3), (copy_q(xqT, ps_q, "tq_done", "aiv_done", "xqT_done"), 1),
                               (copy_q(q2T, ps_h, "t2_done", "gate_done", "q2T_done"), 4),
                               (exponents, 1), (copy_q(q3T, ps_h, "t3_done", "down_done", "q3T_done"), 5), (gates, 4),
                               (quantize(h2, r2, q2f, "h2_done", "q2b_done", "q2f_done"), 3),
                               (quantize(hh, r3, q3f, "hh_done", "q3b_done", "q3f_done"), 4),
                               (quantize(h, r127, qf, "h_done", "qb_done", "qf_done"), 0)], 4)

        @block.gpsimd
        def _(g):
            def gated(k, p):
                got(k, p, g, "ai_done")
                got(k, p, g, "vv_done")
                after(k, p, g, "sg_done", 2)
                nc.gpsimd.tensor_tensor(iv[:, p % 2], ai[:, p % 2, 1], vv[:], ALU.mult).then_inc(m["iv_done"], 1)

            def normed(k, p):
                got(k, p, g, "xl_done")
                after(k, p, g, "xr_done", 4)
                nc.gpsimd.tensor_tensor(xx[:, p], xt[:, p % 2], xl[:], ALU.add).then_inc(m["xx_done"], 1)

            def add(k, p):
                got(k, p, g, "xx_done")
                got(k, p, g, "rt_done")
                after(k, p, g, "y_done", 4)
                nc.gpsimd.tensor_tensor(xr[:, p], xx[:, p], rt[:, p % 2], ALU.add).then_inc(m["xr_done"], 1)

            pipeline(g, UN, [(add, 3), (normed, 0), (gated, 1)], 4)


def linear_cross_attention(nc, x_in, ctx, x_out, w, c):
    H, DH, HD = 8, 64, 512
    HC = HD // P
    KT = T + 1
    with ExitStack() as own:
        sb = lambda n, s, d=FP32: own.enter_context(nc.sbuf_tensor("lc_" + n, s, d))
        pb = lambda n, s: own.enter_context(nc.psum_tensor("lc_ps_" + n, s, FP32))
        sem = own.enter_context(semaphores(nc, "lc_"))
        wq = sb("wq", [P, DC, HD])
        wkv = sb("wkv", [P, DC, 2 * HD])
        wo = sb("wo", [P, HC, D])
        qg, qbias = sb("qg", [S, HD]), sb("qbias", [S, HD])
        og, ob = sb("og", [P, HC]), sb("ob", [P, HC])
        nk = sb("nk", [P, 1])
        nks = sb("nks", [P, HC])
        rows = TokenRows(nc, sb, sem)
        ct = sb("ct", [TN, 2, TC, D])
        xn = sb("xn", [S, D])
        xcT = sb("xcT", [P, DC, T + S])
        vs = sb("vs", [TN + 1, 2, TC, HD])
        kmx = sb("kmx", [P, HC])
        eT = sb("eT", [P, 2, HC, KT])
        ksum = sb("ksum", [P, 2, HC])
        eK = sb("eK", [TN + 1, TC, HD])
        q1 = sb("q1", [S, HD])
        qa = sb("qa", [S, HD])
        qmx = sb("qmx", [S, H])
        qs = sb("qs", [S, HD])
        qr = sb("qr", [S, H])
        qn = sb("qn", [S, HD])
        qT = sb("qT", [P, HC * S])
        cx = sb("cx", [P, HC, P])
        on = sb("on", [S, HD])
        oT = sb("oT", [P, HC, S])
        nqo = Norm(nc, sb, "nqo", S, 2, 1e-5)
        ps_ab = pb("ab", [P, 2, 512])
        ps_q = pb("q", [P, 512])
        ps_t = pb("t", [P, 512])
        ps_k = pb("k", [P, 4, 512])
        c_ready = [sem(f"c_ready{i}") for i in range(2)]
        weights, nulls = sem("weights"), sem("nulls")
        names = ("xn_done t_done xcT_done q_done v01_done k012_done v2_done k3_done qn1_done qg_done qa_done qsub_done "
                 "qexp_done qsum_done qn_done vc01_done vc2_done max012_done max3_done exp012_done exp3_done ksum_done te_done "
                 "eK_done tq_done qT_done cx_done cxc_done o_done on_done to_done oT_done y_ps_done y_done")
        m = {x: sem(x) for x in names.split()}
        chain = sem("chain")

        def n(k, p):
            return 4 * k + p

        def after(k, p, eng, s, back=1):
            if not (isinstance(k, int) and n(k, p) < back):
                eng.wait_ge(m[s], n(k, p) - back + 1)

        def got(k, p, eng, s):
            eng.wait_ge(m[s], n(k, p) + 1)

        block = own.enter_context(nc.Block())
        @block.sync
        def _(sp):
            rows.load(sp, x_in)
            sp.dma_start(wkv[:], w["Wkv"].rearrange("(c p) n -> p c n", p=P)).then_inc(weights, 16)
            sp.dma_start(wq[:], w["Wq"].rearrange("(c p) n -> p c n", p=P)).then_inc(weights, 16)
            sp.dma_start(wo[:], w["Wout"].rearrange("(c p) n -> p c n", p=P)).then_inc(weights, 16)
            for t, a in ((qg, "ln_q_g"), (qbias, "ln_q_b")):
                sp.dma_start(t[:], w[a].rearrange("(a n) -> a n", a=1).to_broadcast([S, HD])).then_inc(weights, 16)
            for t, a in ((og, "ln_out_g"), (ob, "ln_out_b")):
                sp.dma_start(t[:], w[a].rearrange("(c p) -> p c", p=P), allow_slow_non_contiguous=True).then_inc(weights, 16)
            sp.dma_start(nk[0:DH], w["null_kv"][0:1].rearrange("a d -> d a"), allow_slow_non_contiguous=True).then_inc(nulls, 16)
            sp.dma_start(nk[DH:P], w["null_kv"][0:1].rearrange("a d -> d a"), allow_slow_non_contiguous=True).then_inc(nulls, 16)
            for q in range(2):
                sp.dma_start(vs[TN:TN + 1, q, TC - 1].rearrange("a (h d) -> a h d", h=H),
                             w["null_kv"][1:2].unsqueeze(1).to_broadcast([1, H, DH])).then_inc(nulls, 16)

            def load(k, p):

                after(k, p, sp, "t_done", 2)
                sp.dma_start(ct[:, p % 2], ctx[n(k, p)].rearrange("(c t) n -> t c n", c=TC)).then_inc(c_ready[p % 2], 16)

            def store(k, p):
                got(k, p, sp, "y_done")
                sp.dma_start(x_out[n(k, p)], rows.batch(n(k, p))).then_inc(rows.stored, 16)

            pipeline(sp, NB, [(load, 0), (store, 3)], 4)
            sp.wait_ge(rows.stored, 16 * NB)

        @block.vector
        def _(dve):
            V = nc.vector
            ch = Chain(dve, chain)
            ch.link(V.memset(cx[:], 0.0))
            dve.wait_ge(nulls, 16 * 4)
            rows.stats(dve, ch)

            def norm(k, p):
                after(k, p, dve, "t_done")
                rows.normed(n(k, p), xn[:]).then_inc(m["xn_done"], 1)

            def norms(k, p):
                last = isinstance(k, int) and n(k, p) == NB - 1
                ch.begin()
                got(k, p, dve, "o_done")
                if not last:
                    dve.wait_ge(m["q_done"], n(k, p) + 2)
                    nqo.stats(ch, lambda r: (ps_q[0:S, :], ps_k[0:S, 3])[r])
                    dve.wait_ge(m["qg_done"], n(k, p) + 1)
                    nqo.apply(0, q1[:], ps_q[0:S, :]).then_inc(m["qn1_done"], 1)
                else:
                    nqo.stats(ch, lambda r: ps_k[0:S, 3])
                after(k, p, dve, "to_done")
                nqo.apply(1, on[:], ps_k[0:S, 3]).then_inc(m["on_done"], 1)

            def first_norm(k, p):
                if isinstance(k, int) and n(k, p) == 0:
                    ch.begin()
                    got(k, p, dve, "q_done")
                    nqo.stats(ch, lambda r: ps_q[0:S, :])
                    nqo.apply(0, q1[:], ps_q[0:S, :]).then_inc(m["qn1_done"], 1)

            def q_shift(k, p):
                ch.begin()
                got(k, p, dve, "qa_done")
                after(k, p, dve, "qn_done")
                heads = lambda t: t[:].rearrange("s (h d) -> s h d", h=H)
                ch.link(V.tensor_reduce(qmx[:], heads(qa), AX.X, ALU.max))
                V.tensor_tensor(heads(qs), heads(qa), qmx[:].unsqueeze(2).to_broadcast([S, H, DH]), ALU.subtract).then_inc(m["qsub_done"], 1)

            def q_sum(k, p):
                ch.begin()
                got(k, p, dve, "qexp_done")
                ch.link(V.tensor_reduce(qr[:], qs[:].rearrange("s (h d) -> s h d", h=H), AX.X, ALU.add))
                ch.link(V.reciprocal(qr[:], qr[:]))
                V.tensor_scalar(qr[:], qr[:], 8.0, None, ALU.mult).then_inc(m["qsum_done"], 1)

            def values01(k, p):
                got(k, p, dve, "v01_done")
                after(k, p, dve, "cx_done", 2)
                V.tensor_copy(vs[0:TN, p % 2, 0:2], ps_ab[0:TN]).then_inc(m["vc01_done"], 1)

            def values2(k, p):
                got(k, p, dve, "v2_done")
                V.tensor_copy(vs[0:TN, p % 2, 2], ps_ab[0:TN, 0]).then_inc(m["vc2_done"], 1)

            def keys_max(lo, hi, s_in, s_out):
                def fn(k, p):
                    ch.begin()
                    got(k, p, dve, s_in)
                    if lo == 0:
                        after(k, p, dve, "ksum_done")
                    ch.link(V.tensor_reduce(kmx[:, lo:hi], ps_k[:, lo:hi, 0:T], AX.X, ALU.max))
                    V.tensor_scalar(kmx[:, lo:hi], kmx[:, lo:hi], nk[:], -1.0, ALU.max, ALU.mult).then_inc(m[s_out], 1)
                return fn

            def keys_sum(k, p):
                ch.begin()
                got(k, p, dve, "exp3_done")
                after(k, p, dve, "cxc_done")
                ch.link(V.tensor_tensor(ksum[:, p % 2], ksum[:, p % 2], eT[:, p % 2, :, T], ALU.add))
                V.reciprocal(ksum[:, p % 2], ksum[:, p % 2]).then_inc(m["ksum_done"], 1)

            def context(k, p):
                got(k, p, dve, "cx_done")
                after(k, p, dve, "o_done")
                got(k, p, dve, "ksum_done")
                for e in range(2):
                    r = slice(DH * e, DH * (e + 1))
                    last = V.tensor_tensor(cx[r, :, r], ps_k[r, 3].rearrange("d (m n) -> d m n", m=HC)[:, :, r],
                                           ksum[r, p % 2].unsqueeze(2).to_broadcast([DH, HC, DH]), ALU.mult)
                last.then_inc(m["cxc_done"], 1)



            def residual(k, p):
                got(k, p, dve, "y_ps_done")
                V.tensor_tensor(rows.batch(n(k, p)), ps_q[0:S, 0:D], rows.batch(n(k, p)), ALU.add).then_inc(m["y_done"], 1)

            pipeline(dve, NB, [(context, 2), (values01, 1), (norm, 0), (first_norm, 1), (norms, 2),
                               (keys_max(0, 3, "k012_done", "max012_done"), 1), (q_shift, 1), (values2, 1),
                               (keys_max(3, 4, "k3_done", "max3_done"), 1), (residual, 2), (q_sum, 1), (keys_sum, 1)], 4)

        @block.tensor
        def _(pe):
            pe.wait_ge(weights, 16 * 7)
            pe.wait_ge(nulls, 16 * 4)

            def exps_t(k, p):
                got(k, p, pe, "exp3_done")
                after(k, p, pe, "eK_done")
                for t in range(TC):
                    hi = TN + (t == TC - 1)
                    for i in range(HC):
                        last = nc.tensor.transpose(ps_k[0:hi, t, i * P:(i + 1) * P], eT[:, p % 2, i, t * TN:t * TN + hi], c["ident"][:])
                last.then_inc(m["te_done"], 1)

            def transposed(k, p):
                pe.wait_ge(c_ready[p % 2], 16 * (2 * k + p // 2 + 1))
                after(k, p, pe, "vc2_done")
                after(k, p, pe, "vc01_done")
                for t in range(TC):
                    for i in range(DC):
                        nc.tensor.transpose(ps_ab[:, i, t * TN:(t + 1) * TN], ct[:, p % 2, t, i * P:(i + 1) * P], c["ident"][0:TN, 0:TN])
                got(k, p, pe, "xn_done")
                for i in range(DC):
                    last = nc.tensor.transpose(ps_ab[:, i, T:T + S], xn[:, i * P:(i + 1) * P], c["ident"][0:S, 0:S])
                last.then_inc(m["t_done"], 1)

            def queries_t(k, p):
                got(k, p, pe, "qn_done")
                after(k, p, pe, "oT_done")
                for i in range(HC):
                    last = nc.tensor.transpose(ps_t[:, i * S:(i + 1) * S], qn[:, i * P:(i + 1) * P], c["ident"][0:S, 0:S])
                last.then_inc(m["tq_done"], 1)

            def context(k, p):
                got(k, p, pe, "eK_done")
                got(k, p, pe, "vc2_done")
                got(k, p, pe, "vc01_done")
                for i in range(HC):
                    for t in range(TC):
                        hi = TN + (t == TC - 1)
                        last = nc.tensor.matmul(ps_k[:, 3, i * P:(i + 1) * P], eK[0:hi, t, i * P:(i + 1) * P],
                                                vs[0:hi, p % 2, t, i * P:(i + 1) * P], start=t == 0, stop=t == TC - 1)
                last.then_inc(m["cx_done"], 1)

            def queries(k, p):
                got(k, p, pe, "xcT_done")
                after(k, p, pe, "qn1_done")
                after(k, p, pe, "y_done", 2)
                for i in range(DC):
                    last = nc.tensor.matmul(ps_q[0:S, :], xcT[:, i, T:T + S], wq[:, i], start=i == 0, stop=i == DC - 1)
                last.then_inc(m["q_done"], 1)

            def value(t, bank, s_out):
                def fn(k, p):
                    if t == 2:
                        got(k, p, pe, "vc01_done")
                    for i in range(DC):
                        last = nc.tensor.matmul(ps_ab[0:TN, bank], xcT[:, i, t * TN:(t + 1) * TN], wkv[:, i, HD:2 * HD],
                                                start=i == 0, stop=i == DC - 1)
                    if s_out:
                        last.then_inc(m[s_out], 1)
                return fn

            def output(k, p):
                got(k, p, pe, "cxc_done")
                got(k, p, pe, "qT_done")
                for i in range(HC):
                    last = nc.tensor.matmul(ps_k[0:S, 3, i * P:(i + 1) * P], qT[:, i * S:(i + 1) * S], cx[:, i], start=True, stop=True)
                last.then_inc(m["o_done"], 1)

            def keys(chunks, s_out):
                def fn(k, p):
                    if chunks[0] == 0:
                        after(k, p, pe, "eK_done")
                    else:
                        after(k, p, pe, "on_done")
                    for o in chunks:
                        for i in range(DC):
                            last = nc.tensor.matmul(ps_k[:, o, 0:T], wkv[:, i, o * P:(o + 1) * P], xcT[:, i, 0:T],
                                                    start=i == 0, stop=i == DC - 1)
                    last.then_inc(m[s_out], 1)
                return fn

            def output_t(k, p):
                got(k, p, pe, "on_done")
                got(k, p, pe, "qT_done")
                for i in range(HC):
                    last = nc.tensor.transpose(ps_t[:, i * S:(i + 1) * S], on[:, i * P:(i + 1) * P], c["ident"][0:S, 0:S])
                last.then_inc(m["to_done"], 1)

            def project(k, p):
                got(k, p, pe, "oT_done")
                after(k, p, pe, "y_done")
                if not (isinstance(k, int) and n(k, p) == NB - 1):
                    pe.wait_ge(m["qn1_done"], n(k, p) + 2)
                for i in range(HC):
                    last = nc.tensor.matmul(ps_q[0:S, 0:D], oT[:, i], wo[:, i], start=i == 0, stop=i == HC - 1)
                last.then_inc(m["y_ps_done"], 1)

            pipeline(pe, NB, [(exps_t, 2), (transposed, 1), (queries_t, 2), (context, 2), (queries, 1), (value(0, 0, None), 1),
                              (output, 2), (value(1, 1, "v01_done"), 1), (keys((0, 1, 2), "k012_done"), 1),
                              (keys((3,), "k3_done"), 1), (output_t, 2), (value(2, 0, "v2_done"), 1), (project, 2)], 4)

        @block.scalar
        def _(act):
            A = nc.scalar.activation
            act.wait_ge(weights, 16 * 7)
            act.wait_ge(nulls, 16 * 4)

            def copy_e(k, p):
                got(k, p, act, "te_done")
                after(k, p, act, "cx_done")
                A(eK[0:TN, 0:2], ps_k[0:TN, 0:2], ACT.Copy)
                A(eK[:, 2], ps_k[0:TN + 1, 2], ACT.Copy).then_inc(m["eK_done"], 1)

            def copy_t(k, p):
                got(k, p, act, "t_done")
                after(k, p, act, "k3_done")
                A(xcT[:], ps_ab[:, :, 0:T + S], ACT.Copy).then_inc(m["xcT_done"], 1)

            def copy_q(k, p):
                got(k, p, act, "tq_done")
                after(k, p, act, "o_done")
                A(qT[:], ps_t[:, 0:HC * S], ACT.Copy).then_inc(m["qT_done"], 1)

            def q_exp(k, p):
                got(k, p, act, "qsub_done")
                A(qs[:], qs[:], ACT.Exp).then_inc(m["qexp_done"], 1)

            def keys_exp(chunks, s_in, s_out):
                def fn(k, p):
                    got(k, p, act, s_in)
                    after(k, p, act, "te_done", 2)
                    after(k, p, act, "cxc_done", 2)
                    for o in chunks:
                        A(eT[:, p % 2, o, 0:T], ps_k[:, o, 0:T], ACT.Exp, bias=kmx[:, o:o + 1], accum_out=ksum[:, p % 2, o:o + 1])
                        last = A(eT[:, p % 2, o, T:KT], nk[:], ACT.Exp, bias=kmx[:, o:o + 1])
                    last.then_inc(m[s_out], 1)
                return fn

            def copy_o(k, p):
                got(k, p, act, "to_done")
                after(k, p, act, "y_ps_done")
                for i in range(HC):
                    last = A(oT[:, i], ps_t[:, i * S:(i + 1) * S], ACT.Identity, bias=ob[:, i:i + 1], scale=og[:, i:i + 1])
                last.then_inc(m["oT_done"], 1)

            pipeline(act, NB, [(copy_e, 2), (copy_t, 1), (copy_q, 2), (keys_exp((0, 1, 2), "max012_done", "exp012_done"), 1),
                               (copy_o, 2), (q_exp, 1), (keys_exp((3,), "max3_done", "exp3_done"), 1)], 4)

        @block.gpsimd
        def _(g):
            g.wait_ge(weights, 16 * 7)

            def q_affine(k, p):
                got(k, p, g, "qn1_done")
                after(k, p, g, "qsub_done")
                nc.gpsimd.tensor_tensor(qa[:], q1[:], qg[:], ALU.mult).then_inc(m["qg_done"], 1)
                got(k, p, g, "qg_done")
                nc.gpsimd.tensor_tensor(qa[:], qa[:], qbias[:], ALU.add).then_inc(m["qa_done"], 1)

            def q_scaled(k, p):
                got(k, p, g, "qsum_done")
                after(k, p, g, "tq_done")
                heads = lambda t: t[:].rearrange("s (h d) -> s h d", h=H)
                nc.gpsimd.tensor_tensor(heads(qn), heads(qs), qr[:].unsqueeze(2).to_broadcast([S, H, DH]), ALU.mult).then_inc(m["qn_done"], 1)

            pipeline(g, NB, [(q_affine, 1), (q_scaled, 1)], 4)


def int8_projection(nc, x_in, x_out, w, c):
    TP = NT // 2
    with ExitStack() as own:
        sb = lambda n, s, d=FP32: own.enter_context(nc.sbuf_tensor("ip_" + n, s, d))
        pb = lambda n, d=FP32, k=512: own.enter_context(nc.psum_tensor("ip_ps_" + n, [P, k], d))
        sem = own.enter_context(semaphores(nc, "ip_"))
        two = lambda n: [sem(f"{n}{i}") for i in range(2)]

        w8 = sb("w8", [P, DC, D // 4], I32)
        wb = sb("wb", [P, DC, D], BF16)
        wsc = sb("wsc", [P, 2, D])
        bias = sb("bias", [P, 2, D])
        x = sb("x", [P, TP, 2, D])
        h = sb("h", [P, TP, 2, D])
        nrm = Norm(nc, sb, "ln", P, NT, 1e-5)
        part = sb("part", [P, TP])
        diag = sb("diag", [P, P])
        top = sb("top", [P, 1])
        xs = sb("xs", [P, 1])
        inv = sb("inv", [P, 1])
        q = sb("q", [P, 2, 2 * D])
        qb = sb("qb", [P, 2, 2 * D], BF16)
        qT = sb("qT", [P, 2, 2, DC, P], BF16)
        xb = sb("xb", [P, 2, 2, D])
        y = sb("y", [P, 2, 2, D])
        ps_m = pb("m")
        ps_t = [pb(f"t{i}", BF16, 1024) for i in range(2)]
        ps_o = [pb(f"o{i}") for i in range(2)]

        weights, w_ready = sem("weights_loaded"), sem("w_ready")
        x_loaded = [sem(f"x_loaded{i}") for i in range(7)]
        diag_done, top_done, chain = sem("diag_done"), sem("top_done"), sem("chain")
        t_done, qb_done, qT_done, o_done, xb_done, y_done, y_stored = (
            two(m) for m in ("t_done", "qb_done", "qT_done", "o_done", "xb_done", "y_done", "y_stored"))
        pairs = lambda a: a.rearrange("(p t r) n -> t p r n", r=2, t=TP)
        block = own.enter_context(nc.Block())

        def item(k, p):
            return 2 * k + p

        @block.sync
        def _(sp):
            for i in range(7):
                sp.dma_start(x[:, 2 * i:2 * i + 2], x_in.rearrange("(p t r) n -> p t r n", r=2, t=TP)[:, 2 * i:2 * i + 2]
                             ).then_inc(x_loaded[i], 16)
            sp.dma_start(w8[:], w["weight_int8"].rearrange("(c p) n -> p c n", p=P)).then_inc(weights, 16)
            for r in range(2):
                sp.dma_start(wsc[:, r], w["weight_scale"].rearrange("n a -> a n").to_broadcast([P, D])).then_inc(weights, 16)
                sp.dma_start(bias[:, r], w["bias"].rearrange("(a n) -> a n", a=1).to_broadcast([P, D])).then_inc(weights, 16)

            def store(k, p):
                sp.wait_ge(y_done[p], k + 1)
                sp.dma_start(pairs(x_out)[item(k, p)], y[:, p]).then_inc(y_stored[p], 16)

            pipeline(sp, TP, [(store, 0)])
            for p in range(2):
                sp.wait_ge(y_stored[p], 16 * (TP // 2))

        @block.gpsimd
        def _(g):
            g.wait_ge(weights, 16 * 5)
            for i in range(7):
                g.wait_ge(x_loaded[i], 16)

            def add_bias(k, p):
                if later(k):
                    g.wait_ge(y_done[p], k)
                nc.gpsimd.tensor_tensor(xb[:, p], x[:, item(k, p)] if isinstance(k, int) else x[:, bass.ds(item(k, p), 1)].rearrange("p a r n -> p (a r) n"),
                                        bias[:], ALU.add).then_inc(xb_done[p], 1)

            pipeline(g, TP, [(add_bias, 0)])

        @block.tensor
        def _(pe):
            pe.wait_ge(diag_done, 1)
            nc.tensor.matmul(ps_m[:, 0:P], c["ones"][:], diag[:], start=True, stop=True).then_inc(top_done, 1)
            pe.wait_ge(w_ready, 1)

            def transposed(k, p):
                pe.wait_ge(qb_done[p], k + 1)
                if later(k):
                    pe.wait_ge(qT_done[p], k)
                for i in range(2 * DC):
                    last = nc.tensor.transpose(ps_t[p][:, i * P:(i + 1) * P], qb[:, p, i * P:(i + 1) * P], c["ident_bf"][:])
                last.then_inc(t_done[p], 1)

            def product(k, p):
                pe.wait_ge(qT_done[p], k + 1)
                if later(k):
                    pe.wait_ge(y_done[p], k)
                for r in range(2):
                    for i in range(DC):
                        last = nc.tensor.matmul(ps_o[p][:, r * D:(r + 1) * D], qT[:, p, r, i], wb[:, i], start=i == 0, stop=i == DC - 1)
                last.then_inc(o_done[p], 1)

            pipeline(pe, TP, [(transposed, 0), (product, 1)])

        @block.scalar
        def _(act):
            def copy_t(k, p):
                act.wait_ge(t_done[p], k + 1)
                if later(k):
                    act.wait_ge(o_done[p], k)
                nc.scalar.activation(qT[:, p].rearrange("p r c n -> p (r c n)"), ps_t[p][:, 0:4 * P], ACT.Copy).then_inc(qT_done[p], 1)

            pipeline(act, TP, [(copy_t, 0)])

        @block.vector
        def _(dve):
            ch = Chain(dve, chain)
            V = nc.vector

            def row(t):
                if t % 4 == 0:
                    dve.wait_ge(x_loaded[t // 4], 16)
                return x[:, t // 2, t % 2]

            nrm.stats(ch, row)
            for t in range(NT):
                last = nrm.apply(t, h[:, t // 2, t % 2], x[:, t // 2, t % 2])
            ch.link(last)
            ch.link(V.tensor_reduce(part[:], h[:].rearrange("p t r n -> p t (r n)"), AX.X, ALU.max, apply_absolute_value=True))
            ch.link(V.tensor_reduce(top[:], part[:], AX.X, ALU.max))
            V.tensor_scalar(diag[:], c["ident"][:], top[:, 0:1], None, ALU.mult).then_inc(diag_done, 1)
            dve.wait_ge(weights, 16 * 5)
            V.tensor_copy(wb[:], w8[:].bitcast(I8)).then_inc(w_ready, 1)
            dve.wait_ge(top_done, 1)
            ch.link(V.tensor_reduce(top[:], ps_m[:, 0:P], AX.X, ALU.max))
            ch.link(V.tensor_scalar(xs[:], top[:], 1.0 / 127, 1e-5, ALU.mult, ALU.max))
            ch.link(V.reciprocal(inv[:], xs[:]))

            def quantize(k, p):
                ch.begin()
                src = h[:, item(k, p)] if isinstance(k, int) else h[:, bass.ds(item(k, p), 1)].rearrange("p a r n -> p (a r) n")
                ch.link(V.tensor_scalar(q[:, p].rearrange("p (r n) -> p r n", r=2), src, inv[:, 0:1], 127.0, ALU.mult, ALU.min))
                ch.link(V.tensor_scalar(q[:, p], q[:, p], -128.0, MAGIC, ALU.max, ALU.add))
                if later(k):
                    dve.wait_ge(t_done[p], k)
                V.tensor_scalar(qb[:, p], q[:, p], -MAGIC, None, ALU.add).then_inc(qb_done[p], 1)

            def scaled(k, p):
                ch.begin()
                dve.wait_ge(o_done[p], k + 1)
                if later(k):
                    dve.wait_ge(y_stored[p], 16 * k)
                ch.link(V.scalar_tensor_tensor(y[:, p].rearrange("p r n -> p (r n)"), ps_o[p][:], xs[:, 0:1],
                                               wsc[:].rearrange("p r n -> p (r n)"), ALU.mult, ALU.mult))
                dve.wait_ge(xb_done[p], k + 1)
                V.tensor_tensor(y[:, p], y[:, p], xb[:, p], ALU.add).then_inc(y_done[p], 1)

            pipeline(dve, TP, [(quantize, 0), (scaled, 2)])


def program(nc, a, out, phases=6, dump=None, only=False):
    with ExitStack() as keep:
        c = constants(nc, keep)
        build_constants(nc, c, keep)
        g = lambda pre, names: {m: a[pre + m] for m in names}
        dram = lambda name, shape, d=FP32: nc.dram_tensor(name, shape, d).ap()
        xs = [a["x"]] + [dram(f"x{i}", (NB, S, D)) for i in range(1, 6)] + [out]
        if only:
            xs[phases - 1] = a["x"]
        if phases < 6:
            xs[phases] = out
        on = lambda i: i == phases if only else i <= phases
        if on(1):
            linear_attention(nc, xs[0], xs[1], g("L0_attn_", ("Wq", "bq", "Wk", "bk", "Wv", "bv", "Wu", "bu", "Wo", "bo", "scale")), c)
        if on(2):
            cross_attention(nc, xs[1], a["ctx_1024"], xs[2], g("L0_xattn_", ("Wq", "bq", "Wk", "bk", "Wv", "bv", "Wo", "bo")), c)
        if on(3):
            flat = lambda ap: ap.rearrange("b s n -> (b s) n")
            base, xf, logits = dram("base", (TOK, D)), dram("xf", (TOK, D)), dram("logits", (TOK, NE))
            moe_attention(nc, flat(xs[2]), base, xf, logits,
                          g("L0_ffn_", ("ln1_weight", "ln1_bias", "ln2_weight", "ln2_bias", "qkv_weight", "proj_weight",
                                        "router_weight")), c)
            moe(nc, base, xf, logits, flat(xs[3]), g("L0_ffn_", ("moe_w1", "moe_w2", "ln2_weight", "ln2_bias")), c)
        if on(4):
            gated_recurrence(nc, xs[3], xs[4], g("L1_attn_", ("w_a", "w_i", "w_v", "w_gate", "w_down", "decay_bias", "g_pre", "g_post")), c)
        if on(5):
            linear_cross_attention(nc, xs[4], a["ctx_1024"], xs[5],
                                   g("L1_xattn_", ("Wq", "Wkv", "null_kv", "ln_q_g", "ln_q_b", "ln_out_g", "ln_out_b", "Wout")), c)
        if on(6):
            rows = lambda ap: ap.rearrange("b s n -> (b s) n")
            int8_projection(nc, rows(xs[5]), rows(xs[6]), g("L1_ffn_", ("weight_int8", "weight_scale", "bias")), c)


_INPUT_AS_ROWS = ("L0_attn_Wq", "L0_attn_Wk", "L0_attn_Wv", "L0_attn_Wu", "L0_attn_Wo", "L0_ffn_proj_weight",
                  "L1_attn_w_gate", "L1_attn_w_down", "L1_attn_w_a", "L1_attn_w_i", "L1_attn_w_v", "L1_ffn_weight_int8")


def kernel(**inputs):
    import numpy as np
    import concourse.bacc as bacc
    from concourse.bass_utils import run_bass_kernel_spmd

    nc = bacc.Bacc("TRN2", target_bir_lowering=False, num_devices=1)
    arrays, a = {}, {}
    for name, value in inputs.items():
        value = np.asarray(value)
        if name in _INPUT_AS_ROWS:
            value = value.T
        if name == "L0_ffn_qkv_weight":
            value = value.reshape(8, 4, 16, D).transpose(3, 1, 0, 2).reshape(D, 4 * P)
        value = np.ascontiguousarray(value)
        if value.dtype == np.int8:
            value = value.view(np.int32)
        arrays[name] = value
        a[name] = nc.dram_tensor(name, value.shape, mybir.dt.from_np(value.dtype), kind="ExternalInput").ap()
    out = nc.dram_tensor("out", (NB, S, D), FP32, kind="ExternalOutput").ap()
    program(nc, a, out)
    return run_bass_kernel_spmd(nc, [arrays], core_ids=[0]).results[0]["out"]
```

```python
from contextlib import ExitStack, contextmanager

import concourse.bass as bass
from concourse import mybir

FP32 = mybir.dt.float32
BF16 = mybir.dt.bfloat16
I32 = mybir.dt.int32
I8 = mybir.dt.int8
ALU = mybir.AluOpType
ACT = mybir.ActivationFunctionType
AX = mybir.AxisListType

P = 128
NB, S, D = 32, 112, 256
T = 375
DC = D // P
TC, TN = 3, 125
TOK = NB * S
NT = TOK // P
NE, CAP, F = 8, 1120, 1024
ROWS = NE * CAP


@contextmanager
def semaphores(nc, prefix):
    made = []

    def sem(name):
        made.append(nc.alloc_semaphore(name=prefix + name))
        return made[-1]

    yield sem
    nc.clear_and_free_semaphores(made)
    nc.all_engine_barrier()


def later(k):
    return k >= 1 if isinstance(k, int) else True


def pipeline(eng, n, stages, unroll=2):
    most = max(lag for _, lag in stages)

    def step(k, p):
        for fn, lag in stages:
            q = p - lag
            kk, pp = k + q // unroll, q % unroll
            if isinstance(k, int) and not 0 <= unroll * kk + pp < n:
                continue
            fn(kk, pp)

    first = -(-(most + 2) // unroll)
    last = n // unroll
    for s in range(unroll * min(first, last)):
        step(s // unroll, s % unroll)
    if last > first:
        with eng.Fori(first, last) as k:
            for p in range(unroll):
                step(k, p)
    for s in range(n, n + most):
        step(s // unroll, s % unroll)


class Chain:

    def __init__(self, eng, sem):
        self.eng, self.sem, self.n = eng, sem, 0

    def begin(self):
        if self.n:
            self.eng.sem_clear(self.sem)
        self.n = 0

    def link(self, ins):
        self.n += 1
        ins.then_inc(self.sem, 1)
        self.eng.wait_ge(self.sem, self.n)


def rsqrt(nc, ch, y, v, t, ti):
    ch.link(nc.vector.tensor_scalar(ti, v.bitcast(I32), 1, None, ALU.logical_shift_right))
    ch.link(nc.vector.tensor_scalar(y.bitcast(I32), ti, -1.0, float(0x5F3759DF), ALU.mult, ALU.add))
    for _ in range(3):
        ch.link(nc.vector.scalar_tensor_tensor(t, y, -0.5, y, ALU.mult, ALU.mult))
        ch.link(nc.vector.tensor_tensor(t, t, v, ALU.mult))
        ch.link(nc.vector.scalar_tensor_tensor(y, t, 1.5, y, ALU.add, ALU.mult))


class Norm:

    def __init__(self, nc, sb, name, n, rows, eps):
        self.nc, self.eps, self.rows = nc, eps, rows
        self.st = sb(f"{name}_st", [n, rows, 6])
        self.mv = sb(f"{name}_mv", [n, rows, 2])
        self.ve = sb(f"{name}_ve", [n, rows])
        self.rs = sb(f"{name}_rs", [n, rows])
        self.t = sb(f"{name}_t", [n, rows])
        self.ti = sb(f"{name}_ti", [n, rows], I32)

    def stats(self, ch, src):
        nc = self.nc
        for r in range(self.rows):
            last = nc.vector.bn_stats(self.st[:, r, :], src(r))
        ch.link(last)
        for r in range(self.rows):
            last = nc.vector.bn_aggr(self.mv[:, r, :], self.st[:, r, :])
        ch.link(last)
        self.finish(ch)

    def gather(self, ch, r, src):
        ch.link(self.nc.vector.bn_stats(self.st[:, r, :], src))
        ch.link(self.nc.vector.bn_aggr(self.mv[:, r, :], self.st[:, r, :]))

    def finish(self, ch):
        nc = self.nc
        ch.link(nc.vector.tensor_scalar(self.ve[:], self.mv[:, :, 1], self.eps, None, ALU.add))
        rsqrt(nc, ch, self.rs[:], self.ve[:], self.t[:], self.ti[:])

    def apply(self, r, out, src):
        return self.nc.vector.tensor_scalar(out, src, self.mv[:, r, 0:1], self.rs[:, r:r + 1],
                                            ALU.subtract, ALU.mult)


class TokenRows:

    def __init__(self, nc, sb, name, eps=1e-5, parts=8):
        self.nc, self.parts = nc, parts
        self.x = sb(name + "_x", [S, NB, D])
        self.norm = Norm(nc, sb, name + "_ln", S, NB, eps)
        self.loaded = self.stored = None
        self.have_stats = False

    def stage(self, sem, x_in, x_out):
        self.loaded = [sem(f"x_loaded{i}") for i in range(self.parts)] if x_in is not None else None
        self.stored = sem("x_stored") if x_out is not None else None

    def load(self, eng, x_in):
        per = NB // self.parts
        if not self.loaded:
            return
        for i in range(self.parts):
            eng.dma_start(self.x[:, i * per:(i + 1) * per],
                          x_in[i * per:(i + 1) * per].rearrange("b s n -> s b n")).then_inc(self.loaded[i], 16)

    def stats(self, eng, ch):
        per = NB // self.parts
        if self.have_stats:
            self.have_stats = False
            return

        def row(b):
            if self.loaded and b % per == 0:
                eng.wait_ge(self.loaded[b // per], 16)
            return self.x[:, b]

        self.norm.stats(ch, row)

    def batch(self, b, count=1):
        if count > 1:
            return self.x[:, bass.ds(b, count)]
        return self.x[:, b] if isinstance(b, int) else self.x[:, bass.ds(b, 1)].rearrange("s b n -> s (b n)")

    def normed(self, b, out):
        m = self.norm
        mean = m.mv[:, b, 0:1] if isinstance(b, int) else m.mv[:, bass.ds(b, 1), 0]
        scale = m.rs[:, b:b + 1] if isinstance(b, int) else m.rs[:, bass.ds(b, 1)]
        return self.nc.vector.tensor_scalar(out, self.batch(b), mean, scale, ALU.subtract, ALU.mult)


def constants(nc, keep):
    sb = lambda n, s, d=FP32: keep.enter_context(nc.sbuf_tensor(n, s, d))
    c = {}
    c["ident"] = sb("ident", [P, P])
    c["ones"] = sb("ones", [P, P])
    c["head32"] = sb("head32", [P, 4])
    c["head16"] = sb("head16", [P, 8])
    c["before"] = sb("before", [P, P])
    c["first"] = sb("first", [P, NE])
    c["expert_row"] = sb("expert_row", [P, NE])
    c["ident_bf"] = sb("ident_bf", [P, P], BF16)
    c["hidden_bf"] = sb("hidden_bf", [P, P], BF16)
    c["causal_half"] = sb("causal_half", [P, S])
    return c


class ConstantsMaker:

    def __init__(self, nc, c, g, made):
        self.nc, self.c, self.g, self.made, self.n = nc, c, g, made, 0

    def link(self, ins):
        self.n += 1
        ins.then_inc(self.made, 1)
        self.g.wait_ge(self.made, self.n)

    def select(self, ap, compare, fill, base, step, length, per_partition):
        self.link(self.nc.gpsimd.affine_select(out=ap, in_=ap, compare_op=compare, fill=fill, base=base,
                                               pattern=[[step, length]], channel_multiplier=per_partition))

    def band(self, ap, width, length):
        self.link(self.nc.gpsimd.memset(ap, 1.0))
        self.select(ap, ALU.is_ge, 0.0, 0, -width, length, 1)
        self.select(ap, ALU.is_ge, 0.0, width - 1, width, length, -1)

    def first(self):
        c, memset = self.c, self.nc.gpsimd.memset
        self.link(memset(c["ones"][:], 1.0))
        self.link(memset(c["ident"][:], 0.0))
        self.select(c["ident"][:], ALU.not_equal, 1.0, 0, -1, P, 1)
        self.band(c["head32"][:], 32, 4)
        self.link(memset(c["causal_half"][:], 0.5))
        self.select(c["causal_half"][:], ALU.is_ge, 0.0, 0, 1, S, -1)

    def others(self):
        c, memset, iota = self.c, self.nc.gpsimd.memset, self.nc.gpsimd.iota
        self.link(self.nc.gpsimd.tensor_copy(c["ident_bf"][:], c["ident"][:]))
        self.link(memset(c["before"][:], 1.0))
        self.select(c["before"][:], ALU.is_gt, 0.0, 0, 1, P, -1)
        self.link(iota(c["first"][:], pattern=[[-1, NE]], base=NE, channel_multiplier=0, allow_small_or_imprecise_dtypes=True))
        self.link(iota(c["expert_row"][:], pattern=[[CAP, NE]], base=-ROWS, channel_multiplier=0,
                       allow_small_or_imprecise_dtypes=True))
        self.link(memset(c["hidden_bf"][:], -4e9))
        for d in range(P // 4):
            self.select(c["hidden_bf"][:], ALU.not_equal, 0.0, -4 * d, -1, P, 1)
        self.band(c["head16"][:], 16, 8)


def linear_attention(nc, rows, x_in, x_out, w, c):
    N2 = 2 * S
    UN = NB // 2
    with ExitStack() as own:
        sb = lambda n, s, d=FP32: own.enter_context(nc.sbuf_tensor("la_" + n, s, d))
        pb = lambda n: own.enter_context(nc.psum_tensor("la_ps_" + n, [P, 512], FP32))
        sem = own.enter_context(semaphores(nc, "la_"))
        two = lambda n: [sem(f"{n}{i}") for i in range(2)]

        wt = {m: sb("w" + m, [P, DC, D]) for m in "qkuvo"}
        bias = {m: sb("b" + m, [P, DC]) for m in "qku"}
        half_bu = sb("half_bu", [P, DC])
        scale = sb("scale", [P, DC])
        half_scale = sb("half_scale", [P, DC])
        bvo = {m: sb("bb" + m, [S, 2, D]) for m in "vo"}
        rows.stage(sem, x_in, x_out)
        xn = sb("xn", [S, 2, D])
        xnT = sb("xnT", [P, DC, N2])
        e_q = sb("e_q", [P, DC, N2])
        e_k = sb("e_k", [P, DC, N2])
        th_u = sb("th_u", [P, DC, N2])
        u_b = sb("u_b", [P, DC, N2])
        kT = sb("kT", [P, 2, DC, N2])
        qT = sb("qT", [P, DC, N2])
        qm = sb("qm", [P, 2, DC, 2, 4, S])
        v_b = sb("v_b", [S, 2, D])
        th_v = sb("th_v", [S, 2, D])
        v_s = sb("v_s", [S, 2, 2, D])
        su = sb("su", [P, 2, DC, N2])
        en = sb("en", [S, 2, 4, S])
        oT = sb("oT", [P, DC, N2])
        sq = sb("sq", [P, DC, N2])
        gT = sb("gT", [P, DC, N2])

        ss = sb("ss", [S, 2])
        rr = sb("rr", [S, 2])
        rt = sb("rt", [S, 2])
        rti = sb("rti", [S, 2], I32)

        ps_t, ps_q, ps_k, ps_u, ps_v, ps_o = (pb(m) for m in ("t", "q", "k", "u", "v", "o"))
        ps_e = [pb("e0"), pb("e1")]

        weights, others_made = sem("weights_loaded"), sem("others_made")
        xb_done, xn_done, t_done, xnT_done = sem("xb_done"), sem("xn_done"), sem("t_done"), sem("xnT_done")
        q_done, k_done, u_done, v_done = (sem(m + "_done") for m in "qkuv")
        eq_done, ek_done, tu_done, ub_done, tv_done = (sem(m) for m in ("eq_done", "ek_done", "tu_done", "ub_done", "tv_done"))
        eluq_done, eluk_done, qm_done, vb_done, vs_done, su_done = (sem(m) for m in ("eluq_done", "eluk_done", "qm_done", "vb_done", "vs_done", "su_done"))
        e_done = two("e_done")
        em_done = two("em_done")
        o_done, oT_done, sq_done, g_done, ss_done, ssc_done, y_done, r_done = (
            sem(m) for m in ("o_done", "oT_done", "sq_done", "g_done", "ss_done", "ssc_done", "y_done", "r_done"))
        x2_done = two("x2_done")
        chain = sem("chain")

        block = own.enter_context(nc.Block())

        def item(k, p):
            return 2 * k + p

        def after(k, p, eng, s, per=1, back=1):
            if isinstance(k, int) and item(k, p) < back:
                return
            eng.wait_ge(s, (item(k, p) - back + 1) * per)

        @block.sync
        def _(sp):
            rows.load(sp, x_in)
            for m in "qkuvo":
                sp.dma_start(wt[m][:], w["W" + m].rearrange("(c p) n -> p c n", p=P)).then_inc(weights, 16)
            for m in "qku":
                sp.dma_start(bias[m][:], w["b" + m].rearrange("(c p) -> p c", p=P),
                             allow_slow_non_contiguous=True).then_inc(weights, 16)
            sp.dma_start(scale[:], w["scale"].rearrange("(c p) -> p c", p=P),
                             allow_slow_non_contiguous=True).then_inc(weights, 16)
            for m in "vo":
                for b in range(2):
                    sp.dma_start(bvo[m][:, b], w["b" + m].rearrange("(a n) -> a n", a=1).to_broadcast([S, D])).then_inc(weights, 16)



            def store(k, p):
                sp.wait_ge(x2_done[p], k + 1)
                dst = x_out[bass.ds(2 * item(k, p), 2)] if not isinstance(k, int) else x_out[2 * item(k, p):2 * item(k, p) + 2]
                sp.dma_start(dst.rearrange("b s n -> s b n"), rows.batch(2 * item(k, p), 2)).then_inc(rows.stored, 16)

            if x_out is not None:
                pipeline(sp, UN, [(store, 2)])
                sp.wait_ge(rows.stored, 16 * UN)

        @block.gpsimd
        def _(g):
            ConstantsMaker(nc, c, g, others_made).others()
            g.wait_ge(weights, 16 * 13)

            def biased(k, p):
                g.wait_ge(xn_done, item(k, p) + 1)
                x = rows.batch(2 * item(k, p), 2)
                nc.gpsimd.tensor_tensor(x, x, bvo["o"][:], ALU.add).then_inc(xb_done, 1)

            pipeline(g, UN, [(biased, 0)])

        @block.vector
        def _(dve):
            ch = Chain(dve, chain)
            rows.stats(dve, ch)
            dve.wait_ge(weights, 16 * 13)
            ch.link(nc.vector.tensor_scalar(half_bu[:], bias["u"][:], 0.5, None, ALU.mult))
            ch.link(nc.vector.tensor_scalar(half_scale[:], scale[:], 0.5, None, ALU.mult))



            def norm(k, p):
                after(k, p, dve, t_done)
                rows.normed(2 * item(k, p), xn[:, 0])
                rows.normed(2 * item(k, p) + 1, xn[:, 1]).then_inc(xn_done, 1)

            def elu(k, p, dst, e, done, ps, b, elu_done):
                dve.wait_ge(done, item(k, p) + 1)
                ch.link(nc.vector.tensor_scalar(e[:], e[:], 1.0, -1.0, ALU.min, ALU.add))
                for i in range(DC):
                    last = nc.vector.scalar_tensor_tensor(dst[:, i], ps[:, i * N2:(i + 1) * N2], b[:, i:i + 1],
                                                          e[:, i], ALU.add, ALU.max)
                last.then_inc(elu_done, 1)

            def elu_k(k, p):
                ch.begin()
                after(k, p, dve, e_done[0], 2, 2)
                after(k, p, dve, e_done[1], 2, 2)
                elu(k, p, kT[:, p], e_k, ek_done, ps_k, bias["k"], eluk_done)

            def elu_q(k, p):
                ch.begin()
                after(k, p, dve, qm_done)
                elu(k, p, qT, e_q, eq_done, ps_q, bias["q"], eluq_done)

            def masked_q(k, p):
                after(k, p, dve, e_done[0], 2, 2)
                after(k, p, dve, e_done[1], 2, 2)
                dve.wait_ge(eluq_done, item(k, p) + 1)
                for j in range(4):
                    for i in range(DC):
                        last = nc.vector.tensor_scalar(qm[:, p, i, :, j, :], qT[:, i].rearrange("p (b n) -> p b n", b=2),
                                                       c["head32"][:, j:j + 1], None, ALU.mult)
                last.then_inc(qm_done, 1)
            def products(k, p):
                dve.wait_ge(v_done, item(k, p) + 1)
                after(k, p, dve, tv_done)
                nc.vector.tensor_tensor(v_b[:].rearrange("p b n -> p (b n)"), ps_v[0:S, :],
                                        bvo["v"][:].rearrange("p b n -> p (b n)"), ALU.add).then_inc(vb_done, 1)
                dve.wait_ge(tu_done, item(k, p) + 1)
                dve.wait_ge(ub_done, item(k, p) + 1)
                after(k, p, dve, g_done, 1, 2)
                nc.vector.scalar_tensor_tensor(su[:, p], th_u[:], 1.0, u_b[:], ALU.add, ALU.mult).then_inc(su_done, 1)
                dve.wait_ge(tv_done, item(k, p) + 1)
                dve.wait_ge(vb_done, item(k, p) + 1)
                after(k, p, dve, r_done, 4, 2)
                nc.vector.scalar_tensor_tensor(v_s[:, p], th_v[:], 1.0, v_b[:], ALU.add, ALU.mult).then_inc(vs_done, 1)

            def mask(b):
                def fn(k, p):
                    for i in range(DC):
                        dve.wait_ge(e_done[i], 2 * item(k, p) + b + 1)
                        if not (isinstance(k, int) and item(k, p) == 0 and b == 0):
                            dve.wait_ge(r_done, 4 * item(k, p) + 2 * b - 2 + i + 1)
                        nc.vector.tensor_tensor(en[:, i], ps_e[i][0:S, 0:4 * S].rearrange("p (j n) -> p j n", j=4),
                                                c["causal_half"][0:S].unsqueeze(1).to_broadcast([S, 4, S]),
                                                ALU.mult).then_inc(em_done[i], 1)
                return fn

            def gate(k, p):
                dve.wait_ge(oT_done, item(k, p) + 1)
                dve.wait_ge(su_done, item(k, p) + 1)
                after(k, p, dve, y_done)
                for i in range(DC):
                    last = nc.vector.scalar_tensor_tensor(gT[:, i], su[:, p, i], half_scale[:, i:i + 1], oT[:, i],
                                                          ALU.mult, ALU.mult)
                last.then_inc(g_done, 1)

            def root(k, p):
                ch.begin()
                if later(k) or p > 0:
                    dve.wait_ge(x2_done[1 - p], k + p)
                dve.wait_ge(ss_done, item(k, p) + 1)
                ch.link(nc.vector.tensor_copy(ss[:], ps_o[0:S, 2 * N2:2 * N2 + 2]))
                rsqrt(nc, ch, rr[:], ss[:], rt[:], rti[:])
                ch.link(nc.vector.tensor_tensor(rr[:], rr[:], ss[:], ALU.mult))
                ch.link(nc.vector.tensor_scalar(rr[:], rr[:], 1.0 / 16, 1e-8, ALU.mult, ALU.add))
                nc.vector.reciprocal(rr[:], rr[:]).then_inc(ssc_done, 1)

            def residual(k, p):
                dve.wait_ge(y_done, item(k, p) + 1)
                dve.wait_ge(ssc_done, item(k, p) + 1)
                dve.wait_ge(xb_done, item(k, p) + 1)
                for b in range(2):
                    x = rows.batch(2 * item(k, p) + b)
                    last = nc.vector.scalar_tensor_tensor(x, ps_v[0:S, b * D:(b + 1) * D], rr[:, b:b + 1],
                                                          x, ALU.mult, ALU.add)
                last.then_inc(x2_done[p], 1)

            pipeline(dve, UN, [(norm, 0), (mask(0), 1), (mask(1), 1), (elu_q, 0), (masked_q, 0), (gate, 1), (root, 1),
                               (residual, 1), (elu_k, 0), (products, 0)])

        @block.tensor
        def _(pe):
            pe.wait_ge(weights, 16 * 13)

            def transposed(k, p):
                pe.wait_ge(xn_done, item(k, p) + 1)
                after(k, p, pe, xnT_done)
                for i in range(DC):
                    for b in range(2):
                        last = nc.tensor.transpose(ps_t[:, i * N2 + b * S:i * N2 + (b + 1) * S],
                                                   xn[:, b, i * P:(i + 1) * P], c["ident"][0:S, 0:S])
                last.then_inc(t_done, 1)

            def project(m, ps, free, done):
                def fn(k, p):
                    pe.wait_ge(xnT_done, item(k, p) + 1)
                    after(k, p, pe, free)
                    for o in range(DC):
                        for i in range(DC):
                            last = nc.tensor.matmul(ps[:, o * N2:(o + 1) * N2], wt[m][:, i, o * P:(o + 1) * P],
                                                    xnT[:, i], start=i == 0, stop=i == DC - 1)
                    last.then_inc(done, 1)
                return fn

            def values(k, p):
                pe.wait_ge(xnT_done, item(k, p) + 1)
                if not (isinstance(k, int) and item(k, p) == 0):
                    pe.wait_ge(x2_done[1 - p], k + p)
                for b in range(2):
                    for i in range(DC):
                        last = nc.tensor.matmul(ps_v[0:S, b * D:(b + 1) * D], xnT[:, i, b * S:(b + 1) * S],
                                                wt["v"][:, i], start=i == 0, stop=i == DC - 1)
                last.then_inc(v_done, 1)

            def energy(b):
                def fn(k, p):
                    pe.wait_ge(eluk_done, item(k, p) + 1)
                    pe.wait_ge(qm_done, item(k, p) + 1)
                    for i in range(DC):
                        if not (isinstance(k, int) and item(k, p) == 0 and b == 0):
                            pe.wait_ge(em_done[i], 2 * item(k, p) + b)
                        nc.tensor.matmul(ps_e[i][0:S, 0:4 * S], kT[:, p, i, b * S:(b + 1) * S],
                                         qm[:, p, i, b].rearrange("p j n -> p (j n)"),
                                         start=True, stop=True).then_inc(e_done[i], 1)
                return fn

            def weighted(b):
                def fn(k, p):
                    pe.wait_ge(vs_done, item(k, p) + 1)
                    after(k, p, pe, oT_done)
                    after(k, p, pe, ssc_done)
                    for i in range(DC):
                        pe.wait_ge(em_done[i], 2 * item(k, p) + b + 1)
                        for j in range(4):
                            last = nc.tensor.matmul(ps_o[32 * j:32 * j + 32, i * N2 + b * S:i * N2 + (b + 1) * S],
                                                    v_s[:, p, b, i * P + 32 * j:i * P + 32 * j + 32], en[:, i, j],
                                                    start=True, stop=True, skip_group_check=True)
                        last.then_inc(r_done, 1)
                return fn

            def output(k, p):
                pe.wait_ge(sq_done, item(k, p) + 1)
                for b in range(2):
                    for i in range(DC):
                        last = nc.tensor.matmul(ps_o[0:S, 2 * N2 + b:2 * N2 + b + 1], sq[:, i, b * S:(b + 1) * S],
                                                c["ones"][:, 0:1], start=i == 0, stop=i == DC - 1,
                                                skip_group_check=True)
                last.then_inc(ss_done, 1)
                pe.wait_ge(g_done, item(k, p) + 1)
                for b in range(2):
                    for i in range(DC):
                        last = nc.tensor.matmul(ps_v[0:S, b * D:(b + 1) * D], gT[:, i, b * S:(b + 1) * S],
                                                wt["o"][:, i], start=i == 0, stop=i == DC - 1)
                last.then_inc(y_done, 1)

            project_q, project_k, project_u = (project("q", ps_q, eluq_done, q_done), project("k", ps_k, eluk_done, k_done),
                                               project("u", ps_u, ub_done, u_done))
            pipeline(pe, UN, [(energy(0), 1), (transposed, 0), (weighted(0), 1), (energy(1), 1), (project_q, 0),
                              (weighted(1), 1), (project_k, 0), (project_u, 0), (output, 1), (values, 0)])

        @block.scalar
        def _(act):
            def copy_t(k, p):
                act.wait_ge(t_done, item(k, p) + 1)
                after(k, p, act, v_done)
                nc.scalar.activation(xnT[:].rearrange("p c n -> p (c n)"), ps_t[:, 0:2 * N2], ACT.Copy).then_inc(xnT_done, 1)

            def exp(e, ps, b, got, done, free):
                def fn(k, p):
                    act.wait_ge(got, item(k, p) + 1)
                    after(k, p, act, free)
                    for i in range(DC):
                        last = nc.scalar.activation(e[:, i], ps[:, i * N2:(i + 1) * N2], ACT.Exp, bias=b[:, i:i + 1])
                    last.then_inc(done, 1)
                return fn

            def gates(k, p):
                act.wait_ge(u_done, item(k, p) + 1)
                after(k, p, act, su_done)
                for i in range(DC):
                    last = nc.scalar.activation(th_u[:, i], ps_u[:, i * N2:(i + 1) * N2], ACT.Tanh,
                                                bias=half_bu[:, i:i + 1], scale=0.5)
                last.then_inc(tu_done, 1)
                for i in range(DC):
                    last = nc.scalar.activation(u_b[:, i], ps_u[:, i * N2:(i + 1) * N2], ACT.Identity, bias=bias["u"][:, i:i + 1])
                last.then_inc(ub_done, 1)
            def values(k, p):
                act.wait_ge(vb_done, item(k, p) + 1)
                after(k, p, act, vs_done)
                nc.scalar.activation(th_v[:], v_b[:], ACT.Tanh, scale=0.5).then_inc(tv_done, 1)

            def squares(k, p):
                act.wait_ge(r_done, 4 * item(k, p) + 4)
                after(k, p, act, g_done)
                nc.scalar.activation(oT[:].rearrange("p c n -> p (c n)"), ps_o[:, 0:2 * N2], ACT.Copy).then_inc(oT_done, 1)
                act.wait_ge(oT_done, item(k, p) + 1)
                after(k, p, act, ss_done)
                nc.scalar.activation(sq[:], oT[:], ACT.Square).then_inc(sq_done, 1)

            act.wait_ge(weights, 16 * 13)
            exp_q = exp(e_q, ps_q, bias["q"], q_done, eq_done, eluq_done)
            exp_k = exp(e_k, ps_k, bias["k"], k_done, ek_done, eluk_done)
            pipeline(act, UN, [(copy_t, 0), (exp_q, 0), (squares, 1), (exp_k, 0), (gates, 0), (values, 0)])


def cross_attention(nc, rows, x_in, ctx, x_out, w, c):
    H, DH = 16, 16
    HC = H // DC
    HS = H * S
    W4 = 4 * S
    with ExitStack() as own:
        sb = lambda n, s, d=FP32: own.enter_context(nc.sbuf_tensor("ca_" + n, s, d))
        sem = own.enter_context(semaphores(nc, "ca_"))
        two = lambda n: [sem(f"{n}{i}") for i in range(2)]
        per_chunk = lambda n: [sem(f"{n}{i}") for i in range(TC)]

        wt = {m: sb("w" + m, [P, DC, D]) for m in "qkvo"}
        bias = {m: sb("b" + m, [P, DC]) for m in "qk"}
        bv = sb("bv", [TN, D])
        bo = sb("bo", [S, D])

        ct = sb("ct", [TN, 2, TC, D])
        xn = sb("xn", [S, D])
        xcT = sb("xcT", [P, DC, T + S])
        kT = sb("kT", [P, 2, DC, T])
        qb = sb("qb", [P, DC, S])
        qm = sb("qm", [P, 2, DC, HC, S])
        vb = sb("vb", [TN, 2, TC, D])
        vm = sb("vm", [TN, TC, H // 2, 64])
        es = sb("es", [TN, TC, HS])
        mx = sb("mx", [TN, TC, H])
        rs = sb("rs", [TN, TC, H])
        es_sum = sb("es_sum", [TN, H])

        aT = sb("aT", [P, DC, S])
        rows.stage(sem, x_in, x_out)
        bank_a, bank_b, bank_c, bank_d = (own.enter_context(nc.psum_tensor("ca_bank_" + m, [P, 512], FP32)) for m in "abcd")
        ps_s = own.enter_context(nc.psum_tensor("ca_scores", [P, 4, 512], FP32))

        weights = sem("weights_loaded")
        c_ready = two("c_ready")
        vm_zero = sem("vm_zero")
        xn_done, t_done, xcT_done, kq_done, kT_done, qm_done, v_done, vb_done, qb_done = (
            sem(m) for m in ("xn_done", "t_done", "xcT_done", "kq_done", "kT_done", "qm_done", "v_done", "vb_done", "qb_done"))
        s_done, max_done, sub_done = (two(m) for m in ("s_done", "max_done", "sub_done"))
        exp_done, sum_done, vn_done, av_done = (per_chunk(m) for m in ("exp_done", "sum_done", "vn_done", "av_done"))
        aT_done, o_done, xb_done, y_done = (sem(m) for m in ("aT_done", "o_done", "xb_done", "y_done"))
        chain = sem("chain")

        def n(k, p):
            return 2 * k + p

        def after(k, p, eng, s):
            if not (isinstance(k, int) and n(k, p) == 0):
                eng.wait_ge(s, n(k, p))

        block = own.enter_context(nc.Block())

        @block.sync
        def _(sp):
            rows.load(sp, x_in)
            for m in "qkvo":
                sp.dma_start(wt[m][:], w["W" + m].rearrange("(c p) n -> p c n", p=P)).then_inc(weights, 16)
            for m in "qk":
                sp.dma_start(bias[m][:], w["b" + m].rearrange("(c p) -> p c", p=P),
                             allow_slow_non_contiguous=True).then_inc(weights, 16)
            sp.dma_start(bv[:], w["bv"].rearrange("(a n) -> a n", a=1).to_broadcast([TN, D])).then_inc(weights, 16)
            sp.dma_start(bo[:], w["bo"].rearrange("(a n) -> a n", a=1).to_broadcast([S, D])).then_inc(weights, 16)

            def load(k, p):
                if later(k):
                    sp.wait_ge(t_done, n(k, p) - 1)
                sp.dma_start(ct[:, p], ctx[n(k, p)].rearrange("(c t) n -> t c n", c=TC)).then_inc(c_ready[p], 16)



            def store(k, p):
                sp.wait_ge(y_done, n(k, p) + 1)
                sp.dma_start(x_out[n(k, p)], rows.batch(n(k, p))).then_inc(rows.stored, 16)

            pipeline(sp, NB, [(load, 0), (store, 3)])
            sp.wait_ge(rows.stored, 16 * NB)

        @block.vector
        def _(dve):
            ch = Chain(dve, chain)
            rows.stats(dve, ch)

            def norm(k, p):
                after(k, p, dve, t_done)
                rows.normed(n(k, p), xn[:]).then_inc(xn_done, 1)

            def values(k, p):
                dve.wait_ge(v_done, n(k, p) + 1)
                if later(k):
                    dve.wait_ge(vn_done[TC - 1], n(k, p) - 1)
                nc.vector.tensor_tensor(vb[:, p, 0:2], bank_b[0:TN, :].rearrange("t (c n) -> t c n", c=2),
                                        bv[:].unsqueeze(1).to_broadcast([TN, 2, D]), ALU.add)
                nc.vector.tensor_tensor(vb[:, p, 2], bank_c[0:TN, 0:D], bv[:], ALU.add).then_inc(vb_done, 1)

            def shifted(t):
                def fn(k, p):
                    for i in range(DC):
                        scores = ps_s[0:TN, 2 * i:2 * i + 2, 0:W4].rearrange("t b (h n) -> t b h n", h=4)
                        top = mx[:, t, HC * i:HC * (i + 1)].rearrange("t (b h) -> t b h", b=2)
                        dve.wait_ge(s_done[i], TC * n(k, p) + t + 1)
                        nc.vector.tensor_reduce(top, scores, AX.X, ALU.max).then_inc(max_done[i], 1)
                        dve.wait_ge(max_done[i], TC * n(k, p) + t + 1)
                        after(k, p, dve, av_done[t])
                        nc.vector.tensor_tensor(es[:, t, i * HC * S:(i + 1) * HC * S].rearrange("t (b h n) -> t b h n", b=2, h=4),
                                                scores, top.unsqueeze(3).to_broadcast([TN, 2, 4, S]),
                                                ALU.subtract).then_inc(sub_done[i], 1)
                return fn

            def summed(t):
                def fn(k, p):
                    ch.begin()
                    dve.wait_ge(exp_done[t], n(k, p) + 1)
                    after(k, p, dve, vn_done[t])
                    if t < TC - 1:
                        ch.link(nc.vector.tensor_reduce(rs[:, t], es[:, t].rearrange("t (h n) -> t h n", h=H), AX.X, ALU.add))
                        nc.vector.reciprocal(rs[:, t], rs[:, t]).then_inc(sum_done[t], 1)
                    else:
                        nc.vector.reciprocal(rs[:, t], es_sum[:]).then_inc(sum_done[t], 1)
                return fn

            def residual(k, p):
                dve.wait_ge(o_done, n(k, p) + 1)
                dve.wait_ge(xb_done, n(k, p) + 1)
                nc.vector.tensor_tensor(rows.batch(n(k, p)), bank_d[0:S, D:2 * D], rows.batch(n(k, p)), ALU.add).then_inc(y_done, 1)

            pipeline(dve, NB, [(shifted(0), 2), (summed(2), 3), (shifted(1), 2), (summed(0), 2), (values, 1), (norm, 0),
                               (summed(1), 2), (residual, 3), (shifted(2), 2)])

        @block.tensor
        def _(pe):
            pe.wait_ge(weights, 16 * 8)

            def transposed(k, p):
                pe.wait_ge(c_ready[p], 16 * (k + 1))
                after(k, p, pe, kT_done)
                after(k, p, pe, vb_done)
                for i, bank in enumerate((bank_a, bank_b)):
                    for t in range(TC):
                        nc.tensor.transpose(bank[:, t * TN:(t + 1) * TN], ct[:, p, t, i * P:(i + 1) * P],
                                            c["ident"][0:TN, 0:TN])
                pe.wait_ge(xn_done, n(k, p) + 1)
                for i, bank in enumerate((bank_a, bank_b)):
                    last = nc.tensor.transpose(bank[:, T:T + S], xn[:, i * P:(i + 1) * P], c["ident"][0:S, 0:S])
                last.then_inc(t_done, 1)

            def project(k, p):
                pe.wait_ge(xcT_done, n(k, p) + 1)
                for o, bank in enumerate((bank_c, bank_a)):
                    for m, lo, hi in (("k", 0, T), ("q", T, T + S)):
                        for i in range(DC):
                            last = nc.tensor.matmul(bank[:, lo:hi], wt[m][:, i, o * P:(o + 1) * P], xcT[:, i, lo:hi],
                                                    start=i == 0, stop=i == DC - 1)
                last.then_inc(kq_done, 1)
                for t in range(2):
                    for i in range(DC):
                        nc.tensor.matmul(bank_b[0:TN, t * D:(t + 1) * D], xcT[:, i, t * TN:(t + 1) * TN], wt["v"][:, i],
                                         start=i == 0, stop=i == DC - 1)
                pe.wait_ge(kT_done, n(k, p) + 1)
                pe.wait_ge(qb_done, n(k, p) + 1)
                for i in range(DC):
                    last = nc.tensor.matmul(bank_c[0:TN, 0:D], xcT[:, i, 2 * TN:3 * TN], wt["v"][:, i],
                                            start=i == 0, stop=i == DC - 1)
                last.then_inc(v_done, 1)

            def scores(t):
                def fn(k, p):
                    if t == 0:
                        pe.wait_ge(kT_done, n(k, p) + 1)
                    for i in range(DC):
                        if t == 0:
                            pe.wait_ge(qm_done, DC * n(k, p) + i + 1)
                        if t > 0 or not (isinstance(k, int) and n(k, p) == 0):
                            pe.wait_ge(sub_done[i], TC * n(k, p) + t)
                        for h in range(2):
                            last = nc.tensor.matmul(ps_s[0:TN, 2 * i + h, 0:W4], kT[:, p, i, t * TN:(t + 1) * TN],
                                                    qm[:, p, i, 4 * h:4 * h + 4].rearrange("p h n -> p (h n)"),
                                                    start=True, stop=True)
                        last.then_inc(s_done[i], 1)
                return fn

            def weighted(t):
                def fn(k, p):
                    if t == 0:
                        after(k, p, pe, y_done)
                    pe.wait_ge(vn_done[t], n(k, p) + 1)
                    for i in range(DC):
                        for j in range(4):
                            for e in range(2):
                                m = 4 * i + j
                                last = nc.tensor.matmul(bank_d[32 * j:32 * j + 32, i * S:(i + 1) * S],
                                                        vm[:, t, m, 32 * e:32 * e + 32],
                                                        es[:, t, (2 * m + e) * S:(2 * m + e + 1) * S],
                                                        start=t == 0 and i == 0 and e == 0, stop=t == TC - 1 and e == 1,
                                                        skip_group_check=True)
                    last.then_inc(av_done[t], 1)
                return fn

            def output(k, p):
                pe.wait_ge(aT_done, n(k, p) + 1)
                for i in range(DC):
                    last = nc.tensor.matmul(bank_d[0:S, D:2 * D], aT[:, i], wt["o"][:, i], start=i == 0, stop=i == DC - 1)
                last.then_inc(o_done, 1)

            pipeline(pe, NB, [(scores(0), 2), (transposed, 1), (weighted(1), 3), (scores(1), 2), (project, 1),
                              (weighted(2), 3), (output, 3), (scores(2), 2), (weighted(0), 2)])

        @block.scalar
        def _(act):
            act.wait_ge(weights, 16 * 8)

            def exps(t):
                def fn(k, p):
                    for i in range(DC):
                        half = es[:, t, i * HC * S:(i + 1) * HC * S]
                        act.wait_ge(sub_done[i], TC * n(k, p) + t + 1)
                        if t < TC - 1:
                            last = nc.scalar.activation(half, half, ACT.Exp, scale=DH ** -0.5)
                            continue
                        if i == 0:
                            after(k, p, act, sum_done[t])
                        for h in range(HC * i, HC * (i + 1)):
                            head = es[:, t, h * S:(h + 1) * S]
                            last = nc.scalar.activation(head, head, ACT.Exp, scale=DH ** -0.5, accum_out=es_sum[:, h:h + 1])
                    last.then_inc(exp_done[t], 1)
                return fn

            def copy_a(k, p):
                act.wait_ge(av_done[TC - 1], n(k, p) + 1)
                after(k, p, act, o_done)
                nc.scalar.activation(aT[:].rearrange("p c n -> p (c n)"), bank_d[:, 0:DC * S], ACT.Copy).then_inc(aT_done, 1)

            def copy_t(k, p):
                act.wait_ge(t_done, n(k, p) + 1)
                after(k, p, act, v_done)
                for i, bank in enumerate((bank_a, bank_b)):
                    last = nc.scalar.activation(xcT[:, i], bank[:, 0:T + S], ACT.Copy)
                last.then_inc(xcT_done, 1)

            def copy_kq(k, p):
                act.wait_ge(kq_done, n(k, p) + 1)
                if not (isinstance(k, int) and n(k, p) == 0):
                    act.wait_ge(qm_done, DC * n(k, p))
                for o, bank in enumerate((bank_c, bank_a)):
                    last = nc.scalar.activation(qb[:, o], bank[:, T:T + S], ACT.Identity, bias=bias["q"][:, o:o + 1])
                last.then_inc(qb_done, 1)
                if later(k):
                    act.wait_ge(s_done[1], TC * (n(k, p) - 1))
                for o, bank in enumerate((bank_c, bank_a)):
                    last = nc.scalar.activation(kT[:, p, o], bank[:, 0:T], ACT.Identity, bias=bias["k"][:, o:o + 1])
                last.then_inc(kT_done, 1)

            pipeline(act, NB, [(exps(0), 2), (copy_t, 1), (copy_kq, 1), (exps(1), 2), (copy_a, 3), (exps(2), 2)])

        @block.gpsimd
        def _(g):
            nc.gpsimd.memset(vm[:], 0.0).then_inc(vm_zero, 1)
            g.wait_ge(vm_zero, 1)
            g.wait_ge(weights, 16 * 8)

            def mask_q(k, p):
                g.wait_ge(qb_done, n(k, p) + 1)
                if later(k):
                    g.wait_ge(s_done[1], TC * (n(k, p) - 1))
                for i in range(DC):
                    nc.gpsimd.tensor_tensor(qm[:, p, i], qb[:, i].unsqueeze(1).to_broadcast([P, HC, S]),
                                            c["head16"][:].unsqueeze(2).to_broadcast([P, HC, S]),
                                            ALU.mult).then_inc(qm_done, 1)

            def biased(k, p):
                g.wait_ge(xn_done, n(k, p) + 1)
                nc.gpsimd.tensor_tensor(rows.batch(n(k, p)), rows.batch(n(k, p)), bo[:], ALU.add).then_inc(xb_done, 1)

            def normalized(t):
                def fn(k, p):
                    g.wait_ge(sum_done[t], n(k, p) + 1)
                    g.wait_ge(vb_done, n(k, p) + 1)
                    after(k, p, g, av_done[t])
                    for e in range(2):
                        pair = lambda a: a.rearrange("t (m e n) -> t m e n", e=2, n=DH)[:, :, e]
                        last = nc.gpsimd.tensor_tensor(
                            vm[:, t, :, 48 * e:48 * e + DH], pair(vb[:, p, t]),
                            rs[:, t].rearrange("t (m e) -> t m e", e=2)[:, :, e].unsqueeze(2).to_broadcast([TN, H // 2, DH]),
                            ALU.mult)
                    last.then_inc(vn_done[t], 1)
                return fn

            pipeline(g, NB, [(normalized(2), 3), (normalized(0), 2), (mask_q, 1), (biased, 2), (normalized(1), 2)])


def moe_attention(nc, x_in, base, xf, logits, xin, yout, w, c):
    G, DH = 8, 16
    with ExitStack() as own:
        sb = lambda n, s, d=FP32: own.enter_context(nc.sbuf_tensor("ma_" + n, s, d))
        pb = lambda n, s: own.enter_context(nc.psum_tensor("ma_ps_" + n, s, FP32))
        sem = own.enter_context(semaphores(nc, "ma_"))
        two = lambda n: [sem(f"{n}{i}") for i in range(2)]

        wqkv = sb("wqkv", [P, DC, 4, P])
        zeros = sb("zeros", [P, 10 * D])
        clears = ROWS * D // (P * 10 * D)
        wp = sb("wp", [P, DC, D])
        wr = sb("wr", [P, DC, NE])
        aff = {m: sb(m, [P, DC]) for m in ("ln1_weight", "ln1_bias", "ln2_weight", "ln2_bias")}
        x = sb("x", [P, NT, D])
        hid = sb("hid", [P, 4, D])
        xn = sb("xn", [P, D])
        lnT = sb("lnT", [P, DC, P])
        qT = sb("qT", [P, 2, 2, P])
        kb = sb("kb", [P, P])
        km = sb("km", [P, 2, G, P])
        vz = sb("vz", [P, 4, G, 3 * DH])
        es = sb("es", [P, 2, G, P])
        en = sb("en", [P, 2, G, P])
        mx = sb("mx", [P, 2, G])
        rs = sb("rs", [P, 2, G])
        pt = sb("pt", [P, 2, G, P])
        aT = sb("aT", [P, DC, P])
        ha = sb("ha", [P, D])

        xo = sb("xo", [P, 2, D])
        xoT = sb("xoT", [P, DC, P])
        lg = sb("lg", [P, 2, NE])
        n1 = Norm(nc, sb, "n1", P, NT, 1e-5)
        n3 = Norm(nc, sb, "n3", P, 1, 1e-5)
        v2 = sb("v2", [P, NT])
        rs2 = sb("rs2", [P, NT])
        ps_t = pb("t", [P, 512])
        ps_l = pb("l", [P, 512])
        ps_qkv = pb("qkv", [P, 512])
        ps_s = [pb(f"s{r}", [P, 2, 512]) for r in range(2)]
        ps_o = pb("o", [P, 512])

        weights = sem("weights_loaded")
        x_loaded = [sem(f"x_loaded{i}") for i in range(7)]
        z_made, cleared = sem("z_made"), sem("cleared")
        f_stored, l_stored, b_stored = two("f_stored"), two("l_stored"), sem("b_stored")
        s_done, max_done, sub_done, exp_done, sum_done, pn_done, p_done, pt_done = (
            two(m) for m in ("s_done", "max_done", "sub_done", "exp_done", "sum_done", "pn_done", "p_done", "pt_done"))
        hid_done, vz_zero, xn_done, t_done, lnT_done, qkv_done, q_done, kb_done, km_done, vz_done = (
            sem(m) for m in ("hid_done", "vz_zero", "xn_done", "t_done", "lnT_done", "qkv_done", "q_done", "kb_done", "km_done", "vz_done"))
        av_done, aT_done, proj_done, ha_done, bs_done, xo_done, t2_done, xoT_done, r_done, lg_done = (
            sem(m) for m in ("av_done", "aT_done", "proj_done", "ha_done", "bs_done", "xo_done", "t2_done", "xoT_done", "r_done", "lg_done"))
        chain = sem("chain")
        chain2 = sem("chain2")
        tiles = lambda a: a.rearrange("(p t) n -> t p n", t=NT)
        NW = 16 * 7

        def n(k, p):
            return 4 * k + p

        def turn(k, p):
            return 2 * k + p // 2

        def after(k, p, eng, s, back=1):
            if not (isinstance(k, int) and n(k, p) < back):
                eng.wait_ge(s, n(k, p) - back + 1)

        def slot_free(k, p, eng, s):
            if not (isinstance(k, int) and n(k, p) < 2):
                eng.wait_ge(s[p % 2], 16 * turn(k, p))

        def tile(k, p):
            i = n(k, p)
            return x[:, i] if isinstance(i, int) else x[:, bass.ds(i, 1)].rearrange("p a n -> p (a n)")

        block = own.enter_context(nc.Block())

        @block.sync
        def _(sp):
            for i in range(7):
                sp.dma_start(x[:, 4 * i:4 * i + 4], x_in.rearrange("(p t) n -> p t n", t=NT)[:, 4 * i:4 * i + 4]).then_inc(x_loaded[i], 16)
            sp.dma_start(wqkv[:], w["qkv_weight"].rearrange("(c p) (f n) -> p c f n", p=P, f=4)).then_inc(weights, 16)
            sp.dma_start(wp[:], w["proj_weight"].rearrange("(c p) n -> p c n", p=P)).then_inc(weights, 16)
            sp.dma_start(wr[:], w["router_weight"].rearrange("(c p) n -> p c n", p=P)).then_inc(weights, 16)
            for m in aff:
                sp.dma_start(aff[m][:], w[m].rearrange("(c p) -> p c", p=P), allow_slow_non_contiguous=True).then_inc(weights, 16)
            sp.wait_ge(z_made, 1)
            for i in range(clears):
                sp.dma_start(xin.rearrange("(a p r) n -> a p (r n)", p=P, a=clears)[i], zeros[:]).then_inc(cleared, 16)
            sp.dma_start(yout[ROWS:ROWS + 1], zeros[0:1, 0:D]).then_inc(cleared, 16)

            def store_b(k, p):
                sp.wait_ge(ha_done, n(k, p) + 1)
                sp.dma_start(tiles(base)[n(k, p)], tile(k, p)).then_inc(b_stored, 16)

            def store_f(k, p):
                sp.wait_ge(xo_done, n(k, p) + 1)
                sp.dma_start(tiles(xf)[n(k, p)], xo[:, p % 2]).then_inc(f_stored[p % 2], 16)
                sp.wait_ge(lg_done, n(k, p) + 1)
                sp.dma_start(tiles(logits)[n(k, p)], lg[:, p % 2]).then_inc(l_stored[p % 2], 16)

            pipeline(sp, NT, [(store_b, 4), (store_f, 5)], 4)
            sp.wait_ge(b_stored, 16 * NT)
            sp.wait_ge(cleared, 16 * (clears + 1))
            for s in (*f_stored, *l_stored):
                sp.wait_ge(s, 16 * (NT // 2))

        @block.vector
        def _(dve):
            ch, ch2 = Chain(dve, chain), Chain(dve, chain2)

            def loaded_tile(t):
                if t % 4 == 0:
                    dve.wait_ge(x_loaded[t // 4], 16)
                return x[:, t]

            n1.stats(ch, loaded_tile)
            ch.link(nc.vector.tensor_tensor(v2[:], n1.rs[:], n1.rs[:], ALU.mult))
            ch.link(nc.vector.tensor_tensor(v2[:], v2[:], n1.mv[:, :, 1], ALU.mult))
            ch.link(nc.vector.tensor_scalar(v2[:], v2[:], 1e-5, None, ALU.add))
            rsqrt(nc, ch, rs2[:], v2[:], n1.t[:], n1.ti[:])

            def norms(k, p):
                i = n(k, p)
                col = lambda t: t[:, i:i + 1] if isinstance(i, int) else t[:, bass.ds(i, 1)]
                mean = n1.mv[:, i, 0:1] if isinstance(i, int) else n1.mv[:, bass.ds(i, 1), 0]
                after(k, p, dve, ha_done, 4)
                after(k, p, dve, bs_done, 4)
                nc.vector.tensor_scalar(hid[:, p], tile(k, p), mean, col(n1.rs), ALU.subtract, ALU.mult).then_inc(hid_done, 1)
                after(k, p, dve, t_done)
                dve.wait_ge(hid_done, n(k, p) + 1)
                nc.vector.tensor_scalar(xn[:], hid[:, p], col(rs2), None, ALU.mult).then_inc(xn_done, 1)

            def shifted(r):
                def fn(k, p):
                    scores = ps_s[r][:].rearrange("q b (h n) -> q (b h) n", h=4)
                    dve.wait_ge(s_done[r], n(k, p) + 1)
                    nc.vector.tensor_reduce(mx[:, r], scores, AX.X, ALU.max).then_inc(max_done[r], 1)
                    dve.wait_ge(max_done[r], n(k, p) + 1)
                    after(k, p, dve, pn_done[r])
                    nc.vector.tensor_tensor(es[:, r], scores, mx[:, r].unsqueeze(2).to_broadcast([P, G, P]),
                                            ALU.subtract).then_inc(sub_done[r], 1)
                return fn

            def summed(r):
                def fn(k, p):
                    ch2.begin()
                    dve.wait_ge(exp_done[r], n(k, p) + 1)
                    after(k, p, dve, pn_done[r])
                    ch2.link(nc.vector.tensor_reduce(rs[:, r], es[:, r], AX.X, ALU.add))
                    nc.vector.reciprocal(rs[:, r], rs[:, r]).then_inc(sum_done[r], 1)
                return fn

            def residual(k, p):
                ch.begin()
                dve.wait_ge(proj_done, n(k, p) + 1)
                dve.wait_ge(bs_done, n(k, p) + 1)
                after(k, p, dve, xo_done)
                ch.link(nc.vector.tensor_tensor(ha[:], hid[:, p], ps_o[:, D:2 * D], ALU.add))
                nc.vector.tensor_tensor(tile(k, p), tile(k, p), ps_o[:, D:2 * D], ALU.add).then_inc(ha_done, 1)
                n3.stats(ch, lambda r: ha[:])
                after(k, p, dve, t2_done, 2)
                slot_free(k, p, dve, f_stored)
                n3.apply(0, xo[:, p % 2], ha[:]).then_inc(xo_done, 1)

            pipeline(dve, NT, [(norms, 0), (shifted(0), 1), (shifted(1), 1), (summed(0), 1), (summed(1), 1), (residual, 3)], 4)

        @block.tensor
        def _(pe):
            pe.wait_ge(weights, NW)

            def transposed(k, p):
                pe.wait_ge(xn_done, n(k, p) + 1)
                after(k, p, pe, lnT_done)
                for i in range(DC):
                    last = nc.tensor.transpose(ps_t[:, i * P:(i + 1) * P], xn[:, i * P:(i + 1) * P], c["ident"][:])
                last.then_inc(t_done, 1)

            def project(k, p):
                pe.wait_ge(lnT_done, n(k, p) + 1)
                after(k, p, pe, q_done)
                after(k, p, pe, vz_done)
                for f in range(3):
                    for i in range(DC):
                        nc.tensor.matmul(ps_qkv[:, f * P:(f + 1) * P], wqkv[:, i, f], lnT[:, i], start=i == 0, stop=i == DC - 1)
                for i in range(DC):
                    last = nc.tensor.matmul(ps_qkv[:, 3 * P:4 * P], lnT[:, i], wqkv[:, i, 3], start=i == 0, stop=i == DC - 1)
                last.then_inc(qkv_done, 1)

            def scores(r):
                def fn(k, p):
                    pe.wait_ge(km_done, n(k, p) + 1)
                    pe.wait_ge(q_done, n(k, p) + 1)
                    after(k, p, pe, sub_done[r])
                    after(k, p, pe, pt_done[r], 2)
                    for b in range(2):
                        nc.tensor.matmul(ps_s[r][:, b], qT[:, p % 2, r], km[:, p % 2, 4 * b:4 * b + 4].rearrange("p g n -> p (g n)"),
                                         start=True, stop=False)
                        last = nc.tensor.matmul(ps_s[r][:, b], c["ident_bf"][:],
                                                c["hidden_bf"][:].unsqueeze(1).to_broadcast([P, 4, P]), start=False, stop=True)
                    last.then_inc(s_done[r], 1)
                return fn

            def probs(r):
                def fn(k, p):
                    pe.wait_ge(pn_done[r], n(k, p) + 1)
                    if not (isinstance(k, int) and n(k, p) == NT - 1):
                        pe.wait_ge(sub_done[r], n(k, p) + 2)
                    for g in range(G):
                        last = nc.tensor.transpose(ps_s[r][:, g // 4, (g % 4) * P:(g % 4 + 1) * P], en[:, r, g], c["ident"][:])
                    last.then_inc(p_done[r], 1)
                return fn

            def weighted(k, p):
                pe.wait_ge(pt_done[0], n(k, p) + 1)
                pe.wait_ge(pt_done[1], n(k, p) + 1)
                after(k, p, pe, aT_done)
                after(k, p, pe, ha_done)
                for g in range(G):
                    for r in range(2):
                        j = g % 4
                        last = nc.tensor.matmul(ps_o[32 * j:32 * j + 32, g // 4 * P:(g // 4 + 1) * P],
                                                vz[:, p, g, DH * (1 - r):DH * (1 - r) + 32], pt[:, r, g],
                                                start=r == 0, stop=r == 1, skip_group_check=True)
                last.then_inc(av_done, 1)

            def output(k, p):
                pe.wait_ge(aT_done, n(k, p) + 1)
                after(k, p, pe, ha_done)
                for i in range(DC):
                    last = nc.tensor.matmul(ps_o[:, D:2 * D], aT[:, i], wp[:, i], start=i == 0, stop=i == DC - 1)
                last.then_inc(proj_done, 1)

            def route(k, p):
                pe.wait_ge(xo_done, n(k, p) + 1)
                after(k, p, pe, lg_done)
                for i in range(DC):
                    last = nc.tensor.transpose(ps_l[:, i * P:(i + 1) * P], xo[:, p % 2, i * P:(i + 1) * P], c["ident"][:])
                last.then_inc(t2_done, 1)
                pe.wait_ge(xoT_done, n(k, p) + 1)
                for i in range(DC):
                    last = nc.tensor.matmul(ps_l[:, D:D + NE], xoT[:, i], wr[:, i], start=i == 0, stop=i == DC - 1)
                last.then_inc(r_done, 1)

            pipeline(pe, NT, [(scores(0), 1), (scores(1), 1), (transposed, 0), (weighted, 3), (project, 0), (output, 3),
                              (probs(0), 2), (probs(1), 2), (route, 4)], 4)

        @block.scalar
        def _(act):
            act.wait_ge(weights, NW)

            def copy_t(k, p):
                act.wait_ge(t_done, n(k, p) + 1)
                after(k, p, act, qkv_done)
                for i in range(DC):
                    last = nc.scalar.activation(lnT[:, i], ps_t[:, i * P:(i + 1) * P], ACT.Identity,
                                                bias=aff["ln1_bias"][:, i:i + 1], scale=aff["ln1_weight"][:, i:i + 1])
                last.then_inc(lnT_done, 1)

            def copy_qkv(k, p):
                act.wait_ge(qkv_done, n(k, p) + 1)
                after(k, p, act, km_done)
                nc.scalar.activation(kb[:], ps_qkv[:, 2 * P:3 * P], ACT.Copy).then_inc(kb_done, 1)
                after(k, p, act, s_done[1], 2)
                nc.scalar.activation(qT[:, p % 2].rearrange("p r n -> p (r n)"), ps_qkv[:, 0:2 * P], ACT.Copy).then_inc(q_done, 1)
                after(k, p, act, av_done, 4)
                nc.scalar.activation(vz[:, p, :, DH:2 * DH], ps_qkv[:, 3 * P:4 * P].rearrange("p (g n) -> p g n", g=G),
                                     ACT.Copy).then_inc(vz_done, 1)

            def exps(r):
                def fn(k, p):
                    act.wait_ge(sub_done[r], n(k, p) + 1)
                    nc.scalar.activation(es[:, r], es[:, r], ACT.Exp, scale=DH ** -0.5).then_inc(exp_done[r], 1)
                return fn

            def copy_p(r):
                def fn(k, p):
                    act.wait_ge(p_done[r], n(k, p) + 1)
                    after(k, p, act, av_done)
                    nc.scalar.activation(pt[:, r].rearrange("q (b h) n -> q b (h n)", b=2), ps_s[r][:], ACT.Copy).then_inc(pt_done[r], 1)
                return fn

            def copy_a(k, p):
                act.wait_ge(av_done, n(k, p) + 1)
                after(k, p, act, proj_done)
                nc.scalar.activation(aT[:].rearrange("p c n -> p (c n)"), ps_o[:, 0:D], ACT.Copy).then_inc(aT_done, 1)

            def copy_x(k, p):
                act.wait_ge(t2_done, n(k, p) + 1)
                after(k, p, act, r_done)
                for i in range(DC):
                    last = nc.scalar.activation(xoT[:, i], ps_l[:, i * P:(i + 1) * P], ACT.Identity,
                                                bias=aff["ln2_bias"][:, i:i + 1], scale=aff["ln2_weight"][:, i:i + 1])
                last.then_inc(xoT_done, 1)
                act.wait_ge(r_done, n(k, p) + 1)
                slot_free(k, p, act, l_stored)
                nc.scalar.activation(lg[:, p % 2], ps_l[:, D:D + NE], ACT.Copy).then_inc(lg_done, 1)

            act.wait_ge(vz_zero, 1)
            pipeline(act, NT, [(copy_t, 0), (exps(0), 1), (copy_a, 3), (exps(1), 1), (copy_qkv, 0), (copy_p(0), 2),
                               (copy_p(1), 2), (copy_x, 4)], 4)

        @block.gpsimd
        def _(g):
            nc.gpsimd.memset(vz[:], 0.0).then_inc(vz_zero, 1)
            nc.gpsimd.memset(zeros[:], 0.0).then_inc(z_made, 1)

            def mask_k(k, p):
                g.wait_ge(kb_done, n(k, p) + 1)
                after(k, p, g, s_done[1], 2)
                nc.gpsimd.tensor_tensor(km[:, p % 2], kb[:].unsqueeze(1).to_broadcast([P, G, P]),
                                        c["head16"][:].unsqueeze(2).to_broadcast([P, G, P]), ALU.mult).then_inc(km_done, 1)

            def base_x(k, p):
                g.wait_ge(hid_done, n(k, p) + 1)
                nc.gpsimd.tensor_tensor(tile(k, p), tile(k, p), hid[:, p], ALU.add).then_inc(bs_done, 1)

            def normalized(r):
                def fn(k, p):
                    g.wait_ge(sum_done[r], n(k, p) + 1)
                    after(k, p, g, p_done[r])
                    nc.gpsimd.tensor_tensor(en[:, r], es[:, r], rs[:, r].unsqueeze(2).to_broadcast([P, G, P]),
                                            ALU.mult).then_inc(pn_done[r], 1)
                return fn

            pipeline(g, NT, [(mask_k, 0), (base_x, 0), (normalized(0), 1), (normalized(1), 1)], 4)


def routing(nc, logits, slots, gates, c):
    with ExitStack() as own:
        sb = lambda n, s, d=FP32: own.enter_context(nc.sbuf_tensor("ro_" + n, s, d))
        sem = own.enter_context(semaphores(nc, "ro_"))
        lg, ex, one1, one2, a, sel, w, cum, z = (sb(m, [P, NT, NE]) for m in ("lg", "ex", "one1", "one2", "a", "sel", "w", "cum", "z"))
        m1, m2, k1, k2, den = (sb(m, [P, NT]) for m in ("m1", "m2", "k1", "k2", "den"))
        ones = sb("ones", [P, NT])
        sf = sb("sf", [P, 2, NT])
        offs = own.enter_context(nc.psum_tensor("ro_offs", [P, NE], FP32))
        loaded, ready, exp_done, tot_done, offs_done, chain, done = (
            sem(m) for m in ("loaded", "shifted_ready", "exp_done", "tot_done", "offs_done", "chain", "done"))
        block = own.enter_context(nc.Block())

        @block.sync
        def _(sp):
            sp.dma_start(lg[:].rearrange("p t e -> p (t e)"), logits.rearrange("(p t) e -> p (t e)", t=NT)).then_inc(loaded, 16)

        @block.tensor
        def _(pe):
            pe.wait_ge(tot_done, 1)
            nc.tensor.matmul(offs[:], c["before"][:], cum[:, NT - 1], start=True, stop=True).then_inc(offs_done, 1)

        @block.scalar
        def _(act):
            act.wait_ge(ready, 1)
            nc.scalar.activation(ex[:], lg[:], ACT.Exp).then_inc(exp_done, 1)

        @block.vector
        def _(dve):
            ch = Chain(dve, chain)
            V = nc.vector
            over = lambda t: t[:].unsqueeze(2).to_broadcast([P, NT, NE])
            each = lambda t: t[:].unsqueeze(1).to_broadcast([P, NT, NE])
            dve.wait_ge(loaded, 16)
            ch.link(V.memset(ones[:], 1.0))
            ch.link(V.tensor_reduce(m1[:], lg[:], AX.X, ALU.max))
            V.tensor_tensor(lg[:], lg[:], over(m1), ALU.subtract).then_inc(ready, 1)
            dve.wait_ge(ready, 1)
            ch.link(V.scalar_tensor_tensor(a[:], lg[:], 0.0, each(c["first"]), ALU.is_equal, ALU.mult))
            ch.link(V.tensor_reduce(k1[:], a[:], AX.X, ALU.max))
            ch.link(V.tensor_tensor(one1[:], each(c["first"]), over(k1), ALU.is_equal))
            ch.link(V.scalar_tensor_tensor(z[:], one1[:], -3e38, lg[:], ALU.mult, ALU.add))
            ch.link(V.tensor_reduce(m2[:], z[:], AX.X, ALU.max))
            ch.link(V.tensor_tensor(a[:], z[:], over(m2), ALU.is_equal))
            ch.link(V.tensor_tensor(a[:], a[:], each(c["first"]), ALU.mult))
            ch.link(V.tensor_reduce(k2[:], a[:], AX.X, ALU.max))
            ch.link(V.tensor_tensor(one2[:], each(c["first"]), over(k2), ALU.is_equal))
            ch.link(V.tensor_tensor(sel[:], one1[:], one2[:], ALU.add))
            for e in range(NE):
                last = V.tensor_tensor_scan(cum[:, :, e], ones[:], sel[:, :, e], 0.0, ALU.mult, ALU.add)
            last.then_inc(tot_done, 1)
            dve.wait_ge(exp_done, 1)
            ch.link(V.tensor_tensor(w[:], ex[:], sel[:], ALU.mult))
            ch.link(V.tensor_reduce(den[:], w[:], AX.X, ALU.add))
            ch.link(V.reciprocal(den[:], den[:]))
            ch.link(V.tensor_tensor(w[:], w[:], over(den), ALU.mult))
            dve.wait_ge(tot_done, 1)
            dve.wait_ge(offs_done, 1)
            ch.link(V.tensor_tensor(cum[:], cum[:], sel[:], ALU.subtract))
            ch.link(V.tensor_copy(m1[:, 0:NE], offs[:]))
            ch.link(V.tensor_tensor(cum[:], cum[:], m1[:, 0:NE].unsqueeze(1).to_broadcast([P, NT, NE]), ALU.add))
            ch.link(V.tensor_scalar(a[:], cum[:], float(CAP), None, ALU.is_lt))
            ch.link(V.tensor_tensor(w[:], w[:], a[:], ALU.mult))
            ch.link(V.tensor_tensor(cum[:], cum[:], each(c["expert_row"]), ALU.add))
            ch.link(V.tensor_tensor(cum[:], cum[:], a[:], ALU.mult))
            for j, one in enumerate((one1, one2)):
                ch.link(V.tensor_tensor(z[:], cum[:], one[:], ALU.mult))
                ch.link(V.tensor_reduce(sf[:, j], z[:], AX.X, ALU.add))
                ch.link(V.tensor_tensor(z[:], w[:], one[:], ALU.mult))
                ch.link(V.tensor_reduce(gates[:, j], z[:], AX.X, ALU.add))
            V.tensor_scalar(slots[:], sf[:], float(ROWS), None, ALU.add).then_inc(done, 1)


def dispatch(nc, xf, slots, gates, of_batch, xin, w, w1s, w2s, ternary):
    with ExitStack() as own:
        rows = own.enter_context(nc.sbuf_tensor("di_rows", [P, NT, D], FP32))
        sem = own.enter_context(semaphores(nc, "di_"))
        loaded, sent, weights, saved, laid = (sem(m) for m in ("loaded", "sent", "weights", "saved", "laid"))
        ternary.stage(own, sem)
        block = own.enter_context(nc.Block())

        @block.sync
        def _(sp):
            sp.dma_start(rows[:], xf.rearrange("(p t) n -> p t n", t=NT)).then_inc(loaded, 16)
            ternary.load(sp)
            for q in range(2):
                sp.dma_start(w1s[:, q], w["moe_w1"][q].rearrange("(c p) f -> p c f", p=P)).then_inc(weights, 16)
                sp.dma_start(w2s[:, q], w["moe_w2"][q].rearrange("(c p) n -> p c n", p=P)).then_inc(weights, 16)
            for t, m in zip((slots, gates), of_batch):
                sp.dma_start(m["dram"].rearrange("j (p t) -> p j t", t=NT), t[:]).then_inc(saved, 16)
            sp.wait_ge(saved, 16 * 2)
            for m in of_batch:
                for j in range(2):
                    sp.dma_start(m["sbuf"][:, j], m["dram"][j].rearrange("(b s) -> s b", s=S),
                                 allow_slow_non_contiguous=True).then_inc(laid, 16)
            sp.wait_ge(weights, 16 * 4)
            sp.wait_ge(laid, 16 * 4)

        @block.tensor
        def _(pe):
            ternary.totals(pe)

        @block.vector
        def _(dve):
            ternary.round(dve)

        @block.gpsimd
        def _(g):
            g.wait_ge(loaded, 16)
            for t in range(NT):
                for j in range(2):
                    nc.gpsimd.indirect_dma_start(
                        out=xin[0:ROWS], out_offset=bass.IndirectOffsetOnAxis(ap=slots[:, j, t:t + 1], axis=0),
                        in_=rows[:, t], in_offset=None, bounds_check=ROWS - 1, oob_is_err=False).then_inc(sent, 16)
            g.wait_ge(sent, 16 * 2 * NT)


def experts(nc, xin, yout, w1, w2, w1s, w2s, ln_w, ln_b, c):
    R2 = 2 * S
    PER = CAP // R2
    FC = F // P
    UN = NE * PER
    with ExitStack() as own:
        sb = lambda n, s, d=FP32: own.enter_context(nc.sbuf_tensor("ex_" + n, s, d))
        pb = lambda n: own.enter_context(nc.psum_tensor("ex_ps_" + n, [P, 512], FP32))
        sem = own.enter_context(semaphores(nc, "ex_"))
        two = lambda n: [sem(f"{n}{i}") for i in range(2)]
        aff = [sb(m, [P, DC]) for m in ("weight", "bias")]
        xr = sb("xr", [S, 2, 2, D])
        xT = sb("xT", [P, 2, DC, R2])
        hT = sb("hT", [P, 2, FC, R2])
        y = sb("y", [S, 2, 2, D])
        ps_t = pb("t")
        ps_h = [pb(f"h{i}") for i in range(4)]
        ps_y = [pb(f"y{i}") for i in range(2)]
        affine, w_ready = sem("affine"), two("w_ready")
        x_ready, y_stored = two("x_ready"), two("y_stored")
        t_done, xT_done, m2_done, y_done = sem("t_done"), sem("xT_done"), sem("m2_done"), sem("y_done")
        h_done = [sem(f"h_done{i}") for i in range(4)]
        g_done = [sem(f"g_done{i}") for i in range(4)]
        U = 2 * PER
        rows = lambda a: a[0:ROWS].rearrange("(u b s) n -> u s b n", b=2, s=S)

        def n(k, p):
            return U * k + p

        def turn(k, p):
            return PER * k + p // 2

        def after(k, p, eng, s, back=1):
            if not (isinstance(k, int) and n(k, p) < back):
                eng.wait_ge(s, n(k, p) - back + 1)

        block = own.enter_context(nc.Block())

        @block.sync
        def _(sp):
            for t, a in zip(aff, (ln_w, ln_b)):
                sp.dma_start(t[:], a.rearrange("(c p) -> p c", p=P), allow_slow_non_contiguous=True).then_inc(affine, 16)

            def load(k, p):
                if p % PER == 0 and later(k):
                    q = p // PER
                    sp.wait_ge(m2_done, n(k, p) - PER)
                    sp.dma_start(w1s[:, q], w1[2 * k + q].rearrange("(c p) f -> p c f", p=P)).then_inc(w_ready[q], 16)
                    sp.dma_start(w2s[:, q], w2[2 * k + q].rearrange("(c p) n -> p c n", p=P)).then_inc(w_ready[q], 16)
                after(k, p, sp, t_done, 2)
                sp.dma_start(xr[:, p % 2], rows(xin)[n(k, p)]).then_inc(x_ready[p % 2], 16)

            def store(k, p):
                sp.wait_ge(y_done, n(k, p) + 1)
                sp.dma_start(rows(yout)[n(k, p)], y[:, p % 2]).then_inc(y_stored[p % 2], 16)

            pipeline(sp, UN, [(store, 3), (load, 0)], U)
            for s in y_stored:
                sp.wait_ge(s, 16 * (UN // 2))

        @block.tensor
        def _(pe):
            def transposed(k, p):
                pe.wait_ge(x_ready[p % 2], 16 * (turn(k, p) + 1))
                after(k, p, pe, xT_done)
                for i in range(DC):
                    for b in range(2):
                        last = nc.tensor.transpose(ps_t[:, i * R2 + b * S:i * R2 + (b + 1) * S],
                                                   xr[:, p % 2, b, i * P:(i + 1) * P], c["ident"][0:S, 0:S])
                last.then_inc(t_done, 1)

            def up(k, p):
                pe.wait_ge(xT_done, n(k, p) + 1)
                if p % PER == 0 and later(k):
                    pe.wait_ge(w_ready[p // PER], 32 * k)
                for h in range(4):
                    after(k, p, pe, g_done[h])
                    for j in range(2):
                        f = 2 * h + j
                        for i in range(DC):
                            last = nc.tensor.matmul(ps_h[h][:, j * R2:(j + 1) * R2], w1s[:, p // PER, i, f * P:(f + 1) * P],
                                                    xT[:, p % 2, i], start=i == 0, stop=i == DC - 1)
                    last.then_inc(h_done[h], 1)

            def down(k, p):
                after(k, p, pe, y_done, 2)
                for b in range(2):
                    for f in range(FC):
                        if b == 0 and f % 2 == 0:
                            pe.wait_ge(g_done[f // 2], n(k, p) + 1)
                        last = nc.tensor.matmul(ps_y[p % 2][0:S, b * D:(b + 1) * D], hT[:, p % 2, f, b * S:(b + 1) * S],
                                                w2s[:, p // PER, f], start=f == 0, stop=f == FC - 1)
                last.then_inc(m2_done, 1)

            pipeline(pe, UN, [(transposed, 0), (down, 1), (up, 0)], U)

        @block.scalar
        def _(act):
            act.wait_ge(affine, 32)

            def copy_t(k, p):
                act.wait_ge(t_done, n(k, p) + 1)
                after(k, p, act, h_done[3], 2)
                for i in range(DC):
                    last = nc.scalar.activation(xT[:, p % 2, i], ps_t[:, i * R2:(i + 1) * R2], ACT.Identity,
                                                bias=aff[1][:, i:i + 1], scale=aff[0][:, i:i + 1])
                last.then_inc(xT_done, 1)

            def gelus(k, p):
                after(k, p, act, m2_done, 2)
                for h in range(4):
                    act.wait_ge(h_done[h], n(k, p) + 1)
                    nc.scalar.activation(hT[:, p % 2, 2 * h:2 * h + 2].rearrange("p f n -> p (f n)"), ps_h[h][:, 0:2 * R2],
                                         ACT.Gelu).then_inc(g_done[h], 1)

            pipeline(act, UN, [(copy_t, 0), (gelus, 0)], U)

        @block.vector
        def _(dve):
            def copy_y(k, p):
                dve.wait_ge(m2_done, n(k, p) + 1)
                if not (isinstance(k, int) and n(k, p) < 2):
                    dve.wait_ge(y_stored[p % 2], 16 * turn(k, p))
                nc.vector.tensor_copy(y[:, p % 2].rearrange("s b n -> s (b n)"), ps_y[p % 2][0:S, :]).then_inc(y_done, 1)

            pipeline(dve, UN, [(copy_y, 1)], U)


def combine(nc, rows, base, slots, gates, yout, x_out):
    with ExitStack() as own:
        got = own.enter_context(nc.sbuf_tensor("co_rows", [S, 2, NB, D], FP32))
        sem = own.enter_context(semaphores(nc, "co_"))
        rows.stage(sem, base, x_out)
        came = [sem(f"came{i}") for i in range(NB)]
        first, summed, chain = sem("first"), sem("summed"), sem("chain")
        block = own.enter_context(nc.Block())

        @block.sync
        def _(sp):
            rows.load(sp, base)
            if x_out is not None:
                sp.wait_ge(summed, NB)
                sp.dma_start(x_out.rearrange("b s n -> s b n"), rows.x[:]).then_inc(rows.stored, 16)
                sp.wait_ge(rows.stored, 16)

        @block.gpsimd
        def _(g):
            for b in range(NB):
                for j in range(2):
                    nc.gpsimd.indirect_dma_start(
                        out=got[:, j, b], out_offset=None, in_=yout[:],
                        in_offset=bass.IndirectOffsetOnAxis(ap=slots[:, j, b:b + 1], axis=0),
                        bounds_check=ROWS, oob_is_err=False).then_inc(came[b], 16)

        @block.vector
        def _(dve):
            V = nc.vector
            ch = Chain(dve, chain)
            stats = rows.norm

            def sums(b):
                dve.wait_ge(rows.loaded[b // (NB // rows.parts)], 16)
                dve.wait_ge(came[b], 32)
                V.scalar_tensor_tensor(rows.x[:, b], got[:, 0, b], gates[:, 0, b:b + 1], rows.x[:, b],
                                       ALU.mult, ALU.add).then_inc(first, 1)
                dve.wait_ge(first, b + 1)
                V.scalar_tensor_tensor(rows.x[:, b], got[:, 1, b], gates[:, 1, b:b + 1], rows.x[:, b],
                                       ALU.mult, ALU.add).then_inc(summed, 1)
                dve.wait_ge(summed, b + 1)
                return V.bn_stats(stats.st[:, b, :], rows.x[:, b])

            for b in range(NB):
                last = sums(b)
            ch.link(last)
            for b in range(NB):
                last = V.bn_aggr(stats.mv[:, b, :], stats.st[:, b, :])
            ch.link(last)
            stats.finish(ch)
        rows.have_stats = True


def moe(nc, rows, base, xf, logits, xin, yout, x_out, w, ternary, c):
    with ExitStack() as own:
        sb = lambda n, s, d=FP32: own.enter_context(nc.sbuf_tensor("moe_" + n, s, d))
        slots = sb("slots", [P, 2, NT], I32)
        gates = sb("gates", [P, 2, NT])
        w1s = sb("w1", [P, 2, DC, F])
        w2s = sb("w2", [P, 2, F // P, D])
        of_batch = [{"dram": nc.dram_tensor("by_token_" + n, (2, TOK), d).ap(), "sbuf": sb("batch_" + n, [S, 2, NB], d)}
                    for n, d in (("slots", I32), ("gates", FP32))]
        routing(nc, logits, slots, gates, c)
        dispatch(nc, xf, slots, gates, of_batch, xin, w, w1s, w2s, ternary)
        experts(nc, xin, yout, w["moe_w1"], w["moe_w2"], w1s, w2s, w["ln2_weight"], w["ln2_bias"], c)
        combine(nc, rows, base.rearrange("(b s) n -> b s n", s=S), of_batch[0]["sbuf"], of_batch[1]["sbuf"], yout, x_out)


MAGIC = 12582912.0


class TernaryWeights:

    def __init__(self, nc, sb, w, c):
        self.nc, self.w, self.c = nc, w, c
        self.shape = {"w_a": [P, DC, D], "w_i": [P, DC, D], "w_v": [P, DC, D], "w_gate": [P, DC, 512], "w_down": [P, 4, D]}
        self.q = {m: sb("tw_" + m, s, BF16) for m, s in self.shape.items()}
        self.scale = sb("tw_scale", [P, len(self.shape)])

    def stage(self, own, sem):
        sb = lambda n, s: own.enter_context(self.nc.sbuf_tensor("tw_" + n, s, FP32))
        self.raw = {m: sb("raw_" + m, s) for m, s in self.shape.items()}
        self.part, self.mean, self.inv = (sb(m, [P, len(self.shape)]) for m in ("part", "mean", "inv"))
        self.tot = own.enter_context(self.nc.psum_tensor("tw_tot", [P, 16], FP32))
        self.loaded, self.summed, self.total, self.chain = (sem(m) for m in ("tw_loaded", "tw_summed", "tw_total", "tw_chain"))

    def load(self, sp):
        for m in self.shape:
            sp.dma_start(self.raw[m][:], self.w[m].rearrange("(c p) n -> p c n", p=P)).then_inc(self.loaded, 16)

    def totals(self, pe):
        k = len(self.shape)
        for i in range(2):
            pe.wait_ge(self.summed, i + 1)
            self.nc.tensor.matmul(self.tot[:, 8 * i:8 * i + k], self.c["ones"][:], self.part[:], start=True, stop=True).then_inc(self.total, 1)

    def round(self, dve):
        V, ch = self.nc.vector, Chain(dve, self.chain)
        raw, part, mean, tot = self.raw, self.part, self.mean, self.tot
        flat = lambda t: t[:].rearrange("p c n -> p (c n)")
        each = list(enumerate(self.shape))
        count = lambda m: P * raw[m].shape[1] * raw[m].shape[2]
        dve.wait_ge(self.loaded, 16 * len(each))
        for j, m in each:
            last = V.tensor_reduce(part[:, j:j + 1], flat(raw[m]), AX.X, ALU.add)
        last.then_inc(self.summed, 1)
        dve.wait_ge(self.total, 1)
        for j, m in each:
            last = V.tensor_scalar(mean[:, j:j + 1], tot[:, j:j + 1], 1.0 / count(m), None, ALU.mult)
        ch.link(last)
        for j, m in each:
            last = V.tensor_scalar(flat(raw[m]), flat(raw[m]), mean[:, j:j + 1], None, ALU.subtract)
        ch.link(last)
        for j, m in each:
            last = V.tensor_reduce(part[:, j:j + 1], flat(raw[m]), AX.X, ALU.add, apply_absolute_value=True)
        last.then_inc(self.summed, 1)
        dve.wait_ge(self.total, 2)
        for j, m in each:
            last = V.tensor_scalar(self.scale[:, j:j + 1], tot[:, 8 + j:9 + j], 1.0 / count(m), 1e-5, ALU.mult, ALU.max)
        ch.link(last)
        ch.link(V.reciprocal(self.inv[:], self.scale[:]))
        for j, m in each:
            ch.link(V.tensor_scalar(flat(raw[m]), flat(raw[m]), self.inv[:, j:j + 1], 1.0, ALU.mult, ALU.min))
            ch.link(V.tensor_scalar(flat(raw[m]), flat(raw[m]), -1.0, MAGIC, ALU.max, ALU.add))
            ch.link(V.tensor_scalar(flat(self.q[m]), flat(raw[m]), -MAGIC, None, ALU.add))


def gated_recurrence(nc, rows, x_in, x_out, w, ternary, c):
    UN = NB // 2
    CH = 64
    FD = 512
    FCH = FD // P
    N2 = 2 * S
    with ExitStack() as own:
        sb = lambda n, s, d=FP32: own.enter_context(nc.sbuf_tensor("gr_" + n, s, d))
        pb = lambda n, d=FP32: own.enter_context(nc.psum_tensor("gr_ps_" + n, [P, 2048 // mybir.dt.size(d)], d))
        sem = own.enter_context(semaphores(nc, "gr_"))
        wq, wscale = ternary.q, ternary.scale

        decay = sb("decay", [S, D])
        g_pre = sb("g_pre", [S, D])
        g_post = sb("g_post", [S, D])
        rows.stage(sem, x_in, x_out)
        v2 = sb("v2", [S, NB])
        rs2 = sb("rs2", [S, NB])
        w3 = sb("w3", [S, 3])
        zero = sb("zero", [P, CH])
        inside = sb("inside", [P, 2 * DC, S])

        xl = sb("xl", [S, 2, D])
        h = sb("h", [S, 2, D])
        xs = sb("xs", [S, 2])
        r127 = sb("r127", [S, 2, 2])
        sc = sb("sc", [S, 2, 2, 3])
        qf = sb("qf", [S, 2, D])
        qb = sb("qb", [S, 2, D], BF16)
        xqT = sb("xqT", [P, DC, N2], BF16)
        za = sb("za", [S, 2, D])
        eai = sb("eai", [S, 2, 2 * D])
        ai = sb("ai", [S, 2, 2, 2 * D])
        vv = sb("vv", [S, 2 * D])
        om = sb("om", [S, 2, 2 * D])
        iv = sb("iv", [S, 2, 2 * D])
        sg = sb("sg", [S, 2 * D])
        aT = sb("aT", [P, 2 * DC, S])
        cum = sb("cum", [P, 2 * DC, S])
        rc = sb("rc", [P, 2 * DC, S])
        cs = sb("cs", [P, 2 * DC, S])
        rec = sb("rec", [P, 2 * DC, S])
        rt = sb("rt", [S, 2, 2, D])
        xx = sb("xx", [S, 4, 2, D])
        xr = sb("xr", [S, 4, 2, D])
        squares = sb("squares", [S, 2, D])
        ssq = sb("ssq", [S, 2, 2])
        h2 = sb("h2", [S, 2, D])
        xs2 = sb("xs2", [S, 2])
        r2 = sb("r2", [S, 2, 2])
        sgt = sb("sgt", [S, 2, 2])
        q2f = sb("q2f", [S, 2, D])
        q2b = sb("q2b", [S, 2, D], BF16)
        q2T = sb("q2T", [P, DC, N2], BF16)
        th = sb("th", [S, 2, FD])
        zz = sb("zz", [S, 2, FD])
        hh = sb("hh", [S, 2, FD])
        xs3 = sb("xs3", [S, 2])
        r3 = sb("r3", [S, 2, 2])
        sd = sb("sd", [S, 2, 2])
        q3f = sb("q3f", [S, 2, FD])
        q3b = sb("q3b", [S, 2, FD], BF16)
        q3T = sb("q3T", [P, FCH, N2], BF16)
        n3 = Norm(nc, sb, "n3", S, 2, 0.0)
        ps_q, ps_h = pb("q", BF16), pb("h", BF16)
        ps_a, ps_i, ps_v, ps_at, ps_st, ps_r = (pb(m) for m in ("a", "i", "v", "at", "st", "r"))

        const = sem("const")
        names = ("ssq_done xl_done xx_done h_done qf_done qb_done tq_done xqT_done aiv_done za_done ei_done ea_done vv_done ai_done om_done iv_done "
                 "sq_done sg_done t_done wt_done rec_done tr_done rt_done xr_done h2_done q2f_done q2b_done t2_done q2T_done "
                 "gate_done th_done hh_done q3f_done q3b_done t3_done q3T_done down_done y_done")
        m = {x: sem(x) for x in names.split()}
        chain = sem("chain")

        def n(k, p):
            return 4 * k + p



        def after(k, p, eng, s, back=1):
            if not (isinstance(k, int) and n(k, p) < back):
                eng.wait_ge(m[s], n(k, p) - back + 1)

        def got(k, p, eng, s):
            eng.wait_ge(m[s], n(k, p) + 1)

        block = own.enter_context(nc.Block())
        row = lambda a: a.rearrange("(a n) -> a n", a=1).to_broadcast([S, D])
        pairs = lambda a: a.rearrange("(u b) s n -> u s b n", b=2)

        @block.sync
        def _(sp):
            rows.load(sp, x_in)
            for t, a in ((decay, "decay_bias"), (g_pre, "g_pre"), (g_post, "g_post")):
                sp.dma_start(t[:], row(w[a])).then_inc(const, 16)



            def store(k, p):
                got(k, p, sp, "y_done")
                sp.dma_start(pairs(x_out)[n(k, p)], rows.batch(2 * n(k, p), 2)).then_inc(rows.stored, 16)

            if x_out is not None:
                pipeline(sp, UN, [(store, 6)], 4)
                sp.wait_ge(rows.stored, 16 * UN)

        @block.vector
        def _(dve):
            V = nc.vector
            ch = Chain(dve, chain)
            dve.wait_ge(const, 16 * 3)
            ch.link(V.memset(zero[:], 0.0))
            ch.link(V.memset(inside[:], 1.0))
            ch.link(V.memset(inside[:, :, 0:1], 0.0))
            ch.link(V.memset(inside[:, :, CH:CH + 1], 0.0))
            ch.link(V.tensor_copy(w3[:], wscale[0:S, 0:3]))
            ch.link(V.tensor_scalar(w3[:, 1:2], w3[:, 1:2], 0.5, None, ALU.mult))
            rows.stats(dve, ch)
            ln = rows.norm
            ch.link(V.tensor_tensor(v2[:], ln.rs[:], ln.rs[:], ALU.mult))
            ch.link(V.tensor_tensor(v2[:], v2[:], ln.mv[:, :, 1], ALU.mult))
            ch.link(V.tensor_scalar(v2[:], v2[:], 1e-6, None, ALU.add))
            rsqrt(nc, ch, rs2[:], v2[:], ln.t[:], ln.ti[:])

            def scale_of(src, xs_, r):
                ch.link(V.tensor_reduce(xs_[:], src[:], AX.X, ALU.max, apply_absolute_value=True))
                ch.link(V.tensor_scalar(xs_[:], xs_[:], 1e-5, 1.0 / 127, ALU.max, ALU.mult))
                return V.reciprocal(r, xs_[:])

            def d0(k, p):
                ch.begin()
                after(k, p, dve, "xx_done")
                rows.normed(2 * n(k, p), xl[:, 0])
                rows.normed(2 * n(k, p) + 1, xl[:, 1]).then_inc(m["xl_done"], 1)
                got(k, p, dve, "xl_done")
                after(k, p, dve, "qf_done")
                for b in range(2):
                    i = 2 * n(k, p) + b
                    r = rs2[:, i:i + 1] if isinstance(i, int) else rs2[:, bass.ds(i, 1)]
                    last = V.scalar_tensor_tensor(h[:, b], xl[:, b], r, g_pre[:], ALU.mult, ALU.mult)
                ch.link(last)
                after(k, p, dve, "vv_done", 2)
                scale_of(h, xs, r127[:, p % 2])
                V.tensor_tensor(sc[:, p % 2], xs[:].unsqueeze(2).to_broadcast([S, 2, 3]),
                                w3[:].unsqueeze(1).to_broadcast([S, 2, 3]), ALU.mult).then_inc(m["h_done"], 1)

            def integers(src, dst, s_in, s_used, s_out):
                def fn(k, p):
                    got(k, p, dve, s_in)
                    after(k, p, dve, s_used)
                    V.tensor_scalar(dst[:], src[:], -MAGIC, 127.0, ALU.add, ALU.min).then_inc(m[s_out], 1)
                return fn

            def d2(k, p):
                got(k, p, dve, "aiv_done")
                after(k, p, dve, "ea_done")
                for b in range(2):
                    last = V.scalar_tensor_tensor(za[:, b], ps_a[0:S, b * D:(b + 1) * D], sc[:, p % 2, b, 0:1], decay[:],
                                                  ALU.mult, ALU.add)
                last.then_inc(m["za_done"], 1)

            def d3(k, p):
                ch.begin()
                got(k, p, dve, "ea_done")
                got(k, p, dve, "ei_done")
                after(k, p, dve, "t_done", 2)
                after(k, p, dve, "iv_done", 2)
                V.tensor_scalar(ai[:, p % 2], eai[:], 0.5, 0.5, ALU.mult, ALU.add).then_inc(m["ai_done"], 1)
                got(k, p, dve, "ai_done")
                after(k, p, dve, "sg_done", 2)
                ch.link(V.scalar_tensor_tensor(om[:, p % 2], ai[:, p % 2, 0], -1.0, ai[:, p % 2, 0], ALU.mult, ALU.mult))
                V.tensor_scalar(om[:, p % 2], om[:, p % 2], 1.0, 1e-8, ALU.add, ALU.max).then_inc(m["om_done"], 1)



            def d5(k, p):
                ch.begin()
                got(k, p, dve, "t_done")
                flat = lambda t: t[:].rearrange("p j n -> p (j n)")
                ch.link(V.tensor_scalar(flat(aT), ps_at[:, 0:2 * N2], 1e-10, None, ALU.max))
                for j in range(2 * DC):
                    for lo, hi in ((0, CH), (CH, S)):
                        last = V.tensor_tensor_scan(cum[:, j, lo:hi], aT[:, j, lo:hi], zero[:, 0:hi - lo], 1.0, ALU.mult, ALU.add)
                ch.link(last)
                ch.link(V.tensor_scalar(rc[:], cum[:], 1e-10, None, ALU.max))
                ch.link(V.reciprocal(rc[:], rc[:]))
                V.tensor_tensor(flat(rc), ps_st[:, 0:2 * N2], flat(rc), ALU.mult).then_inc(m["wt_done"], 1)
                got(k, p, dve, "wt_done")
                ch.link(V.tensor_tensor_scan(flat(cs), flat(inside), flat(rc), 0.0, ALU.mult, ALU.add))
                after(k, p, dve, "tr_done")
                ch.link(V.tensor_tensor(rec[:], cum[:], cs[:], ALU.mult))
                for j in range(2 * DC):
                    last = V.scalar_tensor_tensor(rec[:, j, CH:S], cum[:, j, CH:S], rec[:, j, CH - 1:CH], rec[:, j, CH:S],
                                                  ALU.mult, ALU.add)
                last.then_inc(m["rec_done"], 1)

            def d6(k, p):
                ch.begin()
                got(k, p, dve, "ssq_done")
                ch.link(V.tensor_scalar(n3.ve[:], ssq[:, p % 2], 1.0 / D, 1e-6, ALU.mult, ALU.add))
                rsqrt(nc, ch, n3.rs[:], n3.ve[:], n3.t[:], n3.ti[:])
                got(k, p, dve, "rt_done")
                after(k, p, dve, "q2f_done")
                for b in range(2):
                    last = V.scalar_tensor_tensor(h2[:, b], rt[:, p % 2, b], n3.rs[:, b:b + 1], g_post[:], ALU.mult, ALU.mult)
                ch.link(last)
                after(k, p, dve, "th_done", 2)
                ch.link(scale_of(h2, xs2, r2[:, p % 2]))
                V.tensor_scalar(sgt[:, p % 2], xs2[:], wscale[0:S, 3:4], 0.5, ALU.mult, ALU.mult).then_inc(m["h2_done"], 1)

            def d8(k, p):
                ch.begin()
                got(k, p, dve, "th_done")
                after(k, p, dve, "q3f_done")
                ch.link(V.scalar_tensor_tensor(hh[:], th[:], 1.0, zz[:], ALU.add, ALU.mult))
                ch.link(scale_of(hh, xs3, r3[:, p % 2]))
                after(k, p, dve, "y_done", 2)
                V.tensor_scalar(sd[:, p % 2], xs3[:], wscale[0:S, 4:5], None, ALU.mult).then_inc(m["hh_done"], 1)

            def d10(k, p):
                got(k, p, dve, "down_done")
                got(k, p, dve, "xr_done")
                for b in range(2):
                    x = rows.batch(2 * n(k, p) + b)
                    last = V.scalar_tensor_tensor(x, ps_v[0:S, b * D:(b + 1) * D], sd[:, p % 2, b:b + 1], xr[:, p, b], ALU.mult, ALU.add)
                last.then_inc(m["y_done"], 1)

            pipeline(dve, UN, [(d6, 3), (d2, 1), (d0, 0), (d8, 4), (d5, 2),
                               (integers(q2f, q2b, "q2f_done", "t2_done", "q2b_done"), 3),
                               (integers(qf, qb, "qf_done", "tq_done", "qb_done"), 0), (d3, 1), (d10, 5),
                               (integers(q3f, q3b, "q3f_done", "t3_done", "q3b_done"), 4)], 4)

        @block.tensor
        def _(pe):
            def reached(k, p, ahead, s):
                pe.wait_ge(m[s], (min(n(k, p) + ahead, UN - 1) if isinstance(k, int) else n(k, p) + ahead) + 1)

            def quantized(src, ps, chunks, s_in, frees, s_out):
                def fn(k, p):
                    got(k, p, pe, s_in)
                    for s_, back in frees:
                        if back > 0:
                            after(k, p, pe, s_, back)
                        else:
                            reached(k, p, -back, s_)
                    for i in range(chunks):
                        for b in range(2):
                            last = nc.tensor.transpose(ps[:, i * N2 + b * S:i * N2 + (b + 1) * S], src[:, b, i * P:(i + 1) * P],
                                                       c["ident_bf"][0:S, 0:S])
                    last.then_inc(m[s_out], 1)
                return fn

            def aiv(k, p):
                got(k, p, pe, "xqT_done")
                after(k, p, pe, "th_done", 4)
                after(k, p, pe, "za_done")
                after(k, p, pe, "ei_done")
                after(k, p, pe, "vv_done")
                after(k, p, pe, "y_done", 5)
                for name, ps in (("w_a", ps_a), ("w_i", ps_i), ("w_v", ps_v)):
                    for b in range(2):
                        for i in range(DC):
                            last = nc.tensor.matmul(ps[0:S, b * D:(b + 1) * D], xqT[:, i, b * S:(b + 1) * S], wq[name][:, i],
                                                    start=i == 0, stop=i == DC - 1)
                last.then_inc(m["aiv_done"], 1)

            def gate(k, p):
                got(k, p, pe, "q2T_done")
                reached(k, p, 3, "za_done")
                reached(k, p, 3, "ei_done")
                after(k, p, pe, "th_done")
                for b, ps in enumerate((ps_a, ps_i)):
                    for i in range(DC):
                        last = nc.tensor.matmul(ps[0:S, :], q2T[:, i, b * S:(b + 1) * S], wq["w_gate"][:, i],
                                                start=i == 0, stop=i == DC - 1)
                last.then_inc(m["gate_done"], 1)

            def down(k, p):
                got(k, p, pe, "q3T_done")
                reached(k, p, 4, "vv_done")
                after(k, p, pe, "y_done")
                for b in range(2):
                    for i in range(FCH):
                        last = nc.tensor.matmul(ps_v[0:S, b * D:(b + 1) * D], q3T[:, i, b * S:(b + 1) * S], wq["w_down"][:, i],
                                                start=i == 0, stop=i == FCH - 1)
                last.then_inc(m["down_done"], 1)

            def channel_major(k, p):
                got(k, p, pe, "sg_done")
                after(k, p, pe, "wt_done")
                for src, ps in ((ai[:, p % 2, 0], ps_at), (sg[:], ps_st)):
                    for i in range(DC):
                        for b in range(2):
                            last = nc.tensor.transpose(ps[:, i * N2 + b * S:i * N2 + (b + 1) * S],
                                                       src[:, b * D + i * P:b * D + (i + 1) * P], c["ident"][0:S, 0:S])
                last.then_inc(m["t_done"], 1)

            def token_major(k, p):
                got(k, p, pe, "rec_done")
                after(k, p, pe, "rt_done")
                after(k, p, pe, "ssq_done")
                for i in range(DC):
                    for b in range(2):
                        last = nc.tensor.transpose(ps_r[0:S, b * D + i * P:b * D + (i + 1) * P], rec[:, 2 * i + b], c["ident"][:])
                last.then_inc(m["tr_done"], 1)

            pipeline(pe, UN, [(quantized(qb, ps_q, DC, "qb_done", [("xqT_done", 1)], "tq_done"), 1), (token_major, 3),
                              (quantized(q2b, ps_h, DC, "q2b_done", [("q2T_done", 1), ("q3T_done", 2)], "t2_done"), 4),
                              (aiv, 1),
                              (quantized(q3b, ps_h, FCH, "q3b_done", [("q3T_done", 1), ("q2T_done", -1)], "t3_done"), 5),
                              (gate, 4), (down, 5), (channel_major, 2)], 4)

        @block.scalar
        def _(act):
            A = nc.scalar.activation

            def root(k, p):
                got(k, p, act, "om_done")
                A(om[:, p % 2], om[:, p % 2], ACT.Sqrt).then_inc(m["sq_done"], 1)

            def copy_rec(k, p):
                got(k, p, act, "tr_done")
                after(k, p, act, "h2_done", 2)
                after(k, p, act, "ssq_done")
                for b in range(2):
                    last = A(squares[:, b], ps_r[0:S, b * D:(b + 1) * D], ACT.Square, accum_out=ssq[:, p % 2, b:b + 1])
                last.then_inc(m["ssq_done"], 1)
                after(k, p, act, "h2_done", 2)
                after(k, p, act, "xr_done", 2)
                A(rt[:, p % 2].rearrange("s b n -> s (b n)"), ps_r[0:S, :], ACT.Copy).then_inc(m["rt_done"], 1)

            def copy_q(dst, ps, s_in, s_used, s_out):
                def fn(k, p):
                    got(k, p, act, s_in)
                    after(k, p, act, s_used)
                    flat = dst[:].rearrange("p c n -> p (c n)")
                    A(flat, ps[:, 0:flat.shape[1]], ACT.Copy).then_inc(m[s_out], 1)
                return fn

            def exponents(k, p):
                got(k, p, act, "aiv_done")
                after(k, p, act, "ai_done")
                for b in range(2):
                    last = A(eai[:, 1, b * D:(b + 1) * D], ps_i[0:S, b * D:(b + 1) * D], ACT.Tanh, scale=sc[:, p % 2, b, 1:2])
                last.then_inc(m["ei_done"], 1)
                after(k, p, act, "iv_done")
                for b in range(2):
                    last = A(vv[:, b * D:(b + 1) * D], ps_v[0:S, b * D:(b + 1) * D], ACT.Copy, scale=sc[:, p % 2, b, 2:3])
                last.then_inc(m["vv_done"], 1)
                got(k, p, act, "za_done")
                A(eai[:, 0], za[:].rearrange("s b n -> s (b n)"), ACT.Tanh, scale=0.5).then_inc(m["ea_done"], 1)

            def gates(k, p):
                got(k, p, act, "gate_done")
                after(k, p, act, "hh_done")
                for b, ps in enumerate((ps_a, ps_i)):
                    A(th[:, b], ps[0:S, :], ACT.Tanh, scale=sgt[:, p % 2, b:b + 1])
                    last = A(zz[:, b], ps[0:S, :], ACT.Copy, scale=sgt[:, p % 2, b:b + 1])
                last.then_inc(m["th_done"], 1)

            def quantize(src, r, dst, s_in, s_used, s_out):
                def fn(k, p):
                    got(k, p, act, s_in)
                    after(k, p, act, s_used)
                    for b in range(2):
                        last = A(dst[:, b], src[:, b], ACT.Copy, bias=MAGIC, scale=r[:, p % 2, b:b + 1])
                    last.then_inc(m[s_out], 1)
                return fn

            pipeline(act, UN, [(copy_rec, 3), (copy_q(xqT, ps_q, "tq_done", "aiv_done", "xqT_done"), 1), (root, 2),
                               (copy_q(q2T, ps_h, "t2_done", "gate_done", "q2T_done"), 4), (exponents, 1),
                               (copy_q(q3T, ps_h, "t3_done", "down_done", "q3T_done"), 5), (gates, 4),
                               (quantize(h2, r2, q2f, "h2_done", "q2b_done", "q2f_done"), 3),
                               (quantize(hh, r3, q3f, "hh_done", "q3b_done", "q3f_done"), 4),
                               (quantize(h, r127, qf, "h_done", "qb_done", "qf_done"), 0)], 4)

        @block.gpsimd
        def _(g):
            def gated(k, p):
                got(k, p, g, "ai_done")
                got(k, p, g, "vv_done")
                after(k, p, g, "sg_done", 2)
                nc.gpsimd.tensor_tensor(iv[:, p % 2], ai[:, p % 2, 1], vv[:], ALU.mult).then_inc(m["iv_done"], 1)

            def signal(k, p):
                got(k, p, g, "sq_done")
                got(k, p, g, "iv_done")
                after(k, p, g, "t_done")
                nc.gpsimd.tensor_tensor(sg[:], om[:, p % 2], iv[:, p % 2], ALU.mult).then_inc(m["sg_done"], 1)

            def normed(k, p):
                got(k, p, g, "xl_done")
                after(k, p, g, "xr_done", 4)
                nc.gpsimd.tensor_tensor(xx[:, p], rows.batch(2 * n(k, p), 2), xl[:], ALU.add).then_inc(m["xx_done"], 1)

            def add(k, p):
                got(k, p, g, "xx_done")
                got(k, p, g, "rt_done")
                after(k, p, g, "y_done", 4)
                nc.gpsimd.tensor_tensor(xr[:, p], xx[:, p], rt[:, p % 2], ALU.add).then_inc(m["xr_done"], 1)

            pipeline(g, UN, [(signal, 2), (normed, 0), (gated, 1), (add, 3)], 4)


def linear_cross_attention(nc, rows, x_in, ctx, x_out, w, c):
    H, DH, HD = 8, 64, 512
    HC = HD // P
    KT = T + 1
    with ExitStack() as own:
        sb = lambda n, s, d=FP32: own.enter_context(nc.sbuf_tensor("lc_" + n, s, d))
        pb = lambda n, s: own.enter_context(nc.psum_tensor("lc_ps_" + n, s, FP32))
        sem = own.enter_context(semaphores(nc, "lc_"))
        wq = sb("wq", [P, DC, HD])
        wkv = sb("wkv", [P, DC, 2 * HD])
        wo = sb("wo", [P, HC, D])
        qg, qbias = sb("qg", [S, HD]), sb("qbias", [S, HD])
        og, ob = sb("og", [P, HC]), sb("ob", [P, HC])
        nk = sb("nk", [P, 1])
        nks = sb("nks", [P, HC])
        rows.stage(sem, x_in, x_out)
        ct = sb("ct", [TN, 2, TC, D])
        xn = sb("xn", [S, D])
        xcT = sb("xcT", [P, DC, T + S])
        vs = sb("vs", [TN + 1, 2, TC, HD])
        kmx = sb("kmx", [P, HC])
        eT = sb("eT", [P, 2, HC, KT])
        ksum = sb("ksum", [P, 2, HC])
        eK = sb("eK", [TN + 1, TC, HD])
        q1 = sb("q1", [S, HD])
        qa = sb("qa", [S, HD])
        qmx = sb("qmx", [S, H])
        qs = sb("qs", [S, HD])
        qr = sb("qr", [S, H])
        qn = sb("qn", [S, HD])
        qT = sb("qT", [P, HC * S])
        cx = sb("cx", [P, HC, P])
        on = sb("on", [S, HD])
        oT = sb("oT", [P, HC, S])
        nqo = Norm(nc, sb, "nqo", S, 2, 1e-5)
        ps_ab = pb("ab", [P, 2, 512])
        ps_q = pb("q", [P, 512])
        ps_t = pb("t", [P, 512])
        ps_k = pb("k", [P, 4, 512])
        c_ready = [sem(f"c_ready{i}") for i in range(2)]
        weights, nulls = sem("weights"), sem("nulls")
        names = ("xn_done t_done xcT_done q_done v01_done k012_done v2_done k3_done qn1_done qg_done qa_done qsub_done "
                 "qexp_done qsum_done qn_done vc01_done vc2_done max012_done max3_done exp012_done exp3_done ksum_done te_done "
                 "eK_done tq_done qT_done cx_done cxc_done o_done on_done to_done oT_done y_ps_done y_done")
        m = {x: sem(x) for x in names.split()}
        chain = sem("chain")

        def n(k, p):
            return 4 * k + p

        def after(k, p, eng, s, back=1):
            if not (isinstance(k, int) and n(k, p) < back):
                eng.wait_ge(m[s], n(k, p) - back + 1)

        def got(k, p, eng, s):
            eng.wait_ge(m[s], n(k, p) + 1)

        block = own.enter_context(nc.Block())
        @block.sync
        def _(sp):
            rows.load(sp, x_in)
            sp.dma_start(wkv[:], w["Wkv"].rearrange("(c p) n -> p c n", p=P)).then_inc(weights, 16)
            sp.dma_start(wq[:], w["Wq"].rearrange("(c p) n -> p c n", p=P)).then_inc(weights, 16)
            sp.dma_start(wo[:], w["Wout"].rearrange("(c p) n -> p c n", p=P)).then_inc(weights, 16)
            for t, a in ((qg, "ln_q_g"), (qbias, "ln_q_b")):
                sp.dma_start(t[:], w[a].rearrange("(a n) -> a n", a=1).to_broadcast([S, HD])).then_inc(weights, 16)
            for t, a in ((og, "ln_out_g"), (ob, "ln_out_b")):
                sp.dma_start(t[:], w[a].rearrange("(c p) -> p c", p=P), allow_slow_non_contiguous=True).then_inc(weights, 16)
            sp.dma_start(nk[0:DH], w["null_kv"][0:1].rearrange("a d -> d a"), allow_slow_non_contiguous=True).then_inc(nulls, 16)
            sp.dma_start(nk[DH:P], w["null_kv"][0:1].rearrange("a d -> d a"), allow_slow_non_contiguous=True).then_inc(nulls, 16)
            for q in range(2):
                sp.dma_start(vs[TN:TN + 1, q, TC - 1].rearrange("a (h d) -> a h d", h=H),
                             w["null_kv"][1:2].unsqueeze(1).to_broadcast([1, H, DH])).then_inc(nulls, 16)

            def load(k, p):

                after(k, p, sp, "t_done", 2)
                sp.dma_start(ct[:, p % 2], ctx[n(k, p)].rearrange("(c t) n -> t c n", c=TC)).then_inc(c_ready[p % 2], 16)

            def store(k, p):
                got(k, p, sp, "y_done")
                sp.dma_start(x_out[n(k, p)], rows.batch(n(k, p))).then_inc(rows.stored, 16)

            pipeline(sp, NB, [(load, 0)] + ([(store, 4)] if x_out is not None else []), 4)
            if x_out is not None:
                sp.wait_ge(rows.stored, 16 * NB)

        @block.vector
        def _(dve):
            V = nc.vector
            ch = Chain(dve, chain)
            ch.link(V.memset(cx[:], 0.0))
            dve.wait_ge(nulls, 16 * 4)
            rows.stats(dve, ch)

            def norm(k, p):
                after(k, p, dve, "t_done")
                rows.normed(n(k, p), xn[:]).then_inc(m["xn_done"], 1)

            def norms(k, p):
                last = isinstance(k, int) and n(k, p) == NB - 1
                ch.begin()
                got(k, p, dve, "o_done")
                if not last:
                    dve.wait_ge(m["q_done"], n(k, p) + 2)
                    nqo.stats(ch, lambda r: (ps_q[0:S, :], ps_k[0:S, 3])[r])
                else:
                    nqo.stats(ch, lambda r: ps_k[0:S, 3])
                after(k, p, dve, "to_done")
                nqo.apply(1, on[:], ps_k[0:S, 3]).then_inc(m["on_done"], 1)
                if not last:
                    dve.wait_ge(m["qg_done"], n(k, p) + 1)
                    nqo.apply(0, q1[:], ps_q[0:S, :]).then_inc(m["qn1_done"], 1)

            def first_norm(k, p):
                if isinstance(k, int) and n(k, p) == 0:
                    ch.begin()
                    got(k, p, dve, "q_done")
                    nqo.stats(ch, lambda r: ps_q[0:S, :])
                    nqo.apply(0, q1[:], ps_q[0:S, :]).then_inc(m["qn1_done"], 1)

            def q_shift(k, p):
                ch.begin()
                got(k, p, dve, "qa_done")
                after(k, p, dve, "qn_done")
                heads = lambda t: t[:].rearrange("s (h d) -> s h d", h=H)
                ch.link(V.tensor_reduce(qmx[:], heads(qa), AX.X, ALU.max))
                V.tensor_tensor(heads(qs), heads(qa), qmx[:].unsqueeze(2).to_broadcast([S, H, DH]), ALU.subtract).then_inc(m["qsub_done"], 1)

            def q_sum(k, p):
                ch.begin()
                got(k, p, dve, "qexp_done")
                ch.link(V.tensor_reduce(qr[:], qs[:].rearrange("s (h d) -> s h d", h=H), AX.X, ALU.add))
                ch.link(V.reciprocal(qr[:], qr[:]))
                V.tensor_scalar(qr[:], qr[:], 8.0, None, ALU.mult).then_inc(m["qsum_done"], 1)



            def keys_max(lo, hi, s_in, s_out):
                def fn(k, p):
                    ch.begin()
                    got(k, p, dve, s_in)
                    if lo == 0:
                        after(k, p, dve, "ksum_done")
                    ch.link(V.tensor_reduce(kmx[:, lo:hi], ps_k[:, lo:hi, 0:T], AX.X, ALU.max))
                    last = V.tensor_scalar(kmx[:, lo:hi], kmx[:, lo:hi], nk[:], -1.0, ALU.max, ALU.mult)
                    if hi == HC:
                        ch.link(last)
                        last = V.tensor_scalar(nks[:], kmx[:], nk[:], None, ALU.add)
                    last.then_inc(m[s_out], 1)
                return fn

            def keys_sum(k, p):
                ch.begin()
                got(k, p, dve, "exp3_done")
                after(k, p, dve, "cxc_done")
                ch.link(V.tensor_tensor(ksum[:, p % 2], ksum[:, p % 2], eT[:, p % 2, :, T], ALU.add))
                V.reciprocal(ksum[:, p % 2], ksum[:, p % 2]).then_inc(m["ksum_done"], 1)

            def context(k, p):
                got(k, p, dve, "cx_done")
                after(k, p, dve, "o_done")
                got(k, p, dve, "ksum_done")
                for e in range(2):
                    r = slice(DH * e, DH * (e + 1))
                    last = V.tensor_tensor(cx[r, :, r], ps_k[r, 3].rearrange("d (m n) -> d m n", m=HC)[:, :, r],
                                           ksum[r, p % 2].unsqueeze(2).to_broadcast([DH, HC, DH]), ALU.mult)
                last.then_inc(m["cxc_done"], 1)



            def residual(k, p):
                got(k, p, dve, "y_ps_done")
                V.tensor_tensor(rows.batch(n(k, p)), ps_q[0:S, 0:D], rows.batch(n(k, p)), ALU.add).then_inc(m["y_done"], 1)

            pipeline(dve, NB, [(context, 2), (first_norm, 1), (norms, 2), (keys_max(0, 3, "k012_done", "max012_done"), 1),
                               (keys_max(3, 4, "k3_done", "max3_done"), 1), (q_shift, 1), (norm, 0), (residual, 2),
                               (q_sum, 1), (keys_sum, 1)], 4)

        @block.tensor
        def _(pe):
            pe.wait_ge(weights, 16 * 7)
            pe.wait_ge(nulls, 16 * 4)

            def exps_t(k, p):
                got(k, p, pe, "exp3_done")
                after(k, p, pe, "eK_done")
                for t in range(TC):
                    hi = TN + (t == TC - 1)
                    for i in range(HC):
                        last = nc.tensor.transpose(ps_k[0:hi, t, i * P:(i + 1) * P], eT[:, p % 2, i, t * TN:t * TN + hi], c["ident"][:])
                last.then_inc(m["te_done"], 1)

            def transposed(k, p):
                pe.wait_ge(c_ready[p % 2], 16 * (2 * k + p // 2 + 1))
                after(k, p, pe, "vc2_done")
                after(k, p, pe, "vc01_done")
                for t in range(TC):
                    for i in range(DC):
                        nc.tensor.transpose(ps_ab[:, i, t * TN:(t + 1) * TN], ct[:, p % 2, t, i * P:(i + 1) * P], c["ident"][0:TN, 0:TN])
                got(k, p, pe, "xn_done")
                for i in range(DC):
                    last = nc.tensor.transpose(ps_ab[:, i, T:T + S], xn[:, i * P:(i + 1) * P], c["ident"][0:S, 0:S])
                last.then_inc(m["t_done"], 1)

            def queries_t(k, p):
                got(k, p, pe, "qn_done")
                after(k, p, pe, "oT_done")
                for i in range(HC):
                    last = nc.tensor.transpose(ps_t[:, i * S:(i + 1) * S], qn[:, i * P:(i + 1) * P], c["ident"][0:S, 0:S])
                last.then_inc(m["tq_done"], 1)

            def context(k, p):
                got(k, p, pe, "eK_done")
                got(k, p, pe, "vc2_done")
                got(k, p, pe, "vc01_done")
                for i in range(HC):
                    for t in range(TC):
                        hi = TN + (t == TC - 1)
                        last = nc.tensor.matmul(ps_k[:, 3, i * P:(i + 1) * P], eK[0:hi, t, i * P:(i + 1) * P],
                                                vs[0:hi, p % 2, t, i * P:(i + 1) * P], start=t == 0, stop=t == TC - 1)
                last.then_inc(m["cx_done"], 1)

            def queries(k, p):
                got(k, p, pe, "xcT_done")
                after(k, p, pe, "qn1_done")
                after(k, p, pe, "y_done", 2)
                for i in range(DC):
                    last = nc.tensor.matmul(ps_q[0:S, :], xcT[:, i, T:T + S], wq[:, i], start=i == 0, stop=i == DC - 1)
                last.then_inc(m["q_done"], 1)

            def value(t, bank, s_out):
                def fn(k, p):
                    if t == 2:
                        got(k, p, pe, "vc01_done")
                    for i in range(DC):
                        last = nc.tensor.matmul(ps_ab[0:TN, bank], xcT[:, i, t * TN:(t + 1) * TN], wkv[:, i, HD:2 * HD],
                                                start=i == 0, stop=i == DC - 1)
                    if s_out:
                        last.then_inc(m[s_out], 1)
                return fn

            def output(k, p):
                got(k, p, pe, "cxc_done")
                got(k, p, pe, "qT_done")
                for i in range(HC):
                    last = nc.tensor.matmul(ps_k[0:S, 3, i * P:(i + 1) * P], qT[:, i * S:(i + 1) * S], cx[:, i], start=True, stop=True)
                last.then_inc(m["o_done"], 1)

            def keys(chunks, s_out):
                def fn(k, p):
                    if chunks[0] == 0:
                        after(k, p, pe, "eK_done")
                    else:
                        after(k, p, pe, "on_done")
                    for o in chunks:
                        for i in range(DC):
                            last = nc.tensor.matmul(ps_k[:, o, 0:T], wkv[:, i, o * P:(o + 1) * P], xcT[:, i, 0:T],
                                                    start=i == 0, stop=i == DC - 1)
                    last.then_inc(m[s_out], 1)
                return fn

            def output_t(k, p):
                got(k, p, pe, "on_done")
                got(k, p, pe, "qT_done")
                for i in range(HC):
                    last = nc.tensor.transpose(ps_t[:, i * S:(i + 1) * S], on[:, i * P:(i + 1) * P], c["ident"][0:S, 0:S])
                last.then_inc(m["to_done"], 1)

            def project(k, p):
                got(k, p, pe, "oT_done")
                after(k, p, pe, "y_done")
                if not (isinstance(k, int) and n(k, p) == NB - 1):
                    pe.wait_ge(m["qn1_done"], n(k, p) + 2)
                for i in range(HC):
                    last = nc.tensor.matmul(ps_q[0:S, 0:D], oT[:, i], wo[:, i], start=i == 0, stop=i == HC - 1)
                last.then_inc(m["y_ps_done"], 1)

            pipeline(pe, NB, [(exps_t, 2), (transposed, 1), (queries_t, 2), (context, 2), (queries, 1),
                              (value(0, 0, None), 1), (output, 2), (value(1, 1, "v01_done"), 1),
                              (keys((0, 1, 2), "k012_done"), 1), (keys((3,), "k3_done"), 1), (output_t, 2),
                              (value(2, 0, "v2_done"), 1), (project, 2)], 4)

        @block.scalar
        def _(act):
            A = nc.scalar.activation
            act.wait_ge(weights, 16 * 7)
            act.wait_ge(nulls, 16 * 4)

            def copy_e(k, p):
                got(k, p, act, "te_done")
                after(k, p, act, "cx_done")
                A(eK[0:TN, 0:2], ps_k[0:TN, 0:2], ACT.Copy)
                A(eK[:, 2], ps_k[0:TN + 1, 2], ACT.Copy).then_inc(m["eK_done"], 1)

            def copy_t(k, p):
                got(k, p, act, "t_done")
                after(k, p, act, "k3_done")
                A(xcT[:], ps_ab[:, :, 0:T + S], ACT.Copy).then_inc(m["xcT_done"], 1)

            def copy_q(k, p):
                got(k, p, act, "tq_done")
                after(k, p, act, "o_done")
                A(qT[:], ps_t[:, 0:HC * S], ACT.Copy).then_inc(m["qT_done"], 1)

            def q_exp(k, p):
                got(k, p, act, "qsub_done")
                A(qs[:], qs[:], ACT.Exp).then_inc(m["qexp_done"], 1)

            def keys_exp(chunks, s_in, s_out):
                def fn(k, p):
                    got(k, p, act, s_in)
                    after(k, p, act, "te_done", 2)
                    after(k, p, act, "cxc_done", 2)
                    for o in chunks:
                        last = A(eT[:, p % 2, o, 0:T], ps_k[:, o, 0:T], ACT.Exp, bias=kmx[:, o:o + 1], accum_out=ksum[:, p % 2, o:o + 1])
                    if chunks[-1] == HC - 1:
                        last = A(eT[:, p % 2, :, T], nks[:], ACT.Exp)
                    last.then_inc(m[s_out], 1)
                return fn

            def values01(k, p):
                got(k, p, act, "v01_done")
                after(k, p, act, "cx_done", 2)
                A(vs[0:TN, p % 2, 0:2], ps_ab[0:TN], ACT.Copy).then_inc(m["vc01_done"], 1)

            def values2(k, p):
                got(k, p, act, "v2_done")
                A(vs[0:TN, p % 2, 2], ps_ab[0:TN, 0], ACT.Copy).then_inc(m["vc2_done"], 1)

            def copy_o(k, p):
                got(k, p, act, "to_done")
                after(k, p, act, "y_ps_done")
                for i in range(HC):
                    last = A(oT[:, i], ps_t[:, i * S:(i + 1) * S], ACT.Identity, bias=ob[:, i:i + 1], scale=og[:, i:i + 1])
                last.then_inc(m["oT_done"], 1)

            pipeline(act, NB, [(copy_e, 2), (copy_t, 1), (copy_q, 2), (values01, 1), (copy_o, 2),
                               (keys_exp((0, 1, 2), "max012_done", "exp012_done"), 1),
                               (keys_exp((3,), "max3_done", "exp3_done"), 1), (values2, 1), (q_exp, 1)], 4)

        @block.gpsimd
        def _(g):
            g.wait_ge(weights, 16 * 7)

            def q_affine(k, p):
                got(k, p, g, "qn1_done")
                after(k, p, g, "qsub_done")
                nc.gpsimd.tensor_tensor(qa[:], q1[:], qg[:], ALU.mult).then_inc(m["qg_done"], 1)
                got(k, p, g, "qg_done")
                nc.gpsimd.tensor_tensor(qa[:], qa[:], qbias[:], ALU.add).then_inc(m["qa_done"], 1)

            def q_scaled(k, p):
                got(k, p, g, "qsum_done")
                after(k, p, g, "tq_done")
                heads = lambda t: t[:].rearrange("s (h d) -> s h d", h=H)
                nc.gpsimd.tensor_tensor(heads(qn), heads(qs), qr[:].unsqueeze(2).to_broadcast([S, H, DH]), ALU.mult).then_inc(m["qn_done"], 1)

            pipeline(g, NB, [(q_affine, 1), (q_scaled, 1)], 4)


def int8_projection(nc, rows, x_in, x_out, w, c):
    UN = NB // 2
    with ExitStack() as own:
        sb = lambda n, s, d=FP32: own.enter_context(nc.sbuf_tensor("ip_" + n, s, d))
        pb = lambda n, d=FP32, k=512: own.enter_context(nc.psum_tensor("ip_ps_" + n, [P, k], d))
        sem = own.enter_context(semaphores(nc, "ip_"))
        two = lambda n: [sem(f"{n}{i}") for i in range(2)]

        w8 = sb("w8", [P, DC, D // 4], I32)
        wb = sb("wb", [P, DC, D], BF16)
        wsc = sb("wsc", [S, 2, D])
        bias = sb("bias", [S, 2, D])
        rows.stage(sem, x_in, x_out)
        h = sb("h", [S, NB, D])
        part = sb("part", [P, 1])
        diag = sb("diag", [P, P])
        top = sb("top", [P, 1])
        xs = sb("xs", [P, 1])
        inv = sb("inv", [P, 1])
        q = sb("q", [S, 2, 2 * D])
        qb = sb("qb", [S, 2, 2 * D], BF16)
        qT = sb("qT", [P, 2, 2, DC, S], BF16)
        xb = sb("xb", [S, 2, 2, D])
        y = sb("y", [S, 2, 2, D])
        ps_m = pb("m")
        ps_t = [pb(f"t{i}", BF16, 1024) for i in range(2)]
        ps_o = [pb(f"o{i}") for i in range(2)]

        weights, w_ready = sem("weights_loaded"), sem("w_ready")
        diag_done, top_done, chain = sem("diag_done"), sem("top_done"), sem("chain")
        t_done, qb_done, qT_done, o_done, xb_done, y_done, y_stored = (
            two(m) for m in ("t_done", "qb_done", "qT_done", "o_done", "xb_done", "y_done", "y_stored"))
        pairs = lambda a: a.rearrange("(u b) s n -> u s b n", b=2)
        part_zero = sem("part_zero")
        block = own.enter_context(nc.Block())

        def item(k, p):
            return 2 * k + p

        @block.sync
        def _(sp):
            rows.load(sp, x_in)
            sp.dma_start(w8[:], w["weight_int8"].rearrange("(c p) n -> p c n", p=P)).then_inc(weights, 16)
            for r in range(2):
                sp.dma_start(wsc[:, r], w["weight_scale"].rearrange("n a -> a n").to_broadcast([S, D])).then_inc(weights, 16)
                sp.dma_start(bias[:, r], w["bias"].rearrange("(a n) -> a n", a=1).to_broadcast([S, D])).then_inc(weights, 16)

            def store(k, p):
                sp.wait_ge(y_done[p], k + 1)
                sp.dma_start(pairs(x_out)[item(k, p)], y[:, p]).then_inc(y_stored[p], 16)

            pipeline(sp, UN, [(store, 0)])
            for p in range(2):
                sp.wait_ge(y_stored[p], 16 * (UN // 2))

        @block.gpsimd
        def _(g):
            nc.gpsimd.memset(part[:], 0.0).then_inc(part_zero, 1)
            g.wait_ge(weights, 16 * 5)
            for loaded in rows.loaded or ():
                g.wait_ge(loaded, 16)

            def add_bias(k, p):
                if later(k):
                    g.wait_ge(y_done[p], k)
                nc.gpsimd.tensor_tensor(xb[:, p], rows.batch(2 * item(k, p), 2), bias[:], ALU.add).then_inc(xb_done[p], 1)

            pipeline(g, UN, [(add_bias, 0)])

        @block.tensor
        def _(pe):
            pe.wait_ge(diag_done, 1)
            nc.tensor.matmul(ps_m[:, 0:P], c["ones"][:], diag[:], start=True, stop=True).then_inc(top_done, 1)
            pe.wait_ge(w_ready, 1)

            def transposed(k, p):
                pe.wait_ge(qb_done[p], k + 1)
                if later(k):
                    pe.wait_ge(qT_done[p], k)
                for i in range(2 * DC):
                    last = nc.tensor.transpose(ps_t[p][:, i * S:(i + 1) * S], qb[:, p, i * P:(i + 1) * P], c["ident_bf"][0:S, 0:S])
                last.then_inc(t_done[p], 1)

            def product(k, p):
                pe.wait_ge(qT_done[p], k + 1)
                if later(k):
                    pe.wait_ge(y_done[p], k)
                for r in range(2):
                    for i in range(DC):
                        last = nc.tensor.matmul(ps_o[p][0:S, r * D:(r + 1) * D], qT[:, p, r, i], wb[:, i], start=i == 0, stop=i == DC - 1)
                last.then_inc(o_done[p], 1)

            pipeline(pe, UN, [(transposed, 0), (product, 1)])

        @block.scalar
        def _(act):
            def copy_t(k, p):
                act.wait_ge(t_done[p], k + 1)
                if later(k):
                    act.wait_ge(o_done[p], k)
                nc.scalar.activation(qT[:, p].rearrange("p r c n -> p (r c n)"), ps_t[p][:, 0:4 * S], ACT.Copy).then_inc(qT_done[p], 1)

            pipeline(act, UN, [(copy_t, 0)])

        @block.vector
        def _(dve):
            ch = Chain(dve, chain)
            V = nc.vector

            rows.stats(dve, ch)
            for i in range(NB):
                last = rows.normed(i, h[:, i])
            ch.link(last)
            dve.wait_ge(part_zero, 1)
            ch.link(V.tensor_reduce(part[0:S], h[:].rearrange("p t n -> p (t n)"), AX.X, ALU.max, apply_absolute_value=True))
            V.tensor_scalar(diag[:], c["ident"][:], part[:, 0:1], None, ALU.mult).then_inc(diag_done, 1)
            dve.wait_ge(weights, 16 * 5)
            V.tensor_copy(wb[:], w8[:].bitcast(I8)).then_inc(w_ready, 1)
            dve.wait_ge(top_done, 1)
            ch.link(V.tensor_reduce(top[:], ps_m[:, 0:P], AX.X, ALU.max))
            ch.link(V.tensor_scalar(xs[:], top[:], 1.0 / 127, 1e-5, ALU.mult, ALU.max))
            ch.link(V.reciprocal(inv[:], xs[:]))

            def quantize(k, p):
                ch.begin()
                src = h[:, bass.ds(2 * item(k, p), 2)]
                ch.link(V.tensor_scalar(q[:, p].rearrange("p (r n) -> p r n", r=2), src, inv[0:S, 0:1], 127.0, ALU.mult, ALU.min))
                ch.link(V.tensor_scalar(q[:, p], q[:, p], -128.0, MAGIC, ALU.max, ALU.add))
                if later(k):
                    dve.wait_ge(t_done[p], k)
                V.tensor_scalar(qb[:, p], q[:, p], -MAGIC, None, ALU.add).then_inc(qb_done[p], 1)

            def scaled(k, p):
                ch.begin()
                dve.wait_ge(o_done[p], k + 1)
                if later(k):
                    dve.wait_ge(y_stored[p], 16 * k)
                ch.link(V.scalar_tensor_tensor(y[:, p].rearrange("p r n -> p (r n)"), ps_o[p][0:S, :], xs[0:S, 0:1],
                                               wsc[:].rearrange("p r n -> p (r n)"), ALU.mult, ALU.mult))
                dve.wait_ge(xb_done[p], k + 1)
                V.tensor_tensor(y[:, p], y[:, p], xb[:, p], ALU.add).then_inc(y_done[p], 1)

            pipeline(dve, UN, [(quantize, 0), (scaled, 2)])


def program(nc, a, out, first=1, last=6):
    with ExitStack() as keep:
        c = constants(nc, keep)
        with ExitStack() as own:
            sem = own.enter_context(semaphores(nc, "constants_"))
            made = sem("made")
            block = own.enter_context(nc.Block())

            @block.gpsimd
            def _(g):
                maker = ConstantsMaker(nc, c, g, made)
                maker.first()
                if first > 1:
                    maker.others()
        g = lambda pre, names: {m: a[pre + m] for m in names}
        dram = lambda name, shape: nc.dram_tensor(name, shape, FP32).ap()
        tokens = lambda ap: ap.rearrange("b s n -> (b s) n")
        on = lambda i: first <= i <= last
        x2 = out if last == 2 else dram("x2", (NB, S, D))
        came = lambda i, x: a["x"] if i == first else x
        went = lambda i, x: out if i == last else x
        with ExitStack() as pair:
            rows = TokenRows(nc, lambda n, s, d=FP32: pair.enter_context(nc.sbuf_tensor(n, s, d)), "rows_a")
            if on(1):
                linear_attention(nc, rows, came(1, a["x"]), went(1, None),
                                 g("L0_attn_", ("Wq", "bq", "Wk", "bk", "Wv", "bv", "Wu", "bu", "Wo", "bo", "scale")), c)
            if on(2):
                cross_attention(nc, rows, came(2, None), a["ctx_1024"], went(2, x2),
                                g("L0_xattn_", ("Wq", "bq", "Wk", "bk", "Wv", "bv", "Wo", "bo")), c)
        ternary = TernaryWeights(nc, lambda n, s, d=FP32: keep.enter_context(nc.sbuf_tensor(n, s, d)),
                                 g("L1_attn_", ("w_a", "w_i", "w_v", "w_gate", "w_down")), c)
        with ExitStack() as pair:
            rows = TokenRows(nc, lambda n, s, d=FP32: pair.enter_context(nc.sbuf_tensor(n, s, d)), "rows_b")
            if on(3):
                base, xf, logits = dram("base", (TOK, D)), dram("xf", (TOK, D)), dram("logits", (TOK, NE))
                xin = dram("expert_in", (ROWS, D))
                yout = dram("expert_out", (ROWS + 1, D))
                w = g("L0_ffn_", ("ln1_weight", "ln1_bias", "ln2_weight", "ln2_bias", "qkv_weight", "proj_weight",
                                  "router_weight", "moe_w1", "moe_w2"))
                moe_attention(nc, tokens(came(3, x2)), base, xf, logits, xin, yout, w, c)
                moe(nc, rows, base, xf, logits, xin, yout, went(3, None), w, ternary, c)
            if on(4) and first == 4:
                with ExitStack() as own:
                    ternary.stage(own, own.enter_context(semaphores(nc, "")))
                    block = own.enter_context(nc.Block())
                    block.sync(ternary.load)
                    block.tensor(ternary.totals)
                    block.vector(ternary.round)
            if on(4):
                gated_recurrence(nc, rows, came(4, None), went(4, None),
                                 g("L1_attn_", ("decay_bias", "g_pre", "g_post")), ternary, c)
            if on(5):
                linear_cross_attention(nc, rows, came(5, None), a["ctx_1024"], went(5, None),
                                       g("L1_xattn_", ("Wq", "Wkv", "null_kv", "ln_q_g", "ln_q_b", "ln_out_g", "ln_out_b", "Wout")), c)
            if on(6):
                int8_projection(nc, rows, came(6, None), out, g("L1_ffn_", ("weight_int8", "weight_scale", "bias")), c)


_INPUT_AS_ROWS = ("L0_attn_Wq", "L0_attn_Wk", "L0_attn_Wv", "L0_attn_Wu", "L0_attn_Wo", "L0_ffn_proj_weight",
                  "L1_attn_w_gate", "L1_attn_w_down", "L1_attn_w_a", "L1_attn_w_i", "L1_attn_w_v", "L1_ffn_weight_int8")


def kernel(**inputs):
    import numpy as np
    import concourse.bacc as bacc
    from concourse.bass_utils import run_bass_kernel_spmd

    nc = bacc.Bacc("TRN2", target_bir_lowering=False, num_devices=1)
    arrays, a = {}, {}
    for name, value in inputs.items():
        value = np.asarray(value)
        if name in _INPUT_AS_ROWS:
            value = value.T
        if name == "L0_ffn_qkv_weight":
            value = value.reshape(8, 4, 16, D).transpose(3, 1, 0, 2).reshape(D, 4 * P)
        value = np.ascontiguousarray(value)
        if value.dtype == np.int8:
            value = value.view(np.int32)
        arrays[name] = value
        a[name] = nc.dram_tensor(name, value.shape, mybir.dt.from_np(value.dtype), kind="ExternalInput").ap()
    out = nc.dram_tensor("out", (NB, S, D), FP32, kind="ExternalOutput").ap()
    program(nc, a, out)
    return run_bass_kernel_spmd(nc, [arrays], core_ids=[0]).results[0]["out"]
```
